# Optimizing a Trainium2 kernel written in Bass

```python
import numpy as np
import jax
import jax.numpy as jnp

def _softmax(x, axis=-1):
    return jax.nn.softmax(x, axis=axis)

def _gelu(x):
    return jax.nn.gelu(x, approximate=True)

def _silu(x):
    return jax.nn.silu(x)

def _sigmoid(x):
    return jax.nn.sigmoid(x)

def _layernorm(x, axis=-1, eps=1e-05):
    m = jnp.mean(x, axis=axis, keepdims=True)
    v = jnp.var(x, axis=axis, keepdims=True)
    return (x - m) / jnp.sqrt(v + eps)

def _scatter_add(tgt, idx, src, axis=0):
    return tgt.at[idx].add(src)

def _segment_sum(src, seg, n):
    return jax.ops.segment_sum(src, seg, n)
kernel_name = 'mk_prb_d2_jaxref_r8_026996'

def setup_inputs(seed: int=0):
    np.random.seed(seed)
    _w = jnp.asarray

    def _L0_attn_setup():
        import jax, jax.numpy as jnp
        import numpy as np
        NUM_LANDMARKS = 64
        key = jax.random.key(seed)
        ks = jax.random.split(key, 4)
        B, S, D = (4, 512, 128)
        init = 0.02
        return {'hidden_states': jax.random.normal(ks[0], (B, S, D), dtype=jnp.float32), 'Wq': jax.random.normal(ks[1], (D, D), dtype=jnp.float32) * init, 'bq': jnp.zeros((D,), dtype=jnp.float32), 'Wk': jax.random.normal(ks[2], (D, D), dtype=jnp.float32) * init, 'bk': jnp.zeros((D,), dtype=jnp.float32), 'Wv': jax.random.normal(ks[3], (D, D), dtype=jnp.float32) * init, 'bv': jnp.zeros((D,), dtype=jnp.float32)}
    _L0_attn_in = _L0_attn_setup()

    def _L0_ffn_setup():
        import jax, jax.numpy as jnp
        import numpy as np
        B, T, D = (2, 128, 128)
        H, DK, K = (8, 128, 8)
        NKEYS = 32
        NEXP = NKEYS * NKEYS

        def _rmsnorm(x, w, eps=1e-06):
            inv = jax.lax.rsqrt(jnp.mean(x * x, axis=-1, keepdims=True) + eps)
            return x * inv * w
        key = jax.random.key(seed)
        ks = jax.random.split(key, 5)
        return {'x': jax.random.normal(ks[0], (B, T, D), jnp.float32), 'w_q': jax.random.normal(ks[1], (H * 2 * DK, D), jnp.float32) * 0.02, 'keys': jax.random.normal(ks[2], (H, NKEYS, 2, DK), jnp.float32) * 0.02, 'expert_down': jax.random.normal(ks[3], (NEXP, D), jnp.float32) * 0.02, 'expert_up': jax.random.normal(ks[4], (NEXP, D), jnp.float32) * 0.02, 'norm_w': jnp.ones((D,), jnp.float32)}
    _L0_ffn_in = _L0_ffn_setup()

    def _L1_attn_setup():
        import jax, jax.numpy as jnp
        import numpy as np
        D_MODEL = 128
        NUM_HEADS = 16
        D_K = 128
        D_V = 128
        D_IN = 128
        THETA = 10000.0
        B, S = (2, 256)

        def _rope(t, theta):
            hd = t.shape[-1]
            inv_freq = 1.0 / theta ** (jnp.arange(0, hd, 2, dtype=jnp.float32) / hd)
            pos = jnp.arange(t.shape[-2], dtype=jnp.float32)
            ang = pos[:, None] * inv_freq[None, :]
            cos, sin = (jnp.cos(ang), jnp.sin(ang))
            tp = t.reshape(t.shape[:-1] + (hd // 2, 2))
            t0, t1 = (tp[..., 0], tp[..., 1])
            out = jnp.stack([t0 * cos - t1 * sin, t0 * sin + t1 * cos], axis=-1)
            return out.reshape(t.shape)
        key = jax.random.key(seed)
        k1, k2, k3, k4, k5 = jax.random.split(key, 5)
        std_qkv = (2.0 / (D_IN + D_K)) ** 0.5
        std_o = (2.0 / (D_V + D_MODEL)) ** 0.5
        x = jax.random.normal(k1, (B, S, D_IN), jnp.float32)
        wq = jax.random.normal(k2, (D_IN, D_K), jnp.float32) * std_qkv
        wk = jax.random.normal(k3, (D_IN, D_K), jnp.float32) * std_qkv
        wv = jax.random.normal(k4, (D_IN, D_V), jnp.float32) * std_qkv
        wo = jax.random.normal(k5, (D_V, D_MODEL), jnp.float32) * std_o
        return {'x': x, 'wq': wq, 'wk': wk, 'wv': wv, 'wo': wo}
    _L1_attn_in = _L1_attn_setup()

    def _L1_ffn_setup():
        import jax, jax.numpy as jnp
        import numpy as np
        NUM_EXPERTS = 8
        N_EMBD = 128
        D_FF = 4 * N_EMBD
        B, S = (4, 256)
        key = jax.random.key(seed)
        ks = jax.random.split(key, 6)
        x = jax.random.normal(ks[0], (B, S, N_EMBD), dtype=jnp.float32)
        gate_w = jax.random.normal(ks[1], (N_EMBD, NUM_EXPERTS), dtype=jnp.float32) * 0.02
        w1 = jax.random.normal(ks[2], (NUM_EXPERTS, N_EMBD, D_FF), dtype=jnp.float32) * 0.02
        b1 = jnp.zeros((NUM_EXPERTS, D_FF), dtype=jnp.float32)
        w2 = jax.random.normal(ks[3], (NUM_EXPERTS, D_FF, N_EMBD), dtype=jnp.float32) * 0.02
        b2 = jnp.zeros((NUM_EXPERTS, N_EMBD), dtype=jnp.float32)
        return {'x': x, 'gate_w': gate_w, 'w1': w1, 'b1': b1, 'w2': w2, 'b2': b2}
    _L1_ffn_in = _L1_ffn_setup()
    _d = {'L0_attn_hidden_states': _L0_attn_in['hidden_states'], 'L0_attn_Wq': _L0_attn_in['Wq'], 'L0_attn_bq': _L0_attn_in['bq'], 'L0_attn_Wk': _L0_attn_in['Wk'], 'L0_attn_bk': _L0_attn_in['bk'], 'L0_attn_Wv': _L0_attn_in['Wv'], 'L0_attn_bv': _L0_attn_in['bv'], 'L0_ffn_w_q': _L0_ffn_in['w_q'], 'L0_ffn_keys': _L0_ffn_in['keys'], 'L0_ffn_expert_down': _L0_ffn_in['expert_down'], 'L0_ffn_expert_up': _L0_ffn_in['expert_up'], 'L0_ffn_norm_w': _L0_ffn_in['norm_w'], 'L1_attn_wq': _L1_attn_in['wq'], 'L1_attn_wk': _L1_attn_in['wk'], 'L1_attn_wv': _L1_attn_in['wv'], 'L1_attn_wo': _L1_attn_in['wo'], 'L1_ffn_gate_w': _L1_ffn_in['gate_w'], 'L1_ffn_w1': _L1_ffn_in['w1'], 'L1_ffn_b1': _L1_ffn_in['b1'], 'L1_ffn_w2': _L1_ffn_in['w2'], 'L1_ffn_b2': _L1_ffn_in['b2']}
    _x0 = _d['L0_attn_hidden_states']
    _d['L0_attn_hidden_states'] = jax.random.normal(jax.random.fold_in(jax.random.key(seed), 1), (16, 256, 128), dtype=_x0.dtype)
    del _x0
    return _d

def reference(L0_attn_hidden_states, L0_attn_Wq, L0_attn_bq, L0_attn_Wk, L0_attn_bk, L0_attn_Wv, L0_attn_bv, L0_ffn_w_q, L0_ffn_keys, L0_ffn_expert_down, L0_ffn_expert_up, L0_ffn_norm_w, L1_attn_wq, L1_attn_wk, L1_attn_wv, L1_attn_wo, L1_ffn_gate_w, L1_ffn_w1, L1_ffn_b1, L1_ffn_w2, L1_ffn_b2):

    def _L0_attn_ref(hidden_states, Wq, bq, Wk, bk, Wv, bv):
        import jax, jax.numpy as jnp
        import numpy as np
        NUM_LANDMARKS = 64
        B, S, D = hidden_states.shape
        L = NUM_LANDMARKS
        q = hidden_states @ Wq + bq
        k = hidden_states @ Wk + bk
        v = hidden_states @ Wv + bv
        q = jax.nn.softmax(q, axis=-1)
        k = jax.nn.softmax(k, axis=-1)
        k_landmarks = k.reshape(B, L, S // L, D).mean(axis=2)
        kernel_1 = jnp.einsum('bqd,bkd->bqk', q, k_landmarks)
        kernel_2 = jnp.einsum('bkd,bld->bkl', k_landmarks, k)
        kernel_3 = k * v
        mid = jnp.einsum('bkl,bld->bkd', kernel_2, kernel_3)
        output = jnp.einsum('bqk,bkd->bqd', kernel_1, mid)
        return output

    def _L0_ffn_ref(x, w_q, keys, expert_down, expert_up, norm_w):
        import jax, jax.numpy as jnp
        import numpy as np
        B, T, D = (2, 128, 128)
        H, DK, K = (8, 128, 8)
        NKEYS = 32
        NEXP = NKEYS * NKEYS

        def _rmsnorm(x, w, eps=1e-06):
            inv = jax.lax.rsqrt(jnp.mean(x * x, axis=-1, keepdims=True) + eps)
            return x * inv * w
        b, t, d = x.shape
        xn = _rmsnorm(x, norm_w)
        q = (xn @ w_q.T).reshape(b, t, H, 2, DK)
        sim1 = jnp.einsum('bthd,hkd->bthk', q[..., 0, :], keys[:, :, 0, :])
        sim2 = jnp.einsum('bthd,hkd->bthk', q[..., 1, :], keys[:, :, 1, :])
        s1, i1 = jax.lax.top_k(sim1, K)
        s2, i2 = jax.lax.top_k(sim2, K)
        all_idx = (i1[..., :, None] * NKEYS + i2[..., None, :]).reshape(b, t, H, K * K)
        all_sc = (s1[..., :, None] + s2[..., None, :]).reshape(b, t, H, K * K)
        fs, pk = jax.lax.top_k(all_sc, K)
        fi = jnp.take_along_axis(all_idx, pk, axis=-1)
        wd = expert_down[fi]
        wu = expert_up[fi]
        hidden = jax.nn.gelu(jnp.einsum('btd,bthkd->bthk', xn, wd), approximate=False)
        hidden = hidden * jax.nn.relu(fs)
        return jnp.einsum('bthk,bthkd->btd', hidden, wu)

    def _L1_attn_ref(x, wq, wk, wv, wo):
        import jax, jax.numpy as jnp
        import numpy as np
        D_MODEL = 128
        NUM_HEADS = 16
        D_K = 128
        D_V = 128
        D_IN = 128
        THETA = 10000.0
        B, S = (2, 256)

        def _rope(t, theta):
            hd = t.shape[-1]
            inv_freq = 1.0 / theta ** (jnp.arange(0, hd, 2, dtype=jnp.float32) / hd)
            pos = jnp.arange(t.shape[-2], dtype=jnp.float32)
            ang = pos[:, None] * inv_freq[None, :]
            cos, sin = (jnp.cos(ang), jnp.sin(ang))
            tp = t.reshape(t.shape[:-1] + (hd // 2, 2))
            t0, t1 = (tp[..., 0], tp[..., 1])
            out = jnp.stack([t0 * cos - t1 * sin, t0 * sin + t1 * cos], axis=-1)
            return out.reshape(t.shape)
        b, s, _ = x.shape
        hd = D_K // NUM_HEADS
        hdv = D_V // NUM_HEADS
        q = jnp.einsum('bsd,de->bse', x, wq).reshape(b, s, NUM_HEADS, hd).transpose(2, 0, 1, 3)
        k = jnp.einsum('bsd,de->bse', x, wk).reshape(b, s, NUM_HEADS, hd).transpose(2, 0, 1, 3)
        v = jnp.einsum('bsd,de->bse', x, wv).reshape(b, s, NUM_HEADS, hdv).transpose(2, 0, 1, 3)
        q = _rope(q, THETA)
        k = _rope(k, THETA)
        scale = 1.0 / jnp.sqrt(jnp.asarray(hd, jnp.float32))
        scores = jnp.einsum('hbqd,hbkd->hbqk', q, k) * scale
        causal = jnp.tril(jnp.ones((s, s), dtype=bool))
        scores = jnp.where(causal, scores, -jnp.inf)
        attn = jax.nn.softmax(scores, axis=-1)
        o = jnp.einsum('hbqk,hbkd->hbqd', attn, v)
        o = o.transpose(1, 2, 0, 3).reshape(b, s, D_V)
        return jnp.einsum('bsd,de->bse', o, wo)

    def _L1_ffn_ref(x, gate_w, w1, b1, w2, b2):
        import jax, jax.numpy as jnp
        import numpy as np
        NUM_EXPERTS = 8
        N_EMBD = 128
        D_FF = 4 * N_EMBD
        B, S = (4, 256)
        Bb, Ss, D = x.shape
        x_flat = x.reshape(-1, D)
        router_logits = x_flat @ gate_w
        router_probs = jax.nn.softmax(router_logits, axis=-1)
        expert_idx = jnp.argmax(router_probs, axis=-1)
        expert_w = jnp.take_along_axis(router_probs, expert_idx[:, None], axis=1)[:, 0]
        out = jnp.zeros_like(x_flat)
        for e in range(NUM_EXPERTS):
            h = jax.nn.gelu(x_flat @ w1[e] + b1[e], approximate=False)
            y = h @ w2[e] + b2[e]
            sel = expert_idx == e
            out = out + jnp.where(sel, expert_w, 0.0)[:, None] * y
        return out.reshape(Bb, Ss, D)
    x = L0_attn_hidden_states
    xn = _layernorm(x, axis=-1)
    x = x + _L0_attn_ref(xn, L0_attn_Wq, L0_attn_bq, L0_attn_Wk, L0_attn_bk, L0_attn_Wv, L0_attn_bv) + _L0_ffn_ref(xn, L0_ffn_w_q, L0_ffn_keys, L0_ffn_expert_down, L0_ffn_expert_up, L0_ffn_norm_w)
    xn = _layernorm(x, axis=-1)
    x = x + _L1_attn_ref(xn, L1_attn_wq, L1_attn_wk, L1_attn_wv, L1_attn_wo) + _L1_ffn_ref(xn, L1_ffn_gate_w, L1_ffn_w1, L1_ffn_b1, L1_ffn_w2, L1_ffn_b2)
    return x

_drawn_inputs = setup_inputs


def setup_inputs(seed=0):
    import zlib

    import numpy as np

    out = dict(_drawn_inputs(seed))
    spreads = {'L0_attn_bq': (0.0, 2.0),
     'L0_attn_bk': (0.0, 2.0),
     'L0_attn_bv': (0.0, 2.0),
     'L0_ffn_norm_w': (1.0, 0.6),
     'L1_ffn_b1': (0.0, 2.0),
     'L1_ffn_b2': (0.0, 2.0)}
    factors = {'L0_attn_Wq': 64.0,
     'L0_attn_Wk': 64.0,
     'L0_attn_Wv': 64.0,
     'L0_ffn_w_q': 8.0,
     'L0_ffn_keys': 8.0,
     'L0_ffn_expert_down': 8.0,
     'L0_ffn_expert_up': 8.0,
     'L1_ffn_gate_w': 9.817,
     'L1_ffn_w1': 25.864,
     'L1_ffn_w2': 18.325,
     'L1_attn_wq': 8.0,
     'L1_attn_wk': 8.0,
     'L1_attn_wv': 8.0,
     'L1_attn_wo': 8.0}
    for name, (base, spread) in spreads.items():
        noise = np.random.default_rng([zlib.crc32(name.encode()), seed]).standard_normal(out[name].shape)
        drawn = base * np.exp(spread * noise) if base else spread * noise
        out[name] = jnp.asarray(drawn.astype(out[name].dtype))
    for name, factor in factors.items():
        out[name] = (out[name] * factor).astype(out[name].dtype)
    return out
```

```python
from contextlib import ExitStack

import concourse.bass as bass
from concourse import mybir

F32 = mybir.dt.float32
BF16 = mybir.dt.bfloat16
I32 = mybir.dt.int32
U32 = mybir.dt.uint32
ALU = mybir.AluOpType
ACT = mybir.ActivationFunctionType
AX_X = mybir.AxisListType.X

P = 128
D = 128
B, S = 16, 256
TB = S // P
NT = B * TB
LAND = 64
PH, NKEYS, TOPK = 8, 32, 8
NEXP = NKEYS * NKEYS
EC = NEXP // P
NH, HD = 16, 8
NE, FF = 8, 512
FC = FF // P
ST = NT + NE - 1
SLOTS = 6
HB = 64
QPART = (0, 1, 2, 0, 0, 1)
KPART = (0, 1, 0, 2, 1, 0)
UNITS = TB * PH
RING = 3
ZC = 256

C_IDENT, C_POOL, C_MASKQ, C_MASKK, C_TRI = 0, 128, 256, 384, 512
C_COS, C_SIN = 640, 896
C_IOTA8, C_IOTAST = 1152, 1160
C_SEL = C_IOTAST + ST
C_ALL = C_SEL + NH * P
C_STAY = C_SEL


def shape_constants(np):
    c = np.zeros((P, C_ALL), np.float32)
    r = np.arange(P)
    c[:, C_IDENT:C_IDENT + P] = np.eye(P)
    for t in range(TB):
        c[r, C_POOL + LAND * t + 32 * t + r // 4] = 0.25
    c[:, C_MASKQ:C_MASKQ + P] = np.where(r[None, :] > r[:, None], -1e30, 0.0)
    c[:, C_MASKK:C_MASKK + P] = np.where(r[:, None] > r[None, :], -1e30, 0.0)
    c[:, C_TRI:C_TRI + P] = r[:, None] < r[None, :]
    freq = (1.0 / 10000.0 ** (np.arange(0, HD, 2, dtype=np.float32) / HD)).astype(np.float32)
    ang = (np.arange(S, dtype=np.float32)[:, None] * freq[None, :]).astype(np.float32)
    for t in range(TB):
        for base, tab in ((C_COS, np.cos(ang)), (C_SIN, np.sin(ang))):
            rows = np.tile(tab[t * P:(t + 1) * P], (1, 2 * NH)).astype(np.float32)
            rows[:, :NH * HD // 2] *= np.float32(1.0 / np.sqrt(np.float32(HD)))
            c[:, base + P * t:base + P * (t + 1)] = rows
    c[:, C_IOTA8:C_IOTA8 + NE] = np.arange(NE)
    c[:, C_IOTAST:C_IOTAST + ST] = np.arange(ST)
    for h in range(NH):
        for half in (0, HB):
            c[half + 3 * h:half + 3 * h + 3, C_SEL + P * h:C_SEL + P * (h + 1)] = 1.0
    return c


class Marks:

    def __init__(self, eng, sem, base):
        self.eng, self.sem, self.base, self.n = eng, sem, base, 0

    def did(self, ins):
        ins.then_inc(self.sem, 1)
        self.n += 1
        return self.n

    def need(self, n):
        self.eng.wait_ge(self.sem, self.base + n)


def bc(ap, axis, n):
    ap = ap.unsqueeze(axis)
    return ap.broadcast_to([n if k == axis else s for k, s in enumerate(ap.shape)])


def build(nc, x, Wq, bq, Wk, bk, Wv, bv, w_q, keys, e_down, e_up, norm_w, wq1, wk1, wv1, wo1,
          gate_w, w1, b1, w2, b2, consts, out):
    with ExitStack() as ctx:
        def sb(name, shape, dt=F32):
            return ctx.enter_context(nc.sbuf_tensor(name, shape, dt))

        def sem(name):
            return ctx.enter_context(nc.semaphore(name))

        bank = [ctx.enter_context(nc.psum_tensor(f"bank{k}", [P, 512], F32)) for k in range(8)]

        cst = sb("cst", [P, C_STAY])
        ident = cst[:, C_IDENT:C_IDENT + P]
        pool_mat = cst[:, C_POOL:C_POOL + TB * LAND].rearrange("p (t l) -> p t l", t=TB)
        ones = sb("ones", [P, P])
        ident_b = sb("ident_b", [P, P], BF16)
        mask_q = sb("mask_q", [P, 2, P], BF16)
        mask_k = sb("mask_k", [P, 2, P], BF16)
        sel_b = sb("sel_b", [P, NH * P], BF16)
        wqkv0 = sb("wqkv0", [P, 3 * D])
        bqkv0 = sb("bqkv0", [P, 3 * D])
        keysT = sb("keysT", [P, 512])
        fold = sb("fold", [P, 512])
        downT = sb("downT", [P, NEXP])
        up = sb("up", [P, EC, D])
        nw = sb("nw", [P, 1])
        wqkvg1 = sb("wqkvg1", [P, 3 * D + NE])
        wo_sb = sb("wo_sb", [P, D])
        w1_sb = sb("w1_sb", [P, NE * FF])
        w2_sb = sb("w2_sb", [P, NE * FC * D])
        b1_rows = sb("b1_rows", [NE * FC, P])
        b1_sb = sb("b1_sb", [P, NE * FC])
        b2_sb = sb("b2_sb", [P, NE * D])
        xall = sb("xall", [P, NT * D])
        xn1all = sb("xn1all", [P, NT * D])
        onehot = sb("onehot", [P, NT * NE])
        esum = sb("esum", [P, NT])
        st = sb("st", [P, TB, 6])
        mv = sb("mv", [P, TB, 2])
        sc = sb("sc", [P, 2, TB])
        sv = sb("sv", [P, 2, TB])
        sq = sb("sq", [P, 2, TB])
        xr = sb("xr", [P, 2, TB, D])
        xrT = sb("xrT", [P, 512])
        z = sb("z", [P, TB, 3, D])
        zmax = sb("zmax", [P, TB, 2])
        ez = sb("ez", [P, TB, 2, D])
        zsum = sb("zsum", [P, TB, 2])
        zrec = sb("zrec", [P, TB, 2])
        kk_sb = sb("kk_sb", [P, TB, D])
        kv_sb = sb("kv_sb", [P, TB, D])
        klS = sb("klS", [LAND, D])
        hS = sb("hS", [P, D])
        eqT = sb("eqT", [P, TB * P])
        gS = sb("gS", [P, D])
        mS = sb("mS", [P, D])
        sims = sb("sims", [P, TB, 2 * PH, NKEYS])
        top = sb("top", [P, TB, 2 * PH, TOPK])
        pair = sb("pair", [P, TB, PH, TOPK * TOPK])
        best = sb("best", [P, TB, PH, TOPK])
        tau = sb("tau", [P, UNITS])
        g = sb("g", [P, 2, NEXP])
        m = sb("m", [P, RING, NEXP])
        coef = sb("coef", [P, TB, NEXP])
        wqp = g[:].rearrange("p a (b d) -> p (a b) d", d=D)
        down_rows = m[:, 0, :].rearrange("p (c d) -> p c d", d=D)
        key_rows = m[:, 1, 0:512].rearrange("p (c d) -> p c d", d=D)
        sel_rows = coef[:].rearrange("p t e -> p (t e)")
        hid = sb("hid", [P, 4, 512])
        hc = sb("hc", [P, 2, 512])
        xn1 = sb("xn1", [P, TB, D])
        xn1T = sb("xn1T", [P, TB * P])
        ra = sb("ra", [P, 2 * NH * HD])
        rb = sb("rb", [P, 2 * NH * HD])
        rot = sb("rot", [P, TB, 2, NH * HD])
        vaug = sb("vaug", [P, TB, NH, HD + 1])
        lg = sb("lg", [P, TB, NE])
        lg8 = sb("lg8", [P, TB, 8])
        lgi = sb("lgi", [P, TB, 8], U32)
        lgf = sb("lgf", [P, TB])
        lgneg = sb("lgneg", [P, TB])
        lge = sb("lge", [P, TB, NE])
        lgs = sb("lgs", [P, TB])
        split = sb("split", [P, TB, 2, NH, HB], BF16)
        rest = sb("rest", [P, TB * 2 * NH, HD])
        QT = sb("QT", [P, NH // 2, TB * P], BF16)
        KT = sb("KT", [P, NH // 2, TB * P], BF16)
        smax = sb("smax", [P, TB, NH])
        srest = sb("srest", [P, TB, NH])
        nmp = sb("nmp", [P, TB, 2, HB], BF16)
        nm = nmp[:, :, 0, 0:3 * NH].rearrange("p t (h r) -> p t h r", r=3)
        nmT = sb("nmT", [P, TB * P], BF16)
        pT = sb("pT", [P, 3, 384])
        orec = sb("orec", [P, TB, NH])
        o_sb = sb("o_sb", [P, TB, D])
        oT = sb("oT", [P, TB * P])
        rank = sb("rank", [P, NT * NE])
        tot = sb("tot", [P, NT * NE])
        incl = sb("incl", [P, NE, NT])
        ntile_i = sb("ntile_i", [P, NE], I32)
        ntile = sb("ntile", [P, NE])
        nincl = sb("nincl", [P, NE])
        dest = sb("dest", [P, NT])
        dest_u = sb("dest_u", [P, NT], U32)
        tcmp = sb("tcmp", [P, ST, NE])
        tile_e = sb("tile_e", [P, ST])
        tile_ei = sb("tile_ei", [P, ST], I32)
        xs = sb("xs", [P, RING, D])
        xsT = sb("xsT", [P, RING, P])
        hT = hid[:, 0:RING, :].rearrange("p k (c q) -> p k c q", q=P)
        w1e = m[:, :, 0:FF]
        ys = hc[:, 0, 0:RING * D].rearrange("p (k d) -> p k d", d=D)
        yg = sb("yg", [P, 4, D])
        fin = pair[:, 0].rearrange("p (a b) c -> p a (b c)", a=4)
        zero = sb("zero", [P, ZC])

        tick = sb("tick", [P, 1])

        y_bank = (6, 7, 1)

        xsorted = nc.dram_tensor("xsorted", [ST * P, D], F32, kind="Internal").ap()
        ysorted = nc.dram_tensor("ysorted", [ST * P, D], F32, kind="Internal").ap()

        S_ = {n: sem(n) for n in (
            "loaded_consts", "loaded_x", "loaded_setup", "loaded_w", "pe_setup", "act_setup", "dve_setup",
            "v_setup",
            "l0_v", "l0_norm", "l0_xrT_ps", "l0_xrT", "l0_qkv_ps", "l0_sim_ps", "l0_z", "l0_zmax",
            "l0_exp", "l0_sims", "l0_kv", "l0_kl_ps", "l0_kl", "l0_g_ps", "l0_g", "l0_m_ps", "l0_m",
            "l0_att_ps", "l0_att", "l0_mask", "l0_coef", "l0_down_ps", "l0_hid", "l0_cT_ps", "l0_hc",
            "l0_up_ps", "l0_x1", "l0_xn1", "l0_xn1T_ps", "l0_xn1T", "l0_kept",
            "l1_v", "l1_qkv_ps", "l1_qkv", "l1_lgneg", "l1_lgsum", "l1_part", "l1_rest", "l1_low",
            "l1_split", "l1_T_ps", "l1_T", "l1_s_ps", "l1_max", "l1_nm", "l1_nmT_ps", "l1_nmT", "l1_p_ps", "l1_p",
            "l1_pv", "l1_o", "l1_oT_ps", "l1_oT", "l1_wo_ps", "l1_x2",
            "r_v", "zeroed", "r_rank_ps", "r_dest", "r_te", "scattered", "f_xT_ps", "f_w1", "f_xT", "f_h_ps",
            "f_h", "f_y_ps", "f_y", "final")}
        s = type("Semaphores", (), S_)
        tile_loaded = [sem(f"tile_loaded{k}") for k in range(RING)]
        tile_stored = [sem(f"tile_stored{k}") for k in range(RING)]
        gathered = [sem(f"gathered{k}") for k in range(4)]
        out_stored = [sem(f"out_stored{k}") for k in range(4)]

        def since(e, which, i, per, n):
            if isinstance(i, int) and i * per + n - per <= 0:
                return
            e.wait_ge(which, i * per + (n - per))

        def apart(e):
            e.wait_ge(s.dve_setup, 1)

        N_L0V, N_L1V = 71, 23

        block = ctx.enter_context(nc.Block())

        @block.sync
        def _(sp):
            sp.dma_start(cst[:], consts[:, 0:C_STAY]).then_inc(s.loaded_consts, 16)
            sp.dma_start(sel_rows, consts[:, C_SEL:C_ALL]).then_inc(s.loaded_consts, 16)
            xv = x.rearrange("b (t p) d -> p (b t) d", p=P)
            xs_ = xall[:].rearrange("p (n d) -> p n d", d=D)
            for q in range(4):
                sp.dma_start(xs_[:, q * 8:(q + 1) * 8, :], xv[:, q * 8:(q + 1) * 8, :]).then_inc(s.loaded_x, 16)
            for k, (w, b) in enumerate(((Wq, bq), (Wk, bk), (Wv, bv))):
                sp.dma_start(wqkv0[:, k * D:(k + 1) * D], w).then_inc(s.loaded_setup, 16)
                sp.dma_start(bqkv0[:, k * D:(k + 1) * D], b.rearrange("(o d) -> o d", o=1).broadcast_to([P, D])).then_inc(s.loaded_setup, 16)
            for k, w in enumerate((wq1, wk1, wv1)):
                sp.dma_start(wqkvg1[:, k * D:(k + 1) * D], w).then_inc(s.loaded_setup, 16)
            sp.dma_start(wqkvg1[:, 3 * D:], gate_w).then_inc(s.loaded_setup, 16)
            sp.dma_start(wo_sb[:], wo1).then_inc(s.loaded_setup, 16)
            sp.wait_ge(s.scattered, 16 * NT)
            for k in range(RING):
                sp.dma_start(xs[:, k, :], xsorted[k * P:(k + 1) * P, :]).then_inc(tile_loaded[k], 16)

            def store(r, k):
                sp.wait_ge(s.f_y, r * RING + (k + 1))
                sp.dma_start(ysorted[bass.ds(r * (RING * P) + k * P, P), :], ys[:, k, :]).then_inc(tile_stored[k], 16)

            with sp.Fori(1, ST // RING) as r:
                for k in range(RING):
                    since(sp, s.f_xT_ps, r, RING, k + 1)
                    sp.dma_start(xs[:, k, :], xsorted[bass.ds(r * (RING * P) + k * P, P), :]).then_inc(tile_loaded[k], 16)
                    store(r - 1, k)
            for k in range(RING):
                store(ST // RING - 1, k)

        @block.gpsimd
        def _(pool):
            pool.dma_start(key_rows, keys.rearrange("h k s d -> (h k s) d").rearrange("(c p) d -> p c d", p=P)).then_inc(s.loaded_w, 16)
            pool.dma_start(wqp, w_q.rearrange("(c p) d -> p c d", p=P)).then_inc(s.loaded_w, 16)
            pool.dma_start(down_rows, e_down.rearrange("(c p) d -> p c d", p=P)).then_inc(s.loaded_w, 16)
            pool.dma_start(up[:], e_up.rearrange("(c p) d -> p c d", p=P)).then_inc(s.loaded_w, 16)
            pool.dma_start(nw[:], norm_w.rearrange("(d o) -> d o", o=1)).then_inc(s.loaded_w, 16)
            pool.dma_start(b1_rows[:], b1.rearrange("e (c p) -> (e c) p", p=P)).then_inc(s.loaded_w, 16)
            pool.dma_start(w1_sb[:].rearrange("p (e f) -> p e f", e=NE), w1.rearrange("e d f -> d e f")).then_inc(s.loaded_w, 16)
            pool.dma_start(w2_sb[:].rearrange("p (e d) -> p e d", d=D), w2.rearrange("e (c p) d -> p (e c) d", p=P)).then_inc(s.loaded_w, 16)
            pool.dma_start(b2_sb[:], b2.rearrange("(o e) d -> o (e d)", o=1).broadcast_to([P, NE * D])).then_inc(s.loaded_w, 16)
            pool.wait_ge(s.dve_setup, 1)
            xz = xsorted.rearrange("(p r) d -> p (r d)", p=P)
            done = 0
            while done < ST * D:
                n = min(ZC, ST * D - done)
                pool.dma_start(xz[:, done:done + n], zero[:, 0:n]).then_inc(s.zeroed, 16)
                done += n

            def layer0(i):
                for u in range(UNITS):
                    t, h = u // PH, u % PH
                    if h == 0:
                        continue
                    pool.wait_ge(s.l0_mask, i * UNITS + (u + 1))
                    k = t * (PH - 1) + h
                    if h > 1:
                        pool.wait_ge(s.l0_coef, i * (UNITS - TB) + (k - 1))
                    pool.tensor_tensor(coef[:, t, :], coef[:, t, :], m[:, u % RING, :], ALU.add).then_inc(s.l0_coef, 1)

            layer0(0)
            with pool.Fori(1, B) as i:
                layer0(i)

            pool.wait_ge(s.zeroed, 16 * -(-ST * D // ZC))
            pool.wait_ge(s.r_dest, 1)
            for n in range(NT):
                pool.indirect_dma_start(xsorted, bass.IndirectOffsetOnAxis(ap=dest_u[:, n:n + 1], axis=0),
                                        xn1all[:, n * D:(n + 1) * D], None).then_inc(s.scattered, 16)
            for k in range(RING):
                pool.wait_ge(tile_stored[k], 16 * (ST // RING))
            for n in range(NT):
                if n >= 4:
                    pool.wait_ge(s.final, n - 3)
                pool.indirect_dma_start(yg[:, n % 4, :], None, ysorted,
                                        bass.IndirectOffsetOnAxis(ap=dest_u[:, n:n + 1], axis=0)).then_inc(gathered[n % 4], 16)

        @block.tensor
        def _(pe):
            mm = pe.matmul

            pe.wait_ge(s.loaded_consts, 32)
            pe.wait_ge(s.loaded_w, 16 * 9)
            for c in range(4):
                ins = pe.transpose(bank[0][:, c * P:(c + 1) * P], key_rows[:, c, :], ident)
            ins.then_inc(s.pe_setup, 1)
            for c in range(EC):
                ins = pe.transpose(bank[1 + c // 4][:, (c % 4) * P:(c % 4 + 1) * P], down_rows[:, c, :], ident)
            ins.then_inc(s.pe_setup, 1)
            pe.transpose(bank[3][:, 0:NE * FC], b1_rows[:], ident[0:NE * FC, 0:NE * FC]).then_inc(s.pe_setup, 1)
            pe.wait_ge(s.act_setup, 1)
            kT = keysT[:].rearrange("p (h k s) -> p h s k", h=PH, s=2)
            for c in range(2 * PH):
                ins = mm(bank[4][:, c * NKEYS:(c + 1) * NKEYS], wqp[:, c, :], kT[:, c // 2, c % 2, :],
                         start=True, stop=True)
            ins.then_inc(s.pe_setup, 1)
            pe.wait_ge(s.act_setup, 5)
            pe.wait_ge(s.dve_setup, 1)
            pe.wait_ge(s.loaded_setup, 16 * 11)

            def l1_front(j):
                pe.wait_ge(s.l0_xn1T, j + 1)
                pe.wait_ge(s.l1_x2, j + 1)
                for t in range(TB):
                    mm(bank[7 - t][:, 0:3 * D + NE], xn1T[:, t * P:(t + 1) * P], wqkvg1[:], start=True,
                       stop=True).then_inc(s.l1_qkv_ps, 1)

            def l1_turn(j):
                pe.wait_ge(s.l1_split, j * 4 + 4)
                pe.wait_ge(s.l1_qkv, j * 2 + 2)
                for n, (t, w) in enumerate(((0, 0), (0, 1), (1, 0), (1, 1))):
                    b = bank[4 + n][:].bitcast(BF16)
                    for c in range(NH // 2):
                        src = split[:, t, w, 2 * c:2 * c + 2, :].rearrange("p h c -> p (h c)")
                        ins = pe.transpose(b[:, c * P:(c + 1) * P], src, ident_b[:])
                    ins.then_inc(s.l1_T_ps, 1)

            def head(ap, h):
                return ap[HB * (h % 2):HB * (h % 2) + SLOTS * HD, h // 2, :]

            def l1_score(j, h):
                if h == 0:
                    pe.wait_ge(s.l1_T, j * 4 + 4)
                if h >= RING:
                    pe.wait_ge(s.l1_max, j * NH + (h - RING + 1))
                b, q, k = bank[4 + h % RING], head(QT, h), head(KT, h)
                mm(b[:, 128:384], ident_b[:], mask_q[:], start=True, stop=False, skip_group_check=True)
                mm(b[:, 0:256], q[:, P:2 * P], k, start=False, stop=False, skip_group_check=True)
                mm(b[:, 256:384], q[:, 0:P], k[:, 0:P], start=False, stop=True,
                   skip_group_check=True).then_inc(s.l1_s_ps, 1)

            def l1_turn_max(j):
                pe.wait_ge(s.l1_nm, j + 1)
                b = bank[7][:].bitcast(BF16)
                for t in range(TB):
                    ins = pe.transpose(b[:, t * P:(t + 1) * P], nmp[:, t].rearrange("p c r -> p (c r)"), ident_b[:])
                ins.then_inc(s.l1_nmT_ps, 1)

            def l1_prob(j, h):
                if h == 0:
                    pe.wait_ge(s.l1_nmT, j + 1)
                    pe.wait_ge(s.l1_max, j * NH + NH)
                if h >= RING:
                    pe.wait_ge(s.l1_p, j * NH + (h - RING + 1))
                b, q, k = bank[4 + h % RING], head(QT, h), head(KT, h)
                diag = b[:, 0:512].rearrange("p (a c) -> p a c", a=2)[:, :, 0:P]
                mm(diag, ident_b[:], mask_k[:], start=True, stop=False, skip_group_check=True)
                mm(b[:, 0:256], k[:, 0:P], q, start=False, stop=False, skip_group_check=True)
                mm(b[:, 256:384], k[:, P:2 * P], q[:, P:2 * P], start=False, stop=False, skip_group_check=True)
                half = slice(HB * (h % 2), HB * (h % 2) + 3 * NH)
                sel = sel_b[half, h * P:(h + 1) * P]
                mm(b[:, 0:256], sel, nmT[half, :], start=False, stop=False, skip_group_check=True)
                mm(b[:, 256:384], sel, nmT[half, P:2 * P], start=False, stop=True,
                   skip_group_check=True).then_inc(s.l1_p_ps, 1)

            def l1_values(j, h):
                pe.wait_ge(s.l1_p, j * NH + (h + 1))
                o = bank[7][:, 0:TB * NH * (HD + 1)].rearrange("p (t h d) -> p t h d", t=TB, h=NH)
                p = pT[:, h % RING, :]
                mm(o[:, 0, h, :], p[:, 0:P], vaug[:, 0, h, :], start=(h == 0), stop=False, skip_group_check=True)
                mm(o[:, 1, h, :], p[:, P:2 * P], vaug[:, 0, h, :], start=False, stop=False, skip_group_check=True)
                mm(o[:, 1, h, :], p[:, 2 * P:3 * P], vaug[:, 1, h, :], start=False, stop=(h == NH - 1),
                   skip_group_check=True).then_inc(s.l1_pv, 1)

            def l1_out(j):
                pe.wait_ge(s.l1_o, j + 1)
                for t in range(TB):
                    ins = pe.transpose(bank[7][:, t * P:(t + 1) * P], o_sb[:, t, :], ident)
                ins.then_inc(s.l1_oT_ps, 1)
                pe.wait_ge(s.l1_oT, j + 1)
                for t in range(TB):
                    ins = mm(bank[6][:, t * P:(t + 1) * P], oT[:, t * P:(t + 1) * P], wo_sb[:], start=True, stop=True)
                ins.then_inc(s.l1_wo_ps, 1)

            def l0_front(i):
                pe.wait_ge(s.l0_norm, i + 1)
                since(pe, s.l0_xn1T, i, 1, 1)
                for w in range(2):
                    for t in range(TB):
                        ins = pe.transpose(bank[0][:, (w * TB + t) * P:(w * TB + t + 1) * P], xr[:, w, t, :], ident)
                ins.then_inc(s.l0_xrT_ps, 1)
                pe.wait_ge(s.l0_xrT, i + 1)
                since(pe, s.l0_x1, i, 1, 1)
                for t in range(TB):
                    mm(bank[1 + t][:, 0:3 * D], xrT[:, t * P:(t + 1) * P], wqkv0[:], start=True,
                       stop=True).then_inc(s.l0_qkv_ps, 1)
                for t in range(TB):
                    mm(bank[3 - 3 * t][:], xrT[:, (TB + t) * P:(TB + t + 1) * P], fold[:], start=True,
                       stop=True).then_inc(s.l0_sim_ps, 1)

            def l0_attention(i):
                pe.wait_ge(s.l0_kv, i + 1)
                for t in range(TB):
                    mm(bank[1][0:LAND, 0:D], pool_mat[:, t, :], kk_sb[:, t, :], start=(t == 0), stop=(t == 1))
                for t in range(TB):
                    mm(bank[1][:, D:2 * D], kk_sb[:, t, :], kv_sb[:, t, :], start=(t == 0), stop=(t == 1))
                for t in range(TB):
                    ins = pe.transpose(bank[2][:, t * P:(t + 1) * P], ez[:, t, 0, :], ident)
                ins.then_inc(s.l0_kl_ps, 1)
                pe.wait_ge(s.l0_kl, i * 3 + 3)
                mm(bank[2][:, 0:D], klS[:], klS[:], start=True, stop=True).then_inc(s.l0_g_ps, 1)
                pe.wait_ge(s.l0_g, i + 1)
                mm(bank[1][:, 0:D], gS[:], hS[:], start=True, stop=True).then_inc(s.l0_m_ps, 1)
                pe.wait_ge(s.l0_m, i + 1)
                for t in range(TB):
                    ins = mm(bank[2][:, t * P:(t + 1) * P], eqT[:, t * P:(t + 1) * P], mS[:], start=True, stop=True)
                ins.then_inc(s.l0_att_ps, 1)

            def l0_down(i):
                for c in range(EC // 2):
                    if c:
                        pe.wait_ge(s.l0_hid, i * 4 + c)
                    for a in range(2):
                        e = 2 * c + a
                        ins = mm(bank[1][:, a * 256:(a + 1) * 256], downT[:, e * P:(e + 1) * P], xrT[:, 256:512],
                                 start=True, stop=True)
                    ins.then_inc(s.l0_down_ps, 1)

            def l0_up(i):
                pe.wait_ge(s.l0_coef, i * (UNITS - TB) + (UNITS - TB))
                pe.wait_ge(s.l0_hid, i * 4 + 4)
                for c in range(EC // 2 + 1):
                    if c < EC // 2:
                        if c >= 2:
                            pe.wait_ge(s.l0_hc, i * 4 + (c - 1))
                        for a in range(2):
                            for t in range(TB):
                                e = 2 * c + a
                                ins = pe.transpose(bank[1 + c % 2][:, (a * TB + t) * P:(a * TB + t + 1) * P],
                                                   coef[:, t, e * P:(e + 1) * P], ident)
                        ins.then_inc(s.l0_cT_ps, 1)
                    if c >= 1:
                        pe.wait_ge(s.l0_hc, i * 4 + c)
                        for a in range(2):
                            for t in range(TB):
                                e = 2 * (c - 1) + a
                                ins = mm(bank[3][:, t * P:(t + 1) * P],
                                         hc[:, (c - 1) % 2, (a * TB + t) * P:(a * TB + t + 1) * P], up[:, e, :],
                                         start=(e == 0 and t == 0), stop=(e == EC - 1), skip_group_check=True)
                        ins.then_inc(s.l0_up_ps, 1)
                pe.wait_ge(s.l0_xn1, i + 1)
                for t in range(TB):
                    ins = pe.transpose(bank[0][:, t * P:(t + 1) * P], xn1[:, t, :], ident)
                ins.then_inc(s.l0_xn1T_ps, 1)

            def body(i, j):
                if j is not None:
                    l1_front(j)
                if i is not None:
                    l0_front(i)
                if j is not None:
                    l1_turn(j)
                if i is not None:
                    l0_attention(i)
                    l0_down(i)
                if j is not None:
                    for h in range(NH):
                        l1_score(j, h)
                    l1_turn_max(j)
                    for h in range(NH + 1):
                        if h < NH:
                            l1_prob(j, h)
                        if h:
                            l1_values(j, h - 1)
                    l1_out(j)
                if i is not None:
                    l0_up(i)

            body(0, None)
            with pe.Fori(1, B) as i:
                body(i, i - 1)
            body(None, B - 1)

            pe.wait_ge(s.l1_x2, B + 1)
            mm(bank[0][:, 0:NT * NE], cst[:, C_TRI:C_TRI + P], onehot[:], start=True, stop=True)
            mm(bank[1][:, 0:NT * NE], ones[:], onehot[:], start=True, stop=True).then_inc(s.r_rank_ps, 1)

            pe.wait_ge(s.r_te, 1)

            def turn(r, k):
                n = r * RING + k
                pe.wait_ge(tile_loaded[k], r * 16 + 16)
                if not isinstance(n, int) or n:
                    pe.wait_ge(s.f_xT, n)
                pe.transpose(bank[2][:, 0:P], xs[:, k, :], ident).then_inc(s.f_xT_ps, 1)

            def hidden(r, k):
                n = r * RING + k
                pe.wait_ge(s.f_xT, n + 1)
                pe.wait_ge(s.f_w1, n + 1)
                since(pe, s.f_h, r, RING * FC, (k + 1) * FC)
                for c in range(FC):
                    ins = mm(bank[3 + k][:, c * P:(c + 1) * P], w1e[:, k, c * P:(c + 1) * P],
                             xsT[:, k, :], start=True, stop=True)
                ins.then_inc(s.f_h_ps, 1)

            def result(r, k):
                n = r * RING + k
                e = pe.value_load(tile_ei[0:1, bass.ds(n, 1)], min_val=0, max_val=NE - 1)
                pe.wait_ge(s.f_h, n * FC + FC)
                since(pe, s.f_y, r, RING, k + 1)
                for c in range(FC):
                    ins = mm(bank[y_bank[k]][:, 0:D], hT[:, k, c, :], w2_sb[:, bass.ds(e * (FC * D) + c * D, D)],
                             start=(c == 0), stop=(c == FC - 1))
                ins.then_inc(s.f_y_ps, 1)

            def sorted_tiles(r, last=False):
                for k in range(RING):
                    if not (last and k + 2 >= RING):
                        turn(r + (k + 2) // RING, (k + 2) % RING)
                    if not (last and k + 1 >= RING):
                        hidden(r + (k + 1) // RING, (k + 1) % RING)
                    result(r, k)

            turn(0, 0)
            turn(0, 1)
            hidden(0, 0)
            sorted_tiles(0)
            with pe.Fori(1, ST // RING - 1) as r:
                sorted_tiles(r)
            sorted_tiles(ST // RING - 1, last=True)

        @block.scalar
        def _(act):
            def copy(o, i_):
                return act.activation(o, i_, ACT.Copy)

            act.wait_ge(s.pe_setup, 1)
            copy(keysT[:], bank[0][:]).then_inc(s.act_setup, 1)
            act.wait_ge(s.pe_setup, 2)
            for c in range(2):
                act.activation(downT[:, c * 512:(c + 1) * 512], bank[1 + c][:], ACT.Copy, scale=nw[:, 0:1]).then_inc(s.act_setup, 1)
            act.wait_ge(s.pe_setup, 3)
            copy(b1_sb[:], bank[3][:, 0:NE * FC]).then_inc(s.act_setup, 1)
            act.wait_ge(s.pe_setup, 4)
            act.activation(fold[:], bank[4][:], ACT.Copy, scale=nw[:, 0:1]).then_inc(s.act_setup, 1)

            def l0_front(i):
                act.wait_ge(s.l0_xrT_ps, i + 1)
                copy(xrT[:], bank[0][:]).then_inc(s.l0_xrT, 1)
                for t in range(TB):
                    act.wait_ge(s.l0_sim_ps, i * TB + (t + 1))
                    copy(sims[:, t].rearrange("p g k -> p (g k)"), bank[3 - 3 * t][:]).then_inc(s.l0_sims, 1)

            def l0_exp(i):
                act.wait_ge(s.l0_zmax, i + 1)
                for t in range(TB):
                    for w in range(2):
                        act.activation(ez[:, t, w, :], z[:, t, w, :], ACT.Exp, bias=zmax[:, t, w:w + 1],
                                       accum_out=zsum[:, t, w:w + 1]).then_inc(s.l0_exp, 1)

            def l0_attention(i):
                act.wait_ge(s.l0_kl_ps, i + 1)
                copy(klS[:], bank[1][0:LAND, 0:D]).then_inc(s.l0_kl, 1)
                copy(hS[:], bank[1][:, D:2 * D]).then_inc(s.l0_kl, 1)
                copy(eqT[:], bank[2][:, 0:TB * P]).then_inc(s.l0_kl, 1)
                act.wait_ge(s.l0_g_ps, i + 1)
                copy(gS[:], bank[2][:, 0:D]).then_inc(s.l0_g, 1)
                act.wait_ge(s.l0_m_ps, i + 1)
                copy(mS[:], bank[1][:, 0:D]).then_inc(s.l0_m, 1)

            def l0_down(i):
                for c in range(EC // 2):
                    act.wait_ge(s.l0_down_ps, i * 4 + (c + 1))
                    act.activation(hid[:, c, :], bank[1][:], ACT.Gelu).then_inc(s.l0_hid, 1)

            def l0_end(i):
                act.wait_ge(s.l0_xn1T_ps, i + 1)
                copy(xn1T[:], bank[0][:, 0:TB * P]).then_inc(s.l0_xn1T, 1)
                copy(xn1all[:, bass.ds(i * (TB * D), TB * D)], xn1[:].rearrange("p t d -> p (t d)")).then_inc(s.l0_kept, 1)

            def l1_split(j):
                for t in range(TB):
                    act.wait_ge(s.l1_lgneg, j + 1)
                    act.activation(lge[:, t, :], lg[:, t, :], ACT.Exp, bias=lgneg[:, t:t + 1],
                                   accum_out=lgs[:, t:t + 1]).then_inc(s.l1_lgsum, 1)
                act.wait_ge(s.l1_qkv, j * 2 + 2)
                sp_all = split[:].rearrange("p t w h c -> p (t w h) c")
                r_all = rot[:].rearrange("p t w (h d) -> p (t w h) d", d=HD)
                copy(sp_all[:, :, 0:HD], r_all).then_inc(s.l1_part, 1)

                def extra(src, w, part, ins=None):
                    for t in range(TB):
                        v = src[:].rearrange("p (t w h) d -> p t w h d", t=TB, w=2)[:, t, w] if src is rest else \
                            src[:, t, w, :].rearrange("p (h d) -> p h d", d=HD)
                        for n, which in enumerate((QPART, KPART)[w]):
                            if which == part and n != part:
                                ins = copy(split[:, t, w, :, n * HD:(n + 1) * HD], v)
                    return ins

                extra(rot, 0, 0)
                extra(rot, 1, 0).then_inc(s.l1_split, 1)
                act.wait_ge(s.l1_rest, j + 1)
                copy(sp_all[:, :, HD:2 * HD], rest[:]).then_inc(s.l1_part, 1)
                extra(rest, 0, 1)
                extra(rest, 1, 1).then_inc(s.l1_split, 1)

            def l1_turn(j):
                for n, (t, w) in enumerate(((0, 0), (0, 1), (1, 0), (1, 1))):
                    act.wait_ge(s.l1_T_ps, j * 4 + (n + 1))
                    copy((QT, KT)[w][:, :, t * P:(t + 1) * P],
                         bank[4 + n][:].bitcast(BF16).rearrange("p (c q) -> p c q", q=P)).then_inc(s.l1_T, 1)

            def l1_prob(j):
                act.wait_ge(s.l1_nmT_ps, j + 1)
                copy(nmT[:], bank[7][:].bitcast(BF16)[:, 0:TB * P]).then_inc(s.l1_nmT, 1)
                for h in range(NH):
                    act.wait_ge(s.l1_p_ps, j * NH + (h + 1))
                    if h >= RING:
                        act.wait_ge(s.l1_pv, j * NH + (h - RING + 1))
                    act.activation(pT[:, h % RING, :], bank[4 + h % RING][:, 0:384], ACT.Exp).then_inc(s.l1_p, 1)

            def l1_out(j):
                act.wait_ge(s.l1_oT_ps, j + 1)
                copy(oT[:], bank[7][:, 0:TB * P]).then_inc(s.l1_oT, 1)

            def body(i, j):
                if i is not None:
                    l0_front(i)
                if j is not None:
                    l1_split(j)
                if i is not None:
                    l0_exp(i)
                if j is not None:
                    l1_turn(j)
                if i is not None:
                    l0_attention(i)
                    l0_down(i)
                if j is not None:
                    l1_prob(j)
                    l1_out(j)
                if i is not None:
                    l0_end(i)

            body(0, None)
            with act.Fori(1, B) as i:
                body(i, i - 1)
            body(None, B - 1)

            act.wait_ge(s.r_te, 1)

            def sorted_tiles(r):
                for k in range(RING):
                    n = r * RING + k
                    e = act.value_load(tile_ei[0:1, bass.ds(n, 1)], min_val=0, max_val=NE - 1)
                    act.wait_ge(s.f_h_ps, n + 1)
                    since(act, s.f_y_ps, r, RING, k + 1)
                    for c in range(FC):
                        act.activation(hT[:, k, c, :], bank[3 + k][:, c * P:(c + 1) * P], ACT.Gelu,
                                       bias=b1_sb[:, bass.ds(e * FC + c, 1)]).then_inc(s.f_h, 1)

            sorted_tiles(0)
            with act.Fori(1, ST // RING) as r:
                sorted_tiles(r)
            for q in range(NT // 4):
                act.wait_ge(s.final, q * 4 + 4)
                for k in range(4):
                    n = q * 4 + k
                    act.dma_start(out.rearrange("b (t p) d -> (b t) p d", p=P)[n], fin[:, k, :]).then_inc(out_stored[k], 16)
            for k in range(4):
                act.wait_ge(out_stored[k], 16 * (NT // 4))

        @block.vector
        def _(v):
            tt, ts, stt, cp = v.tensor_tensor, v.tensor_scalar, v.scalar_tensor_tensor, v.tensor_copy
            v.memset(ones[:], 1.0)
            v.memset(vaug[:], 1.0)
            v.memset(split[:], 0.0)
            v.memset(nmp[:], 0.0).then_inc(s.l1_x2, 1)
            v.wait_ge(s.loaded_consts, 32)
            for a in range(2):
                cp(mask_q[:, a, :], cst[:, C_MASKQ:C_MASKQ + P])
                cp(mask_k[:, a, :], cst[:, C_MASKK:C_MASKK + P])
            cp(sel_b[:], sel_rows)
            cp(ident_b[:], ident)
            v.memset(zero[:], 0.0).then_inc(s.dve_setup, 1)
            v.wait_ge(s.dve_setup, 1)
            v.wait_ge(s.loaded_x, 64)
            v.wait_ge(s.loaded_setup, 16 * 11)

            def carry_wait():
                v.memset(tick[:], 0.0)

            def norm_stats(c, i, kinds):
                for t in range(TB):
                    a = c.did(v.bn_stats(st[:, t, :], xall[:, bass.ds(i * (TB * D) + t * D, D)]))
                c.need(a)
                carry_wait()
                for t in range(TB):
                    a = c.did(v.bn_aggr(mv[:, t, :], st[:, t, :]))
                c.need(a)
                a = c.did(ts(sv[:, 0, :], mv[:, :, 1], 1.0, 1e-5, ALU.mult, ALU.add))
                if kinds == 2:
                    a = c.did(ts(sv[:, 1, :], mv[:, :, 1], 1.0 + 1e-6, 1e-11, ALU.mult, ALU.add))
                c.need(a)
                y, w = sc[:, 0:kinds, :], sv[:, 0:kinds, :]
                q = sq[:, 0:kinds, :]
                c.need(c.did(v.tensor_single_scalar(y.bitcast(I32), w.bitcast(I32), 1, ALU.arith_shift_right)))
                c.need(c.did(ts(y.bitcast(I32), y.bitcast(I32), -1.0, float(0x5F3759DF), ALU.mult, ALU.add)))
                for _ in range(4):
                    c.need(c.did(tt(q, y, y, ALU.mult)))
                    c.need(c.did(stt(q, q, -0.5, w, ALU.mult, ALU.mult)))
                    c.need(c.did(stt(y, q, 1.5, y, ALU.add, ALU.mult)))

            def l0_front(i, c):
                norm_stats(c, i, 2)
                for w in range(2):
                    for t in range(TB):
                        ins = ts(xr[:, w, t, :], xall[:, bass.ds(i * (TB * D) + t * D, D)], mv[:, t, 0:1],
                                 sc[:, w, t:t + 1], ALU.subtract, ALU.mult)
                ins.then_inc(s.l0_norm, 1)

            def l0_softmax(i, c):
                for t in range(TB):
                    v.wait_ge(s.l0_qkv_ps, i * TB + (t + 1))
                    a = c.did(tt(z[:, t].rearrange("p w d -> p (w d)"), bank[1 + t][:, 0:3 * D], bqkv0[:], ALU.add))
                c.need(a)
                for t in range(TB):
                    a = c.did(v.reduce_max(zmax[:, t, :], z[:, t, 0:2, :], axis=AX_X))
                c.need(a)
                ts(zmax[:], zmax[:], -1.0, None, ALU.mult).then_inc(s.l0_zmax, 1)
                v.wait_ge(s.l0_exp, i * 4 + 4)
                c.need(c.did(v.reciprocal(zrec[:], zsum[:])))
                for t in range(TB):
                    a = c.did(ts(kk_sb[:, t, :], ez[:, t, 1, :], zrec[:, t, 1:2], None, ALU.mult))
                c.need(a)
                tt(kv_sb[:], kk_sb[:], z[:, :, 2, :], ALU.mult).then_inc(s.l0_kv, 1)

            def l0_topk(i, c):
                for t in range(TB):
                    apart(v)
                    v.wait_ge(s.l0_sims, i * TB + (t + 1))
                    for q in range(2 * PH):
                        ins = v.max(top[:, t, q, :], sims[:, t, q, :])
                    a = c.did(ins)
                c.need(a)
                for t in range(TB):
                    tp = top[:, t].rearrange("p (h s) k -> p h s k", s=2)
                    a = c.did(tt(pair[:, t].rearrange("p h (a b) -> p h a b", a=TOPK), bc(tp[:, :, 0, :], 3, TOPK),
                                 bc(tp[:, :, 1, :], 2, TOPK), ALU.add))
                c.need(a)
                carry_wait()
                for t in range(TB):
                    for h in range(PH):
                        ins = v.max(best[:, t, h, :], pair[:, t, h, :])
                    a = c.did(ins)
                c.need(a)
                c.need(c.did(ts(tau[:], best[:, :, :, TOPK - 1].rearrange("p t h -> p (t h)"), 0.0, None, ALU.max)))

            def l0_attention(i, c):
                v.wait_ge(s.l0_att_ps, i + 1)
                for t in range(TB):
                    xt = xall[:, bass.ds(i * (TB * D) + t * D, D)]
                    a = c.did(stt(xt, bank[2][:, t * P:(t + 1) * P], zrec[:, t, 0:1], xt, ALU.mult, ALU.add))
                return a

            def l0_unit(i, c, u):
                t, h = u // PH, u % PH
                sm = sims[:, t].rearrange("p (h s) k -> p h s k", s=2)
                gu = g[:, u % 2, :]
                c.need(c.did(tt(gu.rearrange("p (a b) -> p a b", a=NKEYS), bc(sm[:, h, 0, :], 2, NKEYS),
                                bc(sm[:, h, 1, :], 1, NKEYS), ALU.add)))
                if h == 0:
                    dst = coef[:, t, :]
                    since(v, s.l0_cT_ps, i, 4, 4)
                else:
                    dst = m[:, u % RING, :]
                    last = [w for w in range(u) if w % PH and w % RING == u % RING]
                    if last:
                        w = last[-1]
                        v.wait_ge(s.l0_coef, i * (UNITS - TB) + ((w // PH) * (PH - 1) + w % PH))
                    else:
                        since(v, s.l0_coef, i, UNITS - TB, UNITS - TB)
                stt(dst, gu, tau[:, u:u + 1], gu, ALU.is_ge, ALU.mult).then_inc(s.l0_mask, 1)

            def l0_up(i, c):
                for k in range(EC // 2):
                    v.wait_ge(s.l0_cT_ps, i * 4 + (k + 1))
                    if k >= 2:
                        v.wait_ge(s.l0_up_ps, i * 4 + (k - 1))
                    tt(hc[:, k % 2, :], bank[1 + k % 2][:], hid[:, k, :], ALU.mult).then_inc(s.l0_hc, 1)
                v.wait_ge(s.l0_up_ps, i * 4 + 4)
                xt = xall[:, bass.ds(i * (TB * D), TB * D)]
                tt(xt, xt, bank[3][:, 0:TB * P], ALU.add).then_inc(s.l0_x1, 1)
                apart(v)
                v.wait_ge(s.l0_x1, i + 1)
                norm_stats(c, i, 1)
                since(v, s.l0_kept, i, 1, 1)
                for t in range(TB):
                    ins = ts(xn1[:, t, :], xall[:, bass.ds(i * (TB * D) + t * D, D)], mv[:, t, 0:1],
                             sc[:, 0, t:t + 1], ALU.subtract, ALU.mult)
                ins.then_inc(s.l0_xn1, 1)

            def l1_front(j, c):
                cosv = cst[:, C_COS:C_COS + S].rearrange("p (t c) -> p t c", t=TB)
                sinv = cst[:, C_SIN:C_SIN + S].rearrange("p (t c) -> p t c", t=TB)
                for t in range(TB):
                    v.wait_ge(s.l1_qkv_ps, j * TB + (t + 1))
                    src = bank[7 - t][:, 0:256].rearrange("p (c e) -> p c e", e=2)
                    c.did(tt(ra[:].rearrange("p (c e) -> p c e", e=2), src, bc(cosv[:, t], 2, 2), ALU.mult))
                    a = c.did(tt(rb[:].rearrange("p (c e) -> p c e", e=2), src, bc(sinv[:, t], 2, 2), ALU.mult))
                    c.did(cp(vaug[:, t, :, 0:HD], bank[7 - t][:, 256:384].rearrange("p (h d) -> p h d", d=HD)))
                    b_ = c.did(cp(lg[:, t, :], bank[7 - t][:, 384:384 + NE]))
                    c.need(b_)
                    r2 = rot[:, t].rearrange("p w (c e) -> p (w c) e", e=2)
                    ea, eb = (y[:].rearrange("p (c e) -> p c e", e=2) for y in (ra, rb))
                    c.did(tt(r2[:, :, 0], ea[:, :, 0], eb[:, :, 1], ALU.subtract))
                    ins = tt(r2[:, :, 1], ea[:, :, 1], eb[:, :, 0], ALU.add)
                    ins.then_inc(s.l1_qkv, 1)
                    apart(v)
                    v.wait_ge(s.l1_qkv, j * 2 + (t + 1))
                for t in range(TB):
                    a = c.did(v.max(lg8[:, t, :], lg[:, t, :]))
                c.need(a)
                carry_wait()
                for t in range(TB):
                    c.did(v.max_index(lgi[:, t, :], lg8[:, t, :], lg[:, t, :]))
                ts(lgneg[:], lg8[:, :, 0], -1.0, None, ALU.mult).then_inc(s.l1_lgneg, 1)
                v.wait_ge(s.l1_lgneg, j + 1)
                c.need(c.did(cp(lgf[:], lgi[:, :, 0])))
                for t in range(TB):
                    a = c.did(ts(onehot[:, bass.ds(j * (TB * NE) + t * NE, NE)], cst[:, C_IOTA8:C_IOTA8 + NE],
                             lgf[:, t:t + 1], None, ALU.is_equal))
                v.wait_ge(s.l1_part, j * 2 + 1)
                sp_all = split[:].rearrange("p t w h c -> p (t w h) c")
                r_all = rot[:].rearrange("p t w (h d) -> p (t w h) d", d=HD)
                tt(rest[:], r_all, sp_all[:, :, 0:HD], ALU.subtract).then_inc(s.l1_rest, 1)
                v.wait_ge(s.l1_part, j * 2 + 2)
                rs = rest[:].rearrange("p (t w h) d -> p t w h d", t=TB, w=2)
                for w, n in ((0, 2), (1, 3)):
                    for t in range(TB):
                        ins = tt(split[:, t, w, :, n * HD:(n + 1) * HD], rs[:, t, w],
                                 split[:, t, w, :, HD:2 * HD], ALU.subtract)
                    ins.then_inc(s.l1_split, 1)
                v.wait_ge(s.l1_lgsum, j * 2 + 2)
                c.did(cp(esum[:, bass.ds(j * TB, TB)], lgs[:]))

            def l1_max(j, h):
                v.wait_ge(s.l1_s_ps, j * NH + (h + 1))
                b = bank[4 + h % RING]
                v.reduce_max(smax[:, 1, h:h + 1], b[:, 0:256], axis=AX_X)
                v.reduce_max(smax[:, 0, h:h + 1], b[:, 256:384], axis=AX_X).then_inc(s.l1_max, 1)

            def l1_nm(j, c):
                v.wait_ge(s.l1_max, j * NH + NH)
                c.need(c.did(ts(nm[:, :, :, 0], smax[:], -1.0, None, ALU.mult)))
                c.need(c.did(stt(srest[:], smax[:], -1.0, nm[:, :, :, 0], ALU.mult, ALU.subtract)))
                c.need(c.did(cp(nm[:, :, :, 1], srest[:])))
                c.need(c.did(tt(nm[:, :, :, 2], srest[:], nm[:, :, :, 1], ALU.subtract)))
                cp(nmp[:, :, 1, :], nmp[:, :, 0, :]).then_inc(s.l1_nm, 1)

            def l1_norm(j, c):
                v.wait_ge(s.l1_pv, j * NH + NH)
                o = bank[7][:, 0:TB * NH * (HD + 1)].rearrange("p (t h d) -> p t h d", t=TB, h=NH)
                c.need(c.did(v.reciprocal(orec[:], o[:, :, :, HD])))
                for t in range(TB):
                    ins = tt(o_sb[:, t].rearrange("p (h d) -> p h d", d=HD), o[:, t, :, 0:HD],
                             bc(orec[:, t], 2, HD), ALU.mult)
                ins.then_inc(s.l1_o, 1)

            def l1_out(j, c):
                v.wait_ge(s.l1_wo_ps, j + 1)
                xt = xall[:, bass.ds(j * (TB * D), TB * D)]
                tt(xt, xt, bank[6][:, 0:TB * P], ALU.add).then_inc(s.l1_x2, 1)

            def body(i, j):
                c0 = Marks(v, s.l0_v, i * N_L0V) if i is not None else None
                c1 = Marks(v, s.l1_v, j * N_L1V) if j is not None else None
                if i is not None:
                    l0_front(i, c0)
                if j is not None:
                    l1_front(j, c1)
                if i is not None:
                    l0_softmax(i, c0)
                    l0_topk(i, c0)
                for u in range(UNITS):
                    if i is not None:
                        l0_unit(i, c0, u)
                        if u == 2:
                            done = l0_attention(i, c0)
                    if j is not None:
                        if u < 8:
                            l1_max(j, 2 * u)
                            l1_max(j, 2 * u + 1)
                        if u == 7:
                            l1_nm(j, c1)
                if j is not None:
                    l1_norm(j, c1)
                    l1_out(j, c1)
                if i is not None:
                    c0.need(done)
                    l0_up(i, c0)
                assert i is None or c0.n == N_L0V
                assert j is None or c1.n == N_L1V

            body(0, None)
            with v.Fori(1, B) as i:
                body(i, i - 1)
            body(None, B - 1)

            c = Marks(v, s.r_v, 0)
            v.wait_ge(s.r_rank_ps, 1)
            cp(rank[:], bank[0][:, 0:NT * NE])
            c.need(c.did(cp(tot[:], bank[1][:, 0:NT * NE])))
            tv = tot[:].rearrange("p (n e) -> p e n", e=NE)
            for e in range(NE):
                a = c.did(v.tensor_tensor_scan(incl[:, e, :], ones[:, 0:NT], tv[:, e, :], 0.0, ALU.mult, ALU.add))
            c.need(a)
            c.need(c.did(ts(ntile_i[:], incl[:, :, NT - 1], float(P - 1), None, ALU.add)))
            c.need(c.did(v.tensor_single_scalar(ntile_i[:], ntile_i[:], 7, ALU.arith_shift_right)))
            c.need(c.did(cp(ntile[:], ntile_i[:])))
            c.need(c.did(v.tensor_tensor_scan(nincl[:], ones[:, 0:NE], ntile[:], 0.0, ALU.mult, ALU.add)))
            a = c.did(tt(ntile[:], nincl[:], ntile[:], ALU.subtract))
            c.need(c.did(tt(tot[:], rank[:], tot[:], ALU.subtract)))
            rv = rank[:].rearrange("p (n e) -> p n e", e=NE)
            c.need(c.did(tt(tv, tv, incl[:], ALU.add)))
            c.need(c.did(stt(rv, bc(ntile[:], 1, NT), float(P), tot[:].rearrange("p (n e) -> p n e", e=NE),
                             ALU.mult, ALU.add)))
            c.need(c.did(tt(rank[:], rank[:], onehot[:], ALU.mult)))
            c.need(c.did(v.reduce_sum(dest[:], rv, axis=AX_X)))
            cp(dest_u[:], dest[:]).then_inc(s.r_dest, 1)
            c.need(c.did(tt(tcmp[:], bc(cst[:, C_IOTAST:C_IOTAST + ST], 2, NE), bc(nincl[:], 1, ST), ALU.is_ge)))
            c.need(c.did(v.reduce_sum(tile_e[:], tcmp[:], axis=AX_X)))
            ts(tile_ei[:], tile_e[:], float(NE - 1), None, ALU.min).then_inc(s.r_te, 1)
            v.wait_ge(s.r_te, 1)
            c.need(c.did(v.reciprocal(esum[:], esum[:])))

            def ready(r, k):
                n = r * RING + k
                e = v.value_load(tile_ei[0:1, bass.ds(n, 1)], min_val=0, max_val=NE - 1)
                since(v, s.f_h_ps, r, RING, k + 1)
                cp(w1e[:, k, :], w1_sb[:, bass.ds(e * FF, FF)]).then_inc(s.f_w1, 1)
                v.wait_ge(s.f_xT_ps, n + 1)
                cp(xsT[:, k, :], bank[2][:, 0:P]).then_inc(s.f_xT, 1)

            def result(r, k):
                n = r * RING + k
                e = v.value_load(tile_ei[0:1, bass.ds(n, 1)], min_val=0, max_val=NE - 1)
                v.wait_ge(s.f_y_ps, n + 1)
                since(v, tile_stored[k], r, 16, 16)
                tt(ys[:, k, :], bank[y_bank[k]][:, 0:D], b2_sb[:, bass.ds(e * D, D)], ALU.add).then_inc(s.f_y, 1)

            def sorted_tiles(r, last=False):
                for k in range(RING):
                    if not (last and k + 2 >= RING):
                        ready(r + (k + 2) // RING, (k + 2) % RING)
                    result(r, k)

            ready(0, 0)
            ready(0, 1)
            sorted_tiles(0)
            with v.Fori(1, ST // RING - 1) as r:
                sorted_tiles(r)
            sorted_tiles(ST // RING - 1, last=True)
            for n in range(NT):
                v.wait_ge(gathered[n % 4], 16 * (n // 4 + 1))
                if n >= 4:
                    v.wait_ge(out_stored[n % 4], 16 * (n // 4))
                stt(fin[:, n % 4, :], yg[:, n % 4, :], esum[:, n:n + 1], xall[:, n * D:(n + 1) * D],
                    ALU.mult, ALU.add).then_inc(s.final, 1)


_INS = ["L0_attn_hidden_states", "L0_attn_Wq", "L0_attn_bq", "L0_attn_Wk", "L0_attn_bk", "L0_attn_Wv", "L0_attn_bv",
        "L0_ffn_w_q", "L0_ffn_keys", "L0_ffn_expert_down", "L0_ffn_expert_up", "L0_ffn_norm_w",
        "L1_attn_wq", "L1_attn_wk", "L1_attn_wv", "L1_attn_wo", "L1_ffn_gate_w", "L1_ffn_w1", "L1_ffn_b1",
        "L1_ffn_w2", "L1_ffn_b2"]


def kernel(**inputs):
    import numpy as np
    import concourse.bacc as bacc
    from concourse.bass_utils import run_bass_kernel_spmd

    nc = bacc.Bacc("TRN2", target_bir_lowering=False, num_devices=1)
    arrays = {f"in_{name}": np.ascontiguousarray(inputs[name]) for name in _INS}
    arrays["in_shape_constants"] = shape_constants(np)
    args = [nc.dram_tensor(n, a.shape, mybir.dt.from_np(a.dtype), kind="ExternalInput").ap() for n, a in arrays.items()]
    out = nc.dram_tensor("out_dram", (B, S, D), F32, kind="ExternalOutput").ap()
    build(nc, *args, out)
    r = run_bass_kernel_spmd(nc, [arrays], core_ids=[0])
    return r.results[0]["out_dram"]
```

```python
from contextlib import ExitStack

import concourse.bass as bass
from concourse import mybir

F32 = mybir.dt.float32
BF16 = mybir.dt.bfloat16
I32 = mybir.dt.int32
U32 = mybir.dt.uint32
ALU = mybir.AluOpType
ACT = mybir.ActivationFunctionType
AX_X = mybir.AxisListType.X

P = 128
D = 128
B, S = 16, 256
TB = S // P
NT = B * TB
LAND = 64
PH, NKEYS, TOPK = 8, 32, 8
NEXP = NKEYS * NKEYS
EC = NEXP // P
NH, HD = 16, 8
NE, FF = 8, 512
FC = FF // P
ST = NT + NE - 1
SLOTS = 6
HB = 64
QPART = (0, 1, 2, 0, 0, 1)
KPART = (0, 1, 0, 2, 1, 0)
UNITS = TB * PH
RING = 3
POOL_SUMS = tuple(u for u in range(UNITS) if u % 4)
ZC = 256

C_IDENT, C_POOL, C_MASKQ, C_MASKK, C_TRI = 0, 128, 256, 384, 512
C_COS, C_SIN = 640, 896
C_IOTA8, C_IOTAST = 1152, 1160
C_SEL = C_IOTAST + ST
C_ALL = C_SEL + NH * P
C_STAY = C_SEL


def shape_constants(np):
    c = np.zeros((P, C_ALL), np.float32)
    r = np.arange(P)
    c[:, C_IDENT:C_IDENT + P] = np.eye(P)
    for t in range(TB):
        c[r, C_POOL + LAND * t + 32 * t + r // 4] = 0.25
    c[:, C_MASKQ:C_MASKQ + P] = np.where(r[None, :] > r[:, None], -1e30, 0.0)
    c[:, C_MASKK:C_MASKK + P] = np.where(r[:, None] > r[None, :], -1e30, 0.0)
    c[:, C_TRI:C_TRI + P] = r[:, None] < r[None, :]
    freq = (1.0 / 10000.0 ** (np.arange(0, HD, 2, dtype=np.float32) / HD)).astype(np.float32)
    ang = (np.arange(S, dtype=np.float32)[:, None] * freq[None, :]).astype(np.float32)
    for t in range(TB):
        for base, tab in ((C_COS, np.cos(ang)), (C_SIN, np.sin(ang))):
            rows = np.tile(tab[t * P:(t + 1) * P], (1, 2 * NH)).astype(np.float32)
            rows[:, :NH * HD // 2] *= np.float32(1.0 / np.sqrt(np.float32(HD)))
            c[:, base + P * t:base + P * (t + 1)] = rows
    c[:, C_IOTA8:C_IOTA8 + NE] = np.arange(NE)
    c[:, C_IOTAST:C_IOTAST + ST] = np.arange(ST)
    for h in range(NH):
        for half in (0, HB):
            c[half + 3 * h:half + 3 * h + 3, C_SEL + P * h:C_SEL + P * (h + 1)] = 1.0
    return c


class Marks:

    def __init__(self, eng, sem, base):
        self.eng, self.sem, self.base, self.n = eng, sem, base, 0

    def did(self, ins):
        ins.then_inc(self.sem, 1)
        self.n += 1
        return self.n

    def need(self, n):
        self.eng.wait_ge(self.sem, self.base + n)


def bc(ap, axis, n):
    ap = ap.unsqueeze(axis)
    return ap.broadcast_to([n if k == axis else s for k, s in enumerate(ap.shape)])


def build(nc, x, Wq, bq, Wk, bk, Wv, bv, w_q, keys, e_down, e_up, norm_w, wq1, wk1, wv1, wo1,
          gate_w, w1, b1, w2, b2, consts, out):
    with ExitStack() as ctx:
        def sb(name, shape, dt=F32):
            return ctx.enter_context(nc.sbuf_tensor(name, shape, dt))

        def sem(name):
            return ctx.enter_context(nc.semaphore(name))

        bank = [ctx.enter_context(nc.psum_tensor(f"bank{k}", [P, 512], F32)) for k in range(8)]

        cst = sb("cst", [P, C_STAY])
        ident = cst[:, C_IDENT:C_IDENT + P]
        pool_mat = cst[:, C_POOL:C_POOL + TB * LAND].rearrange("p (t l) -> p t l", t=TB)
        ones = sb("ones", [P, P])
        ident_b = sb("ident_b", [P, P], BF16)
        mask_q = sb("mask_q", [P, 2, P], BF16)
        mask_k = sb("mask_k", [P, 2, P], BF16)
        sel_b = sb("sel_b", [P, NH * P], BF16)
        wqkv0 = sb("wqkv0", [P, 3 * D])
        bqkv0 = sb("bqkv0", [P, 3 * D])
        keysT = sb("keysT", [P, 512])
        fold = sb("fold", [P, 512])
        downT = sb("downT", [P, NEXP])
        up = sb("up", [P, EC, D])
        nw = sb("nw", [P, 1])
        wqkvg1 = sb("wqkvg1", [P, 3 * D + NE])
        wo_sb = sb("wo_sb", [P, D])
        w1_sb = sb("w1_sb", [P, NE * FF])
        w2_sb = sb("w2_sb", [P, NE * FC * D])
        b1_rows = sb("b1_rows", [NE * FC, P])
        b1_sb = sb("b1_sb", [P, NE * FC])
        b2_sb = sb("b2_sb", [P, NE * D])
        xall = sb("xall", [P, NT * D])
        onehot = sb("onehot", [P, NT * NE])
        esum = sb("esum", [P, NT])
        st = sb("st", [P, TB, 6])
        mv = sb("mv", [P, TB, 2])
        sc = sb("sc", [P, 2, TB])
        sv = sb("sv", [P, 2, TB])
        sq = sb("sq", [P, 2, TB])
        xr = sb("xr", [P, 2, TB, D])
        xrT = sb("xrT", [P, 512])
        z = sb("z", [P, TB, 3, D])
        zmax = sb("zmax", [P, TB, 2])
        ez = sb("ez", [P, TB, 2, D])
        zsum = sb("zsum", [P, TB, 2])
        zrec = sb("zrec", [P, TB, 2])
        kk_sb = sb("kk_sb", [P, TB, D])
        kv_sb = sb("kv_sb", [P, TB, D])
        klS = sb("klS", [LAND, D])
        hS = sb("hS", [P, D])
        eqT = sb("eqT", [P, TB * P])
        gS = sb("gS", [P, D])
        mS = sb("mS", [P, D])
        sims = sb("sims", [P, TB, 2 * PH, NKEYS])
        sims_next = sb("sims_next", [P, TB, 2 * PH, NKEYS])
        top = sb("top", [P, TB, 2 * PH, TOPK])
        pair = sb("pair", [P, TB, PH, TOPK * TOPK])
        best = sb("best", [P, TB, PH, TOPK])
        tau = sb("tau", [P, UNITS])
        g = sb("g", [P, RING, NEXP])
        m = sb("m", [P, RING, NEXP])
        coef = sb("coef", [P, TB, NEXP])
        wqp = g[:, 0:2].rearrange("p a (b d) -> p (a b) d", d=D)
        down_rows = m[:, 0, :].rearrange("p (c d) -> p c d", d=D)
        key_rows = m[:, 1, 0:512].rearrange("p (c d) -> p c d", d=D)
        sel_rows = coef[:].rearrange("p t e -> p (t e)")
        hid = sb("hid", [P, 4, 512])
        hc = sb("hc", [P, 2, 512])
        xn1 = sb("xn1", [P, TB, D])
        xn1T = sb("xn1T", [P, TB * P])
        ra = sb("ra", [P, 2 * NH * HD])
        rb = sb("rb", [P, 2 * NH * HD])
        rot = sb("rot", [P, TB, 2, NH * HD])
        vaug = sb("vaug", [P, TB, NH, HD + 1])
        vnext = sb("vnext", [P, TB, D])
        lg = sb("lg", [P, TB, NE])
        lg8 = sb("lg8", [P, TB, 8])
        lgi = sb("lgi", [P, TB, 8], U32)
        lgf = sb("lgf", [P, TB])
        lgneg = sb("lgneg", [P, TB])
        lge = sb("lge", [P, TB, NE])
        lgs = sb("lgs", [P, TB])
        split = sb("split", [P, TB, 2, NH, HB], BF16)
        rest = sb("rest", [P, TB * 2 * NH, HD])
        QT = sb("QT", [P, NH // 2, TB * P], BF16)
        KT = sb("KT", [P, NH // 2, TB * P], BF16)
        smax = sb("smax", [P, TB, NH])
        srest = sb("srest", [P, TB, NH])
        nmp = sb("nmp", [P, TB, 2, HB], BF16)
        nm = nmp[:, :, 0, 0:3 * NH].rearrange("p t (h r) -> p t h r", r=3)
        nmT = sb("nmT", [P, TB * P], BF16)
        pT = sb("pT", [P, 3, 384])
        orec = sb("orec", [P, TB, NH])
        o_sb = sb("o_sb", [P, TB, D])
        oT = sb("oT", [P, TB * P])
        rank = sb("rank", [P, NT * NE])
        tot = sb("tot", [P, NT * NE])
        incl = sb("incl", [P, NE, NT])
        ntile_i = sb("ntile_i", [P, NE], I32)
        ntile = sb("ntile", [P, NE])
        nincl = sb("nincl", [P, NE])
        dest = sb("dest", [P, NT])
        dest_u = sb("dest_u", [P, NT], U32)
        tcmp = sb("tcmp", [P, ST, NE])
        tile_e = sb("tile_e", [P, ST])
        tile_ei = sb("tile_ei", [P, ST], I32)
        xs = sb("xs", [P, RING, D])
        xsT = sb("xsT", [P, RING, P])
        back = [coef[:].rearrange("p t (n d) -> p (t n) d", d=D)[:, n, :] for n in range(NT // 2)] + \
               [g[:, 0:2].rearrange("p t (n d) -> p (t n) d", d=D)[:, n, :] for n in range(NT // 2)]
        hT = hid[:, 0:RING, :].rearrange("p k (c q) -> p k c q", q=P)
        w1e = m[:, :, 0:FF]
        ys = hc[:, 0, 0:RING * D].rearrange("p (k d) -> p k d", d=D)
        yg = sb("yg", [P, 4, D])
        fin = pair[:, 0].rearrange("p (a b) c -> p a (b c)", a=4)
        zero = sb("zero", [P, ZC])

        tick = sb("tick", [P, 1])

        y_bank = (6, 7, 1)

        xn1rows = nc.dram_tensor("xn1rows", [B, TB, P, D], F32, kind="Internal").ap()
        xsorted = nc.dram_tensor("xsorted", [ST * P, D], F32, kind="Internal").ap()
        ysorted = nc.dram_tensor("ysorted", [ST * P, D], F32, kind="Internal").ap()

        S_ = {n: sem(n) for n in (
            "loaded_consts", "loaded_x", "loaded_setup", "loaded_w", "pe_setup", "act_setup", "dve_setup",
            "v_setup", "l0_tau", "l0_simcopy", "l0_sum", "l0_own", "u_v", "q_v", "rows_back",
            "l0_v", "l0_norm", "l0_xrT_ps", "l0_xrT", "l0_qkv_ps", "l0_sim_ps", "l0_z", "l0_zmax",
            "l0_exp", "l0_sims", "l0_kv", "l0_kl_ps", "l0_kl", "l0_g_ps", "l0_g", "l0_m_ps", "l0_m",
            "l0_att_ps", "l0_att", "l0_mask", "l0_coef", "l0_down_ps", "l0_hid", "l0_cT_ps", "l0_hc",
            "l0_up_ps", "l0_x1", "l0_xn1", "l0_xn1T_ps", "l0_xn1T", "l0_kept",
            "l1_v", "l1_vals", "l1_qkv_ps", "l1_qkv", "l1_lgneg", "l1_lgsum", "l1_part", "l1_rest", "l1_low",
            "l1_split", "l1_T_ps", "l1_T", "l1_s_ps", "l1_max", "l1_nm", "l1_nmT_ps", "l1_nmT", "l1_p_ps", "l1_p",
            "l1_pv", "l1_o", "l1_oT_ps", "l1_oT", "l1_wo_ps", "l1_x2",
            "r_v", "zeroed", "r_rank_ps", "r_dest", "r_te", "scattered", "f_xT_ps", "f_w1", "f_xT", "f_h_ps",
            "f_h", "f_y_ps", "f_y", "final")}
        s = type("Semaphores", (), S_)
        tile_loaded = [sem(f"tile_loaded{k}") for k in range(RING)]
        tile_stored = [sem(f"tile_stored{k}") for k in range(RING)]
        gathered = [sem(f"gathered{k}") for k in range(4)]
        out_stored = [sem(f"out_stored{k}") for k in range(4)]

        def since(e, which, i, per, n):
            if isinstance(i, int) and i * per + n - per <= 0:
                return
            e.wait_ge(which, i * per + (n - per))

        def apart(e):
            e.wait_ge(s.dve_setup, 1)

        def rounds(e, body):
            def at(i):
                body(*(b if 0 <= b < B else None for b in (i + 1, i, i - 1, i - 2)))

            for i in range(-1, 3):
                at(i)
            with e.Fori(3, B - 1) as i:
                body(i + 1, i, i - 1, i - 2)
            for i in range(B - 1, B + 2):
                at(i)

        N_L0V, N_UV, N_L1V, N_QV = 31, 19, 22, 1

        block = ctx.enter_context(nc.Block())

        @block.sync
        def _(sp):
            sp.dma_start(cst[:], consts[:, 0:C_STAY]).then_inc(s.loaded_consts, 16)
            sp.dma_start(sel_rows, consts[:, C_SEL:C_ALL]).then_inc(s.loaded_consts, 16)
            xv = x.rearrange("b (t p) d -> p (b t) d", p=P)
            xs_ = xall[:].rearrange("p (n d) -> p n d", d=D)
            for q in range(4):
                sp.dma_start(xs_[:, q * 8:(q + 1) * 8, :], xv[:, q * 8:(q + 1) * 8, :]).then_inc(s.loaded_x, 16)
            for k, (w, b) in enumerate(((Wq, bq), (Wk, bk), (Wv, bv))):
                sp.dma_start(wqkv0[:, k * D:(k + 1) * D], w).then_inc(s.loaded_setup, 16)
                sp.dma_start(bqkv0[:, k * D:(k + 1) * D], b.rearrange("(o d) -> o d", o=1).broadcast_to([P, D])).then_inc(s.loaded_setup, 16)
            for k, w in enumerate((wq1, wk1, wv1)):
                sp.dma_start(wqkvg1[:, k * D:(k + 1) * D], w).then_inc(s.loaded_setup, 16)
            sp.dma_start(wqkvg1[:, 3 * D:], gate_w).then_inc(s.loaded_setup, 16)
            sp.dma_start(wo_sb[:], wo1).then_inc(s.loaded_setup, 16)
            def keep_rows(a):
                sp.wait_ge(s.l0_xn1, a + 1)
                sp.dma_start(xn1rows[bass.ds(a, 1)].rearrange("b t p d -> p (b t) d") if not isinstance(a, int) else
                             xn1rows[a:a + 1].rearrange("b t p d -> p (b t) d"), xn1[:]).then_inc(s.l0_kept, 16)

            keep_rows(0)
            with sp.Fori(1, B) as a:
                keep_rows(a)
            sp.wait_ge(s.l0_kept, 16 * B)
            sp.wait_ge(s.l1_x2, B + 1)
            for h in range(2):
                dst = (coef[:] if h == 0 else g[:, 0:2]).rearrange("p t (n d) -> p (t n) d", d=D)
                src = xn1rows[h * (B // 2):(h + 1) * (B // 2)].rearrange("b t p d -> p (b t) d")
                sp.dma_start(dst, src).then_inc(s.rows_back, 16)
            sp.wait_ge(s.scattered, 16 * NT)
            for k in range(RING):
                sp.dma_start(xs[:, k, :], xsorted[k * P:(k + 1) * P, :]).then_inc(tile_loaded[k], 16)

            def store(r, k):
                sp.wait_ge(s.f_y, r * RING + (k + 1))
                sp.dma_start(ysorted[bass.ds(r * (RING * P) + k * P, P), :], ys[:, k, :]).then_inc(tile_stored[k], 16)

            with sp.Fori(1, ST // RING) as r:
                for k in range(RING):
                    since(sp, s.f_xT_ps, r, RING, k + 1)
                    sp.dma_start(xs[:, k, :], xsorted[bass.ds(r * (RING * P) + k * P, P), :]).then_inc(tile_loaded[k], 16)
                    store(r - 1, k)
            for k in range(RING):
                store(ST // RING - 1, k)

        @block.gpsimd
        def _(pool):
            pool.dma_start(key_rows, keys.rearrange("h k s d -> (h k s) d").rearrange("(c p) d -> p c d", p=P)).then_inc(s.loaded_w, 16)
            pool.dma_start(wqp, w_q.rearrange("(c p) d -> p c d", p=P)).then_inc(s.loaded_w, 16)
            pool.dma_start(down_rows, e_down.rearrange("(c p) d -> p c d", p=P)).then_inc(s.loaded_w, 16)
            pool.dma_start(up[:], e_up.rearrange("(c p) d -> p c d", p=P)).then_inc(s.loaded_w, 16)
            pool.dma_start(nw[:], norm_w.rearrange("(d o) -> d o", o=1)).then_inc(s.loaded_w, 16)
            pool.dma_start(b1_rows[:], b1.rearrange("e (c p) -> (e c) p", p=P)).then_inc(s.loaded_w, 16)
            pool.dma_start(w1_sb[:].rearrange("p (e f) -> p e f", e=NE), w1.rearrange("e d f -> d e f")).then_inc(s.loaded_w, 16)
            pool.dma_start(w2_sb[:].rearrange("p (e d) -> p e d", d=D), w2.rearrange("e (c p) d -> p (e c) d", p=P)).then_inc(s.loaded_w, 16)
            pool.dma_start(b2_sb[:], b2.rearrange("(o e) d -> o (e d)", o=1).broadcast_to([P, NE * D])).then_inc(s.loaded_w, 16)
            pool.wait_ge(s.dve_setup, 1)
            xz = xsorted.rearrange("(p r) d -> p (r d)", p=P)
            done = 0
            while done < ST * D:
                n = min(ZC, ST * D - done)
                pool.dma_start(xz[:, done:done + n], zero[:, 0:n]).then_inc(s.zeroed, 16)
                done += n

            def masks(i):
                def sums(u):
                    tu, hu = u // PH, u % PH
                    sm = sims[:, tu].rearrange("p (h s) k -> p h s k", s=2)
                    if u == POOL_SUMS[0]:
                        pool.wait_ge(s.l0_simcopy, i + 1)
                    if u >= RING:
                        pool.wait_ge(s.l0_mask, i * UNITS + (u - RING + 1))
                    else:
                        since(pool, s.l0_mask, i, UNITS, UNITS - RING + u + 1)
                    pool.tensor_tensor(g[:, u % RING, :].rearrange("p (a b) -> p a b", a=NKEYS),
                                       bc(sm[:, hu, 0, :], 2, NKEYS), bc(sm[:, hu, 1, :], 1, NKEYS),
                                       ALU.add).then_inc(s.l0_sum, 1)

                for u in range(UNITS):
                    if u == 0:
                        for w in POOL_SUMS:
                            if w <= 1:
                                sums(w)
                    if u + 2 in POOL_SUMS and u + 2 > 1:
                        sums(u + 2)
                    t, h = u // PH, u % PH
                    if h == 0:
                        continue
                    pool.wait_ge(s.l0_mask, i * UNITS + (u + 1))
                    k = t * (PH - 1) + h
                    if h > 1:
                        pool.wait_ge(s.l0_coef, i * (UNITS - TB) + (k - 1))
                    pool.tensor_tensor(coef[:, t, :], coef[:, t, :], m[:, u % RING, :], ALU.add).then_inc(s.l0_coef, 1)

            masks(0)
            with pool.Fori(1, B) as i:
                masks(i)

            pool.wait_ge(s.zeroed, 16 * -(-ST * D // ZC))
            pool.wait_ge(s.r_dest, 1)
            pool.wait_ge(s.rows_back, 32)
            for n in range(NT):
                pool.indirect_dma_start(xsorted, bass.IndirectOffsetOnAxis(ap=dest_u[:, n:n + 1], axis=0),
                                        back[n], None).then_inc(s.scattered, 16)
            for k in range(RING):
                pool.wait_ge(tile_stored[k], 16 * (ST // RING))
            for n in range(NT):
                if n >= 4:
                    pool.wait_ge(s.final, n - 3)
                pool.indirect_dma_start(yg[:, n % 4, :], None, ysorted,
                                        bass.IndirectOffsetOnAxis(ap=dest_u[:, n:n + 1], axis=0)).then_inc(gathered[n % 4], 16)

        @block.tensor
        def _(pe):
            mm = pe.matmul

            pe.wait_ge(s.loaded_consts, 32)
            pe.wait_ge(s.loaded_w, 16 * 9)
            for c in range(4):
                ins = pe.transpose(bank[0][:, c * P:(c + 1) * P], key_rows[:, c, :], ident)
            ins.then_inc(s.pe_setup, 1)
            for c in range(EC):
                ins = pe.transpose(bank[1 + c // 4][:, (c % 4) * P:(c % 4 + 1) * P], down_rows[:, c, :], ident)
            ins.then_inc(s.pe_setup, 1)
            pe.transpose(bank[3][:, 0:NE * FC], b1_rows[:], ident[0:NE * FC, 0:NE * FC]).then_inc(s.pe_setup, 1)
            pe.wait_ge(s.act_setup, 1)
            kT = keysT[:].rearrange("p (h k s) -> p h s k", h=PH, s=2)
            for c in range(2 * PH):
                ins = mm(bank[4][:, c * NKEYS:(c + 1) * NKEYS], wqp[:, c, :], kT[:, c // 2, c % 2, :],
                         start=True, stop=True)
            ins.then_inc(s.pe_setup, 1)
            pe.wait_ge(s.act_setup, 5)
            pe.wait_ge(s.dve_setup, 1)
            pe.wait_ge(s.loaded_setup, 16 * 11)

            def l1_front(j, f, m_):
                pe.wait_ge(s.l0_xn1T, j + 1)
                if f is not None:
                    pe.wait_ge(s.l0_z, f + 1)
                elif m_ is not None:
                    pe.wait_ge(s.l0_hid, m_ * 4 + 4)
                for t in range(TB):
                    mm(bank[1 + t][:, 0:3 * D + NE], xn1T[:, t * P:(t + 1) * P], wqkvg1[:], start=True,
                       stop=True).then_inc(s.l1_qkv_ps, 1)

            def l1_turn(j, q, which):
                for n in which:
                    ww, tt_ = n % 2, n // 2
                    if n == which[0]:
                        pe.wait_ge(s.l1_split, j * 4 + 4)
                        if q is not None:
                            pe.wait_ge(s.l1_p, q * NH + NH)
                    if n == 3 and q is not None:
                        pe.wait_ge(s.l1_o, q + 1)
                    b = bank[4 + n][:].bitcast(BF16)
                    for c in range(NH // 2):
                        src = split[:, tt_, ww, 2 * c:2 * c + 2, :].rearrange("p h c -> p (h c)")
                        ins = pe.transpose(b[:, c * P:(c + 1) * P], src, ident_b[:])
                    ins.then_inc(s.l1_T_ps, 1)

            def head(ap, h):
                return ap[HB * (h % 2):HB * (h % 2) + SLOTS * HD, h // 2, :]

            def l1_score(j, h):
                if h == 0:
                    pe.wait_ge(s.l1_T, j * 4 + 4)
                if h >= RING:
                    pe.wait_ge(s.l1_max, j * NH + (h - RING + 1))
                b, q, k = bank[4 + h % RING], head(QT, h), head(KT, h)
                mm(b[:, 128:384], ident_b[:], mask_q[:], start=True, stop=False, skip_group_check=True)
                mm(b[:, 0:256], q[:, P:2 * P], k, start=False, stop=False, skip_group_check=True)
                mm(b[:, 256:384], q[:, 0:P], k[:, 0:P], start=False, stop=True,
                   skip_group_check=True).then_inc(s.l1_s_ps, 1)

            def l1_turn_max(j):
                pe.wait_ge(s.l1_nm, j + 1)
                b = bank[7][:].bitcast(BF16)
                for t in range(TB):
                    ins = pe.transpose(b[:, t * P:(t + 1) * P], nmp[:, t].rearrange("p c r -> p (c r)"), ident_b[:])
                ins.then_inc(s.l1_nmT_ps, 1)

            def l1_prob(j, h):
                if h == 0:
                    pe.wait_ge(s.l1_nmT, j + 1)
                if h >= RING:
                    pe.wait_ge(s.l1_p, j * NH + (h - RING + 1))
                b, q, k = bank[4 + h % RING], head(QT, h), head(KT, h)
                diag = b[:, 0:512].rearrange("p (a c) -> p a c", a=2)[:, :, 0:P]
                mm(diag, ident_b[:], mask_k[:], start=True, stop=False, skip_group_check=True)
                mm(b[:, 0:256], k[:, 0:P], q, start=False, stop=False, skip_group_check=True)
                mm(b[:, 256:384], k[:, P:2 * P], q[:, P:2 * P], start=False, stop=False, skip_group_check=True)
                half = slice(HB * (h % 2), HB * (h % 2) + 3 * NH)
                sel = sel_b[half, h * P:(h + 1) * P]
                mm(b[:, 0:256], sel, nmT[half, :], start=False, stop=False, skip_group_check=True)
                mm(b[:, 256:384], sel, nmT[half, P:2 * P], start=False, stop=True,
                   skip_group_check=True).then_inc(s.l1_p_ps, 1)

            def l1_values(j, h):
                if h == 0:
                    pe.wait_ge(s.l1_vals, j + 1)
                pe.wait_ge(s.l1_p, j * NH + (h + 1))
                o = bank[7][:, 0:TB * NH * (HD + 1)].rearrange("p (t h d) -> p t h d", t=TB, h=NH)
                p = pT[:, h % RING, :]
                mm(o[:, 0, h, :], p[:, 0:P], vaug[:, 0, h, :], start=(h == 0), stop=False, skip_group_check=True)
                mm(o[:, 1, h, :], p[:, P:2 * P], vaug[:, 0, h, :], start=False, stop=False, skip_group_check=True)
                mm(o[:, 1, h, :], p[:, 2 * P:3 * P], vaug[:, 1, h, :], start=False, stop=(h == NH - 1),
                   skip_group_check=True).then_inc(s.l1_pv, 1)

            def l1_out(j, f):
                pe.wait_ge(s.l1_o, j + 1)
                if f is not None:
                    pe.wait_ge(s.l0_sims, f * TB + 2)
                for t in range(TB):
                    ins = pe.transpose(bank[0][:, t * P:(t + 1) * P], o_sb[:, t, :], ident)
                ins.then_inc(s.l1_oT_ps, 1)
                pe.wait_ge(s.l1_oT, j + 1)
                for t in range(TB):
                    ins = mm(bank[3][:, t * P:(t + 1) * P], oT[:, t * P:(t + 1) * P], wo_sb[:], start=True, stop=True)
                ins.then_inc(s.l1_wo_ps, 1)

            def l0_turn(f):
                pe.wait_ge(s.l0_norm, f + 1)
                if not isinstance(f, int) or f > 3:
                    pe.wait_ge(s.l1_oT, f - 3)
                for w in range(2):
                    for t in range(TB):
                        ins = pe.transpose(bank[0][:, (w * TB + t) * P:(w * TB + t + 1) * P], xr[:, w, t, :], ident)
                ins.then_inc(s.l0_xrT_ps, 1)

            def l0_project(f, m_, a):
                pe.wait_ge(s.l0_xrT, f + 1)
                if m_ is not None:
                    pe.wait_ge(s.l0_hid, m_ * 4 + 4)
                for t in range(TB):
                    mm(bank[1 + t][:, 0:3 * D], xrT[:, t * P:(t + 1) * P], wqkv0[:], start=True,
                       stop=True).then_inc(s.l0_qkv_ps, 1)
                if a is not None:
                    pe.wait_ge(s.l0_xn1T, a + 1)
                for t in range(TB):
                    mm(bank[3 * t][:], xrT[:, (TB + t) * P:(TB + t + 1) * P], fold[:], start=True,
                       stop=True).then_inc(s.l0_sim_ps, 1)

            def l0_attention_1(f, a):
                pe.wait_ge(s.l0_kv, f + 1)
                if a is not None:
                    pe.wait_ge(s.l1_qkv, a * 2 + 2)
                for t in range(TB):
                    mm(bank[1][0:LAND, 0:D], pool_mat[:, t, :], kk_sb[:, t, :], start=(t == 0), stop=(t == 1))
                for t in range(TB):
                    mm(bank[1][:, D:2 * D], kk_sb[:, t, :], kv_sb[:, t, :], start=(t == 0), stop=(t == 1))
                for t in range(TB):
                    ins = pe.transpose(bank[2][:, t * P:(t + 1) * P], ez[:, t, 0, :], ident)
                ins.then_inc(s.l0_kl_ps, 1)

            def l0_attention_2(f):
                pe.wait_ge(s.l0_kl, f * 3 + 3)
                mm(bank[2][:, 0:D], klS[:], klS[:], start=True, stop=True).then_inc(s.l0_g_ps, 1)

            def l0_attention_3(f):
                pe.wait_ge(s.l0_g, f + 1)
                mm(bank[1][:, 0:D], gS[:], hS[:], start=True, stop=True).then_inc(s.l0_m_ps, 1)

            def l0_attention_4(f):
                pe.wait_ge(s.l0_m, f + 1)
                for t in range(TB):
                    ins = mm(bank[2][:, t * P:(t + 1) * P], eqT[:, t * P:(t + 1) * P], mS[:], start=True, stop=True)
                ins.then_inc(s.l0_att_ps, 1)

            def l0_down(i, a):
                if a is not None:
                    pe.wait_ge(s.l0_hc, a * 4 + 4)
                else:
                    pe.wait_ge(s.l0_m, i + 1)
                    pe.wait_ge(s.l0_att, i + 1)
                for c in range(EC // 2):
                    if c >= 2:
                        pe.wait_ge(s.l0_hid, i * 4 + (c - 1))
                    for h in range(2):
                        e = 2 * c + h
                        ins = mm(bank[1 + c % 2][:, h * 256:(h + 1) * 256], downT[:, e * P:(e + 1) * P],
                                 xrT[:, 256:512], start=True, stop=True)
                    ins.then_inc(s.l0_down_ps, 1)

            def l0_up(a, m_):
                pe.wait_ge(s.l0_coef, a * (UNITS - TB) + (UNITS - TB))
                if m_ is not None:
                    pe.wait_ge(s.l0_m, m_ + 1)
                    pe.wait_ge(s.l0_att, m_ + 1)
                if not isinstance(a, int) or a:
                    pe.wait_ge(s.l1_qkv, a * 2)
                    pe.wait_ge(s.l1_x2, a)
                for c in range(EC // 2 + 1):
                    if c < EC // 2:
                        if c >= 2:
                            pe.wait_ge(s.l0_hc, a * 4 + (c - 1))
                        for h in range(2):
                            for t in range(TB):
                                e = 2 * c + h
                                ins = pe.transpose(bank[1 + c % 2][:, (h * TB + t) * P:(h * TB + t + 1) * P],
                                                   coef[:, t, e * P:(e + 1) * P], ident)
                        ins.then_inc(s.l0_cT_ps, 1)
                    if c >= 1:
                        pe.wait_ge(s.l0_hc, a * 4 + c)
                        for h in range(2):
                            for t in range(TB):
                                e = 2 * (c - 1) + h
                                ins = mm(bank[3][:, t * P:(t + 1) * P],
                                         hc[:, (c - 1) % 2, (h * TB + t) * P:(h * TB + t + 1) * P], up[:, e, :],
                                         start=(e == 0 and t == 0), stop=(e == EC - 1), skip_group_check=True)
                        ins.then_inc(s.l0_up_ps, 1)

            def l0_turn_x1(a):
                pe.wait_ge(s.l0_xn1, a + 1)
                for t in range(TB):
                    ins = pe.transpose(bank[3][:, t * P:(t + 1) * P], xn1[:, t, :], ident)
                ins.then_inc(s.l0_xn1T_ps, 1)

            def l1_heads(q, first, last):
                if q is None:
                    return
                for h in range(first, last + 1):
                    l1_prob(q, h)
                    if h:
                        l1_values(q, h - 1)
                if last == NH - 1:
                    l1_values(q, NH - 1)

            def body(f, m_, a, q):
                if a is not None:
                    l0_up(a, m_)
                if m_ is not None:
                    l0_down(m_, a)
                if f is not None:
                    l0_turn(f)
                l1_heads(q, 0, 1)
                if a is not None:
                    l0_turn_x1(a)
                if f is not None:
                    l0_project(f, m_, a)
                l1_heads(q, 2, 4)
                if a is not None:
                    l1_front(a, f, m_)
                l1_heads(q, 5, 8)
                if f is not None:
                    l0_attention_1(f, a)
                l1_heads(q, 9, 9)
                if f is not None:
                    l0_attention_2(f)
                l1_heads(q, 10, 10)
                if f is not None:
                    l0_attention_3(f)
                l1_heads(q, 11, 12)
                if f is not None:
                    l0_attention_4(f)
                l1_heads(q, 13, 15)
                if a is not None:
                    l1_turn(a, q, (0, 1, 2))
                if q is not None:
                    l1_out(q, f)
                if a is not None:
                    l1_turn(a, q, (3,))
                    for h in range(NH):
                        l1_score(a, h)
                    l1_turn_max(a)

            rounds(pe, body)

            pe.wait_ge(s.l1_x2, B + 1)
            mm(bank[0][:, 0:NT * NE], cst[:, C_TRI:C_TRI + P], onehot[:], start=True, stop=True)
            mm(bank[1][:, 0:NT * NE], ones[:], onehot[:], start=True, stop=True).then_inc(s.r_rank_ps, 1)

            pe.wait_ge(s.r_te, 1)

            def turn(r, k):
                n = r * RING + k
                pe.wait_ge(tile_loaded[k], r * 16 + 16)
                if not isinstance(n, int) or n:
                    pe.wait_ge(s.f_xT, n)
                pe.transpose(bank[2][:, 0:P], xs[:, k, :], ident).then_inc(s.f_xT_ps, 1)

            def hidden(r, k):
                n = r * RING + k
                pe.wait_ge(s.f_xT, n + 1)
                pe.wait_ge(s.f_w1, n + 1)
                since(pe, s.f_h, r, RING * FC, (k + 1) * FC)
                for c in range(FC):
                    ins = mm(bank[3 + k][:, c * P:(c + 1) * P], w1e[:, k, c * P:(c + 1) * P],
                             xsT[:, k, :], start=True, stop=True)
                ins.then_inc(s.f_h_ps, 1)

            def result(r, k):
                n = r * RING + k
                e = pe.value_load(tile_ei[0:1, bass.ds(n, 1)], min_val=0, max_val=NE - 1)
                pe.wait_ge(s.f_h, n * FC + FC)
                since(pe, s.f_y, r, RING, k + 1)
                for c in range(FC):
                    ins = mm(bank[y_bank[k]][:, 0:D], hT[:, k, c, :], w2_sb[:, bass.ds(e * (FC * D) + c * D, D)],
                             start=(c == 0), stop=(c == FC - 1))
                ins.then_inc(s.f_y_ps, 1)

            def sorted_tiles(r, last=False):
                for k in range(RING):
                    if not (last and k + 2 >= RING):
                        turn(r + (k + 2) // RING, (k + 2) % RING)
                    if not (last and k + 1 >= RING):
                        hidden(r + (k + 1) // RING, (k + 1) % RING)
                    result(r, k)

            turn(0, 0)
            turn(0, 1)
            hidden(0, 0)
            sorted_tiles(0)
            with pe.Fori(1, ST // RING - 1) as r:
                sorted_tiles(r)
            sorted_tiles(ST // RING - 1, last=True)

        @block.scalar
        def _(act):
            def copy(o, i_):
                return act.activation(o, i_, ACT.Copy)

            act.wait_ge(s.pe_setup, 1)
            copy(keysT[:], bank[0][:]).then_inc(s.act_setup, 1)
            act.wait_ge(s.pe_setup, 2)
            for c in range(2):
                act.activation(downT[:, c * 512:(c + 1) * 512], bank[1 + c][:], ACT.Copy, scale=nw[:, 0:1]).then_inc(s.act_setup, 1)
            act.wait_ge(s.pe_setup, 3)
            copy(b1_sb[:], bank[3][:, 0:NE * FC]).then_inc(s.act_setup, 1)
            act.wait_ge(s.pe_setup, 4)
            act.activation(fold[:], bank[4][:], ACT.Copy, scale=nw[:, 0:1]).then_inc(s.act_setup, 1)

            def l0_simcopy(i):
                since(act, s.l0_mask, i, UNITS, UNITS)
                copy(sims[:], sims_next[:]).then_inc(s.l0_simcopy, 1)

            def l0_turned(f):
                act.wait_ge(s.l0_xrT_ps, f + 1)
                copy(xrT[:], bank[0][:]).then_inc(s.l0_xrT, 1)

            def l0_sims(f):
                since(act, s.l0_tau, f, 1, 1)
                for t in range(TB):
                    act.wait_ge(s.l0_sim_ps, f * TB + (t + 1))
                    copy(sims_next[:, t].rearrange("p g k -> p (g k)"), bank[3 * t][:]).then_inc(s.l0_sims, 1)

            def l0_exp(i):
                act.wait_ge(s.l0_zmax, i + 1)
                for t in range(TB):
                    for w in range(2):
                        act.activation(ez[:, t, w, :], z[:, t, w, :], ACT.Exp, bias=zmax[:, t, w:w + 1],
                                       accum_out=zsum[:, t, w:w + 1]).then_inc(s.l0_exp, 1)

            def l0_attention_1(i):
                act.wait_ge(s.l0_kl_ps, i + 1)
                copy(klS[:], bank[1][0:LAND, 0:D]).then_inc(s.l0_kl, 1)
                copy(hS[:], bank[1][:, D:2 * D]).then_inc(s.l0_kl, 1)
                copy(eqT[:], bank[2][:, 0:TB * P]).then_inc(s.l0_kl, 1)

            def l0_attention_2(i):
                act.wait_ge(s.l0_g_ps, i + 1)
                copy(gS[:], bank[2][:, 0:D]).then_inc(s.l0_g, 1)

            def l0_attention_3(i):
                act.wait_ge(s.l0_m_ps, i + 1)
                copy(mS[:], bank[1][:, 0:D]).then_inc(s.l0_m, 1)

            def l0_down(i):
                for c in range(EC // 2):
                    act.wait_ge(s.l0_down_ps, i * 4 + (c + 1))
                    act.activation(hid[:, c, :], bank[1 + c % 2][:], ACT.Gelu).then_inc(s.l0_hid, 1)

            def l0_turned_x1(i):
                act.wait_ge(s.l0_xn1T_ps, i + 1)
                copy(xn1T[:], bank[3][:, 0:TB * P]).then_inc(s.l0_xn1T, 1)

            def l1_split(j):
                for t in range(TB):
                    act.wait_ge(s.l1_lgneg, j + 1)
                    act.activation(lge[:, t, :], lg[:, t, :], ACT.Exp, bias=lgneg[:, t:t + 1],
                                   accum_out=lgs[:, t:t + 1]).then_inc(s.l1_lgsum, 1)
                act.wait_ge(s.l1_qkv, j * 2 + 2)
                sp_all = split[:].rearrange("p t w h c -> p (t w h) c")
                r_all = rot[:].rearrange("p t w (h d) -> p (t w h) d", d=HD)
                copy(sp_all[:, :, 0:HD], r_all).then_inc(s.l1_part, 1)

                def extra(src, w, part, ins=None):
                    for t in range(TB):
                        v = src[:].rearrange("p (t w h) d -> p t w h d", t=TB, w=2)[:, t, w] if src is rest else \
                            src[:, t, w, :].rearrange("p (h d) -> p h d", d=HD)
                        for n, which in enumerate((QPART, KPART)[w]):
                            if which == part and n != part:
                                ins = copy(split[:, t, w, :, n * HD:(n + 1) * HD], v)
                    return ins

                extra(rot, 0, 0)
                extra(rot, 1, 0).then_inc(s.l1_split, 1)
                act.wait_ge(s.l1_rest, j + 1)
                copy(sp_all[:, :, HD:2 * HD], rest[:]).then_inc(s.l1_part, 1)
                extra(rest, 0, 1)
                extra(rest, 1, 1).then_inc(s.l1_split, 1)

            def l1_turn(j):
                for n, (t, w) in enumerate(((0, 0), (0, 1), (1, 0), (1, 1))):
                    act.wait_ge(s.l1_T_ps, j * 4 + (n + 1))
                    copy((QT, KT)[w][:, :, t * P:(t + 1) * P],
                         bank[4 + n][:].bitcast(BF16).rearrange("p (c q) -> p c q", q=P)).then_inc(s.l1_T, 1)

            def l1_turn_max(j):
                act.wait_ge(s.l1_nmT_ps, j + 1)
                copy(nmT[:], bank[7][:].bitcast(BF16)[:, 0:TB * P]).then_inc(s.l1_nmT, 1)

            def l1_heads(q, first, last):
                if q is None:
                    return
                for h in range(first, last + 1):
                    act.wait_ge(s.l1_p_ps, q * NH + (h + 1))
                    if h >= RING:
                        act.wait_ge(s.l1_pv, q * NH + (h - RING + 1))
                    act.activation(pT[:, h % RING, :], bank[4 + h % RING][:, 0:384], ACT.Exp).then_inc(s.l1_p, 1)

            def l1_out(j):
                act.wait_ge(s.l1_oT_ps, j + 1)
                copy(oT[:], bank[0][:, 0:TB * P]).then_inc(s.l1_oT, 1)

            def body(f, m_, a, q):
                if m_ is not None:
                    l0_simcopy(m_)
                    l0_down(m_)
                if f is not None:
                    l0_turned(f)
                l1_heads(q, 0, 1)
                if a is not None:
                    l0_turned_x1(a)
                if f is not None:
                    l0_sims(f)
                l1_heads(q, 2, 4)
                if f is not None:
                    l0_exp(f)
                l1_heads(q, 5, 5)
                if a is not None:
                    l1_split(a)
                l1_heads(q, 6, 8)
                if f is not None:
                    l0_attention_1(f)
                l1_heads(q, 9, 9)
                if f is not None:
                    l0_attention_2(f)
                l1_heads(q, 10, 10)
                if f is not None:
                    l0_attention_3(f)
                l1_heads(q, 11, 15)
                if q is not None:
                    l1_out(q)
                if a is not None:
                    l1_turn(a)
                    l1_turn_max(a)

            rounds(act, body)

            act.wait_ge(s.r_te, 1)

            def sorted_tiles(r):
                for k in range(RING):
                    n = r * RING + k
                    e = act.value_load(tile_ei[0:1, bass.ds(n, 1)], min_val=0, max_val=NE - 1)
                    act.wait_ge(s.f_h_ps, n + 1)
                    since(act, s.f_y_ps, r, RING, k + 1)
                    for c in range(FC):
                        act.activation(hT[:, k, c, :], bank[3 + k][:, c * P:(c + 1) * P], ACT.Gelu,
                                       bias=b1_sb[:, bass.ds(e * FC + c, 1)]).then_inc(s.f_h, 1)

            sorted_tiles(0)
            with act.Fori(1, ST // RING) as r:
                sorted_tiles(r)
            for q in range(NT // 4):
                act.wait_ge(s.final, q * 4 + 4)
                for k in range(4):
                    n = q * 4 + k
                    act.dma_start(out.rearrange("b (t p) d -> (b t) p d", p=P)[n], fin[:, k, :]).then_inc(out_stored[k], 16)
            for k in range(4):
                act.wait_ge(out_stored[k], 16 * (NT // 4))

        @block.vector
        def _(v):
            tt, ts, stt, cp = v.tensor_tensor, v.tensor_scalar, v.scalar_tensor_tensor, v.tensor_copy
            v.memset(ones[:], 1.0)
            v.memset(vaug[:], 1.0)
            v.memset(split[:], 0.0)
            v.memset(nmp[:], 0.0).then_inc(s.l1_x2, 1)
            v.wait_ge(s.loaded_consts, 32)
            for a in range(2):
                cp(mask_q[:, a, :], cst[:, C_MASKQ:C_MASKQ + P])
                cp(mask_k[:, a, :], cst[:, C_MASKK:C_MASKK + P])
            cp(sel_b[:], sel_rows)
            cp(ident_b[:], ident)
            v.memset(zero[:], 0.0).then_inc(s.dve_setup, 1)
            v.wait_ge(s.dve_setup, 1)
            v.wait_ge(s.loaded_x, 64)
            v.wait_ge(s.loaded_setup, 16 * 11)

            def carry_wait():
                v.memset(tick[:], 0.0)

            def norm_stats(c, i, kinds):
                for t in range(TB):
                    a = c.did(v.bn_stats(st[:, t, :], xall[:, bass.ds(i * (TB * D) + t * D, D)]))
                c.need(a)
                carry_wait()
                for t in range(TB):
                    a = c.did(v.bn_aggr(mv[:, t, :], st[:, t, :]))
                c.need(a)
                a = c.did(ts(sv[:, 0, :], mv[:, :, 1], 1.0, 1e-5, ALU.mult, ALU.add))
                if kinds == 2:
                    a = c.did(ts(sv[:, 1, :], mv[:, :, 1], 1.0 + 1e-6, 1e-11, ALU.mult, ALU.add))
                c.need(a)
                y, w = sc[:, 0:kinds, :], sv[:, 0:kinds, :]
                q = sq[:, 0:kinds, :]
                c.need(c.did(v.tensor_single_scalar(y.bitcast(I32), w.bitcast(I32), 1, ALU.arith_shift_right)))
                c.need(c.did(ts(y.bitcast(I32), y.bitcast(I32), -1.0, float(0x5F3759DF), ALU.mult, ALU.add)))
                for _ in range(4):
                    c.need(c.did(tt(q, y, y, ALU.mult)))
                    c.need(c.did(stt(q, q, -0.5, w, ALU.mult, ALU.mult)))
                    c.need(c.did(stt(y, q, 1.5, y, ALU.add, ALU.mult)))

            def l0_front(i, c):
                norm_stats(c, i, 2)
                for w in range(2):
                    for t in range(TB):
                        ins = ts(xr[:, w, t, :], xall[:, bass.ds(i * (TB * D) + t * D, D)], mv[:, t, 0:1],
                                 sc[:, w, t:t + 1], ALU.subtract, ALU.mult)
                ins.then_inc(s.l0_norm, 1)

            def l0_softmax_1(i, c):
                for t in range(TB):
                    v.wait_ge(s.l0_qkv_ps, i * TB + (t + 1))
                    ins = tt(z[:, t].rearrange("p w d -> p (w d)"), bank[1 + t][:, 0:3 * D], bqkv0[:], ALU.add)
                ins.then_inc(s.l0_z, 1)
                v.wait_ge(s.l0_z, i + 1)
                for t in range(TB):
                    a = c.did(v.reduce_max(zmax[:, t, :], z[:, t, 0:2, :], axis=AX_X))
                c.need(a)
                ts(zmax[:], zmax[:], -1.0, None, ALU.mult).then_inc(s.l0_zmax, 1)

            def l0_softmax_2(i, c):
                v.wait_ge(s.l0_exp, i * 4 + 4)
                c.need(c.did(v.reciprocal(zrec[:], zsum[:])))
                for t in range(TB):
                    a = c.did(ts(kk_sb[:, t, :], ez[:, t, 1, :], zrec[:, t, 1:2], None, ALU.mult))
                c.need(a)
                tt(kv_sb[:], kk_sb[:], z[:, :, 2, :], ALU.mult).then_inc(s.l0_kv, 1)

            def l0_topk(i, c, t):
                apart(v)
                v.wait_ge(s.l0_sims, i * TB + (t + 1))
                for q in range(2 * PH):
                    ins = v.max(top[:, t, q, :], sims_next[:, t, q, :])
                c.need(c.did(ins))
                tp = top[:, t].rearrange("p (h s) k -> p h s k", s=2)
                c.need(c.did(tt(pair[:, t].rearrange("p h (a b) -> p h a b", a=TOPK), bc(tp[:, :, 0, :], 3, TOPK),
                                bc(tp[:, :, 1, :], 2, TOPK), ALU.add)))
                carry_wait()
                for h in range(PH):
                    ins = v.max(best[:, t, h, :], pair[:, t, h, :])
                c.did(ins)

            def l0_tau(i, c):
                since(v, s.l0_mask, i, UNITS, UNITS)
                c.need(c.n)
                ts(tau[:], best[:, :, :, TOPK - 1].rearrange("p t h -> p (t h)"), 0.0, None,
                   ALU.max).then_inc(s.l0_tau, 1)

            def l0_attention(i, c):
                v.wait_ge(s.l0_att_ps, i + 1)
                for t in range(TB):
                    xt = xall[:, bass.ds(i * (TB * D) + t * D, D)]
                    ins = stt(xt, bank[2][:, t * P:(t + 1) * P], zrec[:, t, 0:1], xt, ALU.mult, ALU.add)
                ins.then_inc(s.l0_att, 1)

            def l0_unit(i, u):
                t, h = u // PH, u % PH
                sm = sims[:, t].rearrange("p (h s) k -> p h s k", s=2)
                gu = g[:, u % RING, :]
                if u in POOL_SUMS:
                    v.wait_ge(s.l0_sum, i * len(POOL_SUMS) + (POOL_SUMS.index(u) + 1))
                else:
                    if u == 0:
                        v.wait_ge(s.l0_simcopy, i + 1)
                        v.wait_ge(s.l0_tau, i + 1)
                    else:
                        v.wait_ge(s.l0_mask, i * UNITS + (u - RING + 1))
                    tt(gu.rearrange("p (a b) -> p a b", a=NKEYS), bc(sm[:, h, 0, :], 2, NKEYS),
                       bc(sm[:, h, 1, :], 1, NKEYS), ALU.add).then_inc(s.l0_own, 1)
                    v.wait_ge(s.l0_own, i * (UNITS - len(POOL_SUMS)) + (u // 4 + 1))
                if h == 0:
                    dst = coef[:, t, :]
                    since(v, s.l0_cT_ps, i, 4, 4)
                else:
                    dst = m[:, u % RING, :]
                    last = [w for w in range(u) if w % PH and w % RING == u % RING]
                    if last:
                        w = last[-1]
                        v.wait_ge(s.l0_coef, i * (UNITS - TB) + ((w // PH) * (PH - 1) + w % PH))
                    else:
                        since(v, s.l0_coef, i, UNITS - TB, UNITS - TB)
                stt(dst, gu, tau[:, u:u + 1], gu, ALU.is_ge, ALU.mult).then_inc(s.l0_mask, 1)

            def l0_up_1(i, c):
                for k in range(EC // 2):
                    v.wait_ge(s.l0_cT_ps, i * 4 + (k + 1))
                    if k >= 2:
                        v.wait_ge(s.l0_up_ps, i * 4 + (k - 1))
                    tt(hc[:, k % 2, :], bank[1 + k % 2][:], hid[:, k, :], ALU.mult).then_inc(s.l0_hc, 1)
                v.wait_ge(s.l0_up_ps, i * 4 + 4)
                xt = xall[:, bass.ds(i * (TB * D), TB * D)]
                tt(xt, xt, bank[3][:, 0:TB * P], ALU.add).then_inc(s.l0_x1, 1)

            def l0_up_2(i, c):
                apart(v)
                v.wait_ge(s.l0_x1, i + 1)
                norm_stats(c, i, 1)
                since(v, s.l0_kept, i, 16, 16)
                for t in range(TB):
                    ins = ts(xn1[:, t, :], xall[:, bass.ds(i * (TB * D) + t * D, D)], mv[:, t, 0:1],
                             sc[:, 0, t:t + 1], ALU.subtract, ALU.mult)
                ins.then_inc(s.l0_xn1, 1)

            def l1_front(j, c):
                cosv = cst[:, C_COS:C_COS + S].rearrange("p (t c) -> p t c", t=TB)
                sinv = cst[:, C_SIN:C_SIN + S].rearrange("p (t c) -> p t c", t=TB)
                for t in range(TB):
                    v.wait_ge(s.l1_qkv_ps, j * TB + (t + 1))
                    src = bank[1 + t][:, 0:256].rearrange("p (c e) -> p c e", e=2)
                    c.did(tt(ra[:].rearrange("p (c e) -> p c e", e=2), src, bc(cosv[:, t], 2, 2), ALU.mult))
                    a = c.did(tt(rb[:].rearrange("p (c e) -> p c e", e=2), src, bc(sinv[:, t], 2, 2), ALU.mult))
                    c.did(cp(vnext[:, t, :], bank[1 + t][:, 256:384]))
                    b_ = c.did(cp(lg[:, t, :], bank[1 + t][:, 384:384 + NE]))
                    c.need(b_)
                    r2 = rot[:, t].rearrange("p w (c e) -> p (w c) e", e=2)
                    ea, eb = (y[:].rearrange("p (c e) -> p c e", e=2) for y in (ra, rb))
                    c.did(tt(r2[:, :, 0], ea[:, :, 0], eb[:, :, 1], ALU.subtract))
                    ins = tt(r2[:, :, 1], ea[:, :, 1], eb[:, :, 0], ALU.add)
                    ins.then_inc(s.l1_qkv, 1)
                    apart(v)
                    v.wait_ge(s.l1_qkv, j * 2 + (t + 1))
                for t in range(TB):
                    a = c.did(v.max(lg8[:, t, :], lg[:, t, :]))
                c.need(a)
                carry_wait()
                for t in range(TB):
                    c.did(v.max_index(lgi[:, t, :], lg8[:, t, :], lg[:, t, :]))
                ts(lgneg[:], lg8[:, :, 0], -1.0, None, ALU.mult).then_inc(s.l1_lgneg, 1)
                v.wait_ge(s.l1_lgneg, j + 1)
                c.need(c.did(cp(lgf[:], lgi[:, :, 0])))
                for t in range(TB):
                    a = c.did(ts(onehot[:, bass.ds(j * (TB * NE) + t * NE, NE)], cst[:, C_IOTA8:C_IOTA8 + NE],
                             lgf[:, t:t + 1], None, ALU.is_equal))

            def l1_rest(j, c):
                v.wait_ge(s.l1_part, j * 2 + 1)
                sp_all = split[:].rearrange("p t w h c -> p (t w h) c")
                r_all = rot[:].rearrange("p t w (h d) -> p (t w h) d", d=HD)
                tt(rest[:], r_all, sp_all[:, :, 0:HD], ALU.subtract).then_inc(s.l1_rest, 1)
                v.wait_ge(s.l1_part, j * 2 + 2)
                rs = rest[:].rearrange("p (t w h) d -> p t w h d", t=TB, w=2)
                for w, n in ((0, 2), (1, 3)):
                    for t in range(TB):
                        ins = tt(split[:, t, w, :, n * HD:(n + 1) * HD], rs[:, t, w],
                                 split[:, t, w, :, HD:2 * HD], ALU.subtract)
                    ins.then_inc(s.l1_split, 1)
                v.wait_ge(s.l1_lgsum, j * 2 + 2)
                c.did(cp(esum[:, bass.ds(j * TB, TB)], lgs[:]))

            def l1_max(j, h):
                v.wait_ge(s.l1_s_ps, j * NH + (h + 1))
                b = bank[4 + h % RING]
                v.reduce_max(smax[:, 1, h:h + 1], b[:, 0:256], axis=AX_X)
                v.reduce_max(smax[:, 0, h:h + 1], b[:, 256:384], axis=AX_X).then_inc(s.l1_max, 1)

            def l1_nm(j, c):
                v.wait_ge(s.l1_max, j * NH + NH)
                c.need(c.did(ts(nm[:, :, :, 0], smax[:], -1.0, None, ALU.mult)))
                c.need(c.did(stt(srest[:], smax[:], -1.0, nm[:, :, :, 0], ALU.mult, ALU.subtract)))
                c.need(c.did(cp(nm[:, :, :, 1], srest[:])))
                c.need(c.did(tt(nm[:, :, :, 2], srest[:], nm[:, :, :, 1], ALU.subtract)))
                cp(nmp[:, :, 1, :], nmp[:, :, 0, :]).then_inc(s.l1_nm, 1)

            def l1_norm(j, c):
                v.wait_ge(s.l1_pv, j * NH + NH)
                o = bank[7][:, 0:TB * NH * (HD + 1)].rearrange("p (t h d) -> p t h d", t=TB, h=NH)
                c.need(c.did(v.reciprocal(orec[:], o[:, :, :, HD])))
                for t in range(TB):
                    ins = tt(o_sb[:, t].rearrange("p (h d) -> p h d", d=HD), o[:, t, :, 0:HD],
                             bc(orec[:, t], 2, HD), ALU.mult)
                ins.then_inc(s.l1_o, 1)

            def l1_values(j):
                cp(vaug[:, :, :, 0:HD].rearrange("p t h d -> p (t h) d"),
                   vnext[:].rearrange("p t (h d) -> p (t h) d", d=HD)).then_inc(s.l1_vals, 1)

            def l1_out(j):
                v.wait_ge(s.l1_wo_ps, j + 1)
                xt = xall[:, bass.ds(j * (TB * D), TB * D)]
                tt(xt, xt, bank[3][:, 0:TB * P], ALU.add).then_inc(s.l1_x2, 1)

            def body(f, m_, a, q):
                cf, cu, ca, cq = (None if b is None else Marks(v, x_, b * n) for b, x_, n in
                                  ((f, s.l0_v, N_L0V), (a, s.u_v, N_UV), (a, s.l1_v, N_L1V), (q, s.q_v, N_QV)))

                def units(first, last):
                    if m_ is not None:
                        for u in range(first, last + 1):
                            l0_unit(m_, u)

                if a is not None:
                    l0_up_1(a, cu)
                units(0, 0)
                if f is not None:
                    l0_front(f, cf)
                if a is not None:
                    l0_up_2(a, cu)
                units(1, 2)
                if f is not None:
                    l0_softmax_1(f, cf)
                units(3, 3)
                if a is not None:
                    l1_front(a, ca)
                if f is not None:
                    l0_softmax_2(f, cf)
                units(4, 4)
                if a is not None:
                    l1_rest(a, ca)
                units(5, 6)
                if f is not None:
                    l0_topk(f, cf, 0)
                units(7, 8)
                if f is not None:
                    l0_topk(f, cf, 1)
                units(9, 10)
                if f is not None:
                    l0_attention(f, cf)
                units(11, 12)
                if q is not None:
                    l1_norm(q, cq)
                if a is not None:
                    l1_values(a)
                units(13, 13)
                if q is not None:
                    l1_out(q)
                for h in range(NH):
                    if a is not None:
                        l1_max(a, h)
                    if h == 5:
                        units(14, 14)
                    if h == 11:
                        units(15, 15)
                if a is not None:
                    l1_nm(a, ca)
                if f is not None:
                    l0_tau(f, cf)
                for c, n in ((cf, N_L0V), (cu, N_UV), (ca, N_L1V), (cq, N_QV)):
                    assert c is None or c.n == n, [x_ and x_.n for x_ in (cf, cu, ca, cq)]

            rounds(v, body)

            c = Marks(v, s.r_v, 0)
            v.wait_ge(s.r_rank_ps, 1)
            cp(rank[:], bank[0][:, 0:NT * NE])
            c.need(c.did(cp(tot[:], bank[1][:, 0:NT * NE])))
            tv = tot[:].rearrange("p (n e) -> p e n", e=NE)
            for e in range(NE):
                a = c.did(v.tensor_tensor_scan(incl[:, e, :], ones[:, 0:NT], tv[:, e, :], 0.0, ALU.mult, ALU.add))
            c.need(a)
            c.need(c.did(ts(ntile_i[:], incl[:, :, NT - 1], float(P - 1), None, ALU.add)))
            c.need(c.did(v.tensor_single_scalar(ntile_i[:], ntile_i[:], 7, ALU.arith_shift_right)))
            c.need(c.did(cp(ntile[:], ntile_i[:])))
            c.need(c.did(v.tensor_tensor_scan(nincl[:], ones[:, 0:NE], ntile[:], 0.0, ALU.mult, ALU.add)))
            a = c.did(tt(ntile[:], nincl[:], ntile[:], ALU.subtract))
            c.need(c.did(tt(tot[:], rank[:], tot[:], ALU.subtract)))
            rv = rank[:].rearrange("p (n e) -> p n e", e=NE)
            c.need(c.did(tt(tv, tv, incl[:], ALU.add)))
            c.need(c.did(stt(rv, bc(ntile[:], 1, NT), float(P), tot[:].rearrange("p (n e) -> p n e", e=NE),
                             ALU.mult, ALU.add)))
            c.need(c.did(tt(rank[:], rank[:], onehot[:], ALU.mult)))
            c.need(c.did(v.reduce_sum(dest[:], rv, axis=AX_X)))
            cp(dest_u[:], dest[:]).then_inc(s.r_dest, 1)
            c.need(c.did(tt(tcmp[:], bc(cst[:, C_IOTAST:C_IOTAST + ST], 2, NE), bc(nincl[:], 1, ST), ALU.is_ge)))
            c.need(c.did(v.reduce_sum(tile_e[:], tcmp[:], axis=AX_X)))
            ts(tile_ei[:], tile_e[:], float(NE - 1), None, ALU.min).then_inc(s.r_te, 1)
            v.wait_ge(s.r_te, 1)
            c.need(c.did(v.reciprocal(esum[:], esum[:])))

            def ready(r, k):
                n = r * RING + k
                e = v.value_load(tile_ei[0:1, bass.ds(n, 1)], min_val=0, max_val=NE - 1)
                since(v, s.f_h_ps, r, RING, k + 1)
                cp(w1e[:, k, :], w1_sb[:, bass.ds(e * FF, FF)]).then_inc(s.f_w1, 1)
                v.wait_ge(s.f_xT_ps, n + 1)
                cp(xsT[:, k, :], bank[2][:, 0:P]).then_inc(s.f_xT, 1)

            def result(r, k):
                n = r * RING + k
                e = v.value_load(tile_ei[0:1, bass.ds(n, 1)], min_val=0, max_val=NE - 1)
                v.wait_ge(s.f_y_ps, n + 1)
                since(v, tile_stored[k], r, 16, 16)
                tt(ys[:, k, :], bank[y_bank[k]][:, 0:D], b2_sb[:, bass.ds(e * D, D)], ALU.add).then_inc(s.f_y, 1)

            def sorted_tiles(r, last=False):
                for k in range(RING):
                    if not (last and k + 2 >= RING):
                        ready(r + (k + 2) // RING, (k + 2) % RING)
                    result(r, k)

            ready(0, 0)
            ready(0, 1)
            sorted_tiles(0)
            with v.Fori(1, ST // RING - 1) as r:
                sorted_tiles(r)
            sorted_tiles(ST // RING - 1, last=True)
            for n in range(NT):
                v.wait_ge(gathered[n % 4], 16 * (n // 4 + 1))
                if n >= 4:
                    v.wait_ge(out_stored[n % 4], 16 * (n // 4))
                stt(fin[:, n % 4, :], yg[:, n % 4, :], esum[:, n:n + 1], xall[:, n * D:(n + 1) * D],
                    ALU.mult, ALU.add).then_inc(s.final, 1)


_INS = ["L0_attn_hidden_states", "L0_attn_Wq", "L0_attn_bq", "L0_attn_Wk", "L0_attn_bk", "L0_attn_Wv", "L0_attn_bv",
        "L0_ffn_w_q", "L0_ffn_keys", "L0_ffn_expert_down", "L0_ffn_expert_up", "L0_ffn_norm_w",
        "L1_attn_wq", "L1_attn_wk", "L1_attn_wv", "L1_attn_wo", "L1_ffn_gate_w", "L1_ffn_w1", "L1_ffn_b1",
        "L1_ffn_w2", "L1_ffn_b2"]


def kernel(**inputs):
    import numpy as np
    import concourse.bacc as bacc
    from concourse.bass_utils import run_bass_kernel_spmd

    nc = bacc.Bacc("TRN2", target_bir_lowering=False, num_devices=1)
    arrays = {f"in_{name}": np.ascontiguousarray(inputs[name]) for name in _INS}
    arrays["in_shape_constants"] = shape_constants(np)
    args = [nc.dram_tensor(n, a.shape, mybir.dt.from_np(a.dtype), kind="ExternalInput").ap() for n, a in arrays.items()]
    out = nc.dram_tensor("out_dram", (B, S, D), F32, kind="ExternalOutput").ap()
    build(nc, *args, out)
    r = run_bass_kernel_spmd(nc, [arrays], core_ids=[0])
    return r.results[0]["out_dram"]
```

```python
from contextlib import ExitStack

import concourse.bass as bass
from concourse import mybir

F32 = mybir.dt.float32
BF16 = mybir.dt.bfloat16
I32 = mybir.dt.int32
U32 = mybir.dt.uint32
ALU = mybir.AluOpType
ACT = mybir.ActivationFunctionType
AX_X = mybir.AxisListType.X

P = 128
D = 128
B, S = 16, 256
TB = S // P
NT = B * TB
LAND = 64
PH, NKEYS, TOPK = 8, 32, 8
NEXP = NKEYS * NKEYS
EC = NEXP // P
NH, HD = 16, 8
NE, FF = 8, 512
FC = FF // P
ST = NT + NE - 1
SLOTS = 6
HB = 64
QPART = (0, 1, 2, 0, 0, 1)
KPART = (0, 1, 0, 2, 1, 0)
UNITS = TB * PH
RING = 3
GRING = 4
OWN_SUMS = (0, 4, 8)
POOL_SUMS = tuple(u for u in range(UNITS) if u not in OWN_SUMS)
N_ADDS = UNITS - TB - 1
DX = D + 2
NO_TOKEN = 2 * NT * P
ZR = 7
NZ = -(-ST // ZR)
BACK0 = TB * NEXP // DX

C_IDENT, C_POOL, C_MASKQ, C_MASKK, C_TRI = 0, 128, 256, 384, 512
C_COS, C_SIN = 640, 896
C_IOTA8, C_IOTAST = 1152, 1160
C_TOKEN = C_IOTAST + ST
C_SEL = C_TOKEN + NT
C_ALL = C_SEL + NH * P
C_STAY = C_SEL


def shape_constants(np):
    c = np.zeros((P, C_ALL), np.float32)
    r = np.arange(P)
    c[:, C_IDENT:C_IDENT + P] = np.eye(P)
    for t in range(TB):
        c[r, C_POOL + LAND * t + 32 * t + r // 4] = 0.25
    c[:, C_MASKQ:C_MASKQ + P] = np.where(r[None, :] > r[:, None], -1e30, 0.0)
    c[:, C_MASKK:C_MASKK + P] = np.where(r[:, None] > r[None, :], -1e30, 0.0)
    c[:, C_TRI:C_TRI + P] = r[:, None] < r[None, :]
    freq = (1.0 / 10000.0 ** (np.arange(0, HD, 2, dtype=np.float32) / HD)).astype(np.float32)
    ang = (np.arange(S, dtype=np.float32)[:, None] * freq[None, :]).astype(np.float32)
    for t in range(TB):
        for base, tab in ((C_COS, np.cos(ang)), (C_SIN, np.sin(ang))):
            rows = np.tile(tab[t * P:(t + 1) * P], (1, 2 * NH)).astype(np.float32)
            rows[:, :NH * HD // 2] *= np.float32(1.0 / np.sqrt(np.float32(HD)))
            c[:, base + P * t:base + P * (t + 1)] = rows
    c[:, C_IOTA8:C_IOTA8 + NE] = np.arange(NE)
    c[:, C_IOTAST:C_IOTAST + ST] = np.arange(ST)
    c[:, C_TOKEN:C_TOKEN + NT] = P * np.arange(NT)[None, :] + r[:, None]
    for h in range(NH):
        for half in (0, HB):
            c[half + 3 * h:half + 3 * h + 3, C_SEL + P * h:C_SEL + P * (h + 1)] = 1.0
    return c


class Marks:

    def __init__(self, eng, sem, base):
        self.eng, self.sem, self.base, self.n = eng, sem, base, 0

    def did(self, ins):
        ins.then_inc(self.sem, 1)
        self.n += 1
        return self.n

    def need(self, n):
        self.eng.wait_ge(self.sem, self.base + n)


def bc(ap, axis, n):
    ap = ap.unsqueeze(axis)
    return ap.broadcast_to([n if k == axis else s for k, s in enumerate(ap.shape)])


def build(nc, x, Wq, bq, Wk, bk, Wv, bv, w_q, keys, e_down, e_up, norm_w, wq1, wk1, wv1, wo1,
          gate_w, w1, b1, w2, b2, consts, out):
    with ExitStack() as ctx:
        def sb(name, shape, dt=F32):
            return ctx.enter_context(nc.sbuf_tensor(name, shape, dt))

        def sem(name):
            return ctx.enter_context(nc.semaphore(name))

        bank = [ctx.enter_context(nc.psum_tensor(f"bank{k}", [P, 512], F32)) for k in range(8)]

        cst = sb("cst", [P, C_STAY])
        ident = cst[:, C_IDENT:C_IDENT + P]
        pool_mat = cst[:, C_POOL:C_POOL + TB * LAND].rearrange("p (t l) -> p t l", t=TB)
        ones = sb("ones", [P, P])
        ident_b = sb("ident_b", [P, P], BF16)
        mask_q = sb("mask_q", [P, 2, P], BF16)
        mask_k = sb("mask_k", [P, 2, P], BF16)
        sel_b = sb("sel_b", [P, NH * P], BF16)
        wqkv0 = sb("wqkv0", [P, 3 * D])
        bqkv0 = sb("bqkv0", [P, 3 * D])
        fold = sb("fold", [P, 512])
        downT = sb("downT", [P, NEXP])
        up = sb("up", [P, EC, D])
        nw = sb("nw", [P, 1])
        wqkvg1 = sb("wqkvg1", [P, 3 * D + NE])
        wo_sb = sb("wo_sb", [P, D])
        w1_sb = sb("w1_sb", [P, NE * FF])
        w2_sb = sb("w2_sb", [P, NE * FC * D])
        b1_sb = sb("b1_sb", [P, NE * FC])
        b2_sb = sb("b2_sb", [P, NE * D])
        xall = sb("xall", [P, NT * D])
        onehot = sb("onehot", [P, NT * NE])
        esum = sb("esum", [P, NT])
        st = sb("st", [P, 2, TB, 6])
        mv = sb("mv", [P, 2, TB, 2])
        sc = sb("sc", [P, 3, TB])
        sv = sb("sv", [P, 3, TB])
        sq = sb("sq", [P, 3, TB])
        xr = sb("xr", [P, 2, TB, D])
        xrT = sb("xrT", [P, 512])
        z = sb("z", [P, TB, 3, D])
        zmax = sb("zmax", [P, TB, 2])
        ez = sb("ez", [P, TB, 2, D])
        zsum = sb("zsum", [P, TB, 2])
        zrec = sb("zrec", [P, TB, 2])
        kk_sb = sb("kk_sb", [P, TB, D])
        kv_sb = sb("kv_sb", [P, TB, D])
        klS = sb("klS", [LAND, D])
        hS = sb("hS", [P, D])
        eqT = sb("eqT", [P, TB * P])
        gS = sb("gS", [P, D])
        mS = sb("mS", [P, D])
        sims = sb("sims", [P, TB, 2 * PH, NKEYS])
        sims_next = sb("sims_next", [P, TB, 2 * PH, NKEYS])
        top = sb("top", [P, TB, 2 * PH, TOPK])
        pair = sb("pair", [P, TB, PH, TOPK * TOPK])
        best = sb("best", [P, TB, PH, TOPK])
        tau = sb("tau", [P, UNITS])
        g = sb("g", [P, GRING, NEXP])
        m = sb("m", [P, RING, NEXP])
        coef = sb("coef", [P, TB, NEXP])
        wqp = g[:, 0:2].rearrange("p a (b d) -> p (a b) d", d=D)
        down_rows = m[:, 0, :].rearrange("p (c d) -> p c d", d=D)
        key_rows = m[:, 1, 0:512].rearrange("p (c d) -> p c d", d=D)
        sel_rows = coef[:].rearrange("p t e -> p (t e)")
        hid = sb("hid", [P, 4, 512])
        keysT = hid[:, 0, :]
        empty = hid[:, 1:3, :].rearrange("p a b -> p (a b)")[:, 0:ZR * DX].rearrange("p (n d) -> p n d", d=DX)
        b1_rows = hid[0:NE * FC, 3, 0:P]
        xn1 = sb("xn1", [P, TB, D])
        xn1T = sb("xn1T", [P, TB * P])
        rab = sb("rab", [P, 2, 2 * NH * HD])
        ra, rb = rab[:, 0, :], rab[:, 1, :]
        oun = rab[:].rearrange("p a b -> p (a b)")
        rot = sb("rot", [P, TB, 2, NH * HD])
        vaug = sb("vaug", [P, TB, NH, 32])
        vcols = vaug[:].rearrange("p t (c e) m -> p (t c) e m", e=2)
        vnext = sb("vnext", [P, TB, D])
        lg = sb("lg", [P, TB, NE])
        lg8 = sb("lg8", [P, TB, 8])
        lgi = sb("lgi", [P, TB, 8], U32)
        lgf = sb("lgf", [P, TB])
        lgneg = sb("lgneg", [P, TB])
        lge = sb("lge", [P, TB, NE])
        lgs = sb("lgs", [P, TB])
        split = sb("split", [P, TB, 2, NH, HB], BF16)
        rest = sb("rest", [P, TB * 2 * NH, HD])
        QT = sb("QT", [P, NH // 2, TB * P], BF16)
        KT = sb("KT", [P, NH // 2, TB * P], BF16)
        smax = sb("smax", [P, TB, NH])
        srest = sb("srest", [P, TB, NH])
        nmp = sb("nmp", [P, TB, 2, HB], BF16)
        nm = nmp[:, :, 0, 0:3 * NH].rearrange("p t (h r) -> p t h r", r=3)
        nmT = sb("nmT", [P, TB * P], BF16)
        pT = sb("pT", [P, 3, 384])
        orec = sb("orec", [P, TB, NH])
        o_sb = sb("o_sb", [P, TB, D])
        oT = sb("oT", [P, TB * P])
        rank = sb("rank", [P, NT * NE])
        tot = sb("tot", [P, NT * NE])
        incl = sb("incl", [P, NE, NT])
        ntile_i = sb("ntile_i", [P, NE], I32)
        ntile = sb("ntile", [P, NE])
        nincl = sb("nincl", [P, NE])
        dest = sb("dest", [P, NT])
        dest_u = sb("dest_u", [P, NT], U32)
        tcmp = sb("tcmp", [P, ST, NE])
        tile_e = sb("tile_e", [P, ST])
        tile_ei = sb("tile_ei", [P, ST], I32)
        xs = sb("xs", [P, RING, DX])
        meta = sb("meta", [P, RING, 2])
        xsT = sb("xsT", [P, RING, P])
        back = (coef[:].rearrange("p t e -> p (t e)")[:, 0:BACK0 * DX].rearrange("p (n d) -> p n d", d=DX),
                g[:].rearrange("p t e -> p (t e)")[:, 0:(NT - BACK0) * DX].rearrange("p (n d) -> p n d", d=DX))
        parts = ((back[0], slice(0, BACK0)), (back[1], slice(BACK0, NT)))
        hT = hid[:, 0:RING, :].rearrange("p k (c q) -> p k c q", q=P)
        w1e = m[:, :, 0:FF]
        ys = sb("ys", [P, RING, D])
        yt = sb("yt", [P, RING, D])
        y_token = sb("y_token", [P, RING], U32)

        tick = sb("tick", [P, 1])
        pool_tick = sb("pool_tick", [P, 1])

        c_bank = (4, 5, 6, 0)
        q_bank = (4, 5, 6, 1)
        y_bank = (6, 7, 1)

        xn1rows = nc.dram_tensor("xn1rows", [B, TB, P, D], F32, kind="Internal").ap()
        xsorted = nc.dram_tensor("xsorted", [ST * P, DX], F32, kind="Internal").ap()

        S_ = {n: sem(n) for n in (
            "loaded_consts", "loaded_x0", "loaded_x", "loaded_qkv", "loaded_setup", "loaded_keys", "loaded_up", "loaded_w",
            "pe_setup", "act_setup", "dve_setup",
            "v_setup", "l0_tau", "l0_simcopy", "l0_sum", "l0_own", "n_v", "q_v", "rows_back",
            "l0_v", "l0_norm", "l0_xrT_ps", "l0_xrT", "l0_qkv_ps", "l0_sim_ps", "l0_z", "l0_zmax",
            "l0_exp", "l0_sims", "l0_kv", "l0_kl_ps", "l0_kl", "l0_g_ps", "l0_g", "l0_m_ps", "l0_m",
            "l0_att_ps", "l0_att", "l0_mask", "l0_coef", "l0_down_ps", "l0_hid", "l0_cT_ps", "l0_hc",
            "l0_up_ps", "l0_x1", "l0_xn1", "l0_xn1T_ps", "l0_xn1T", "l0_kept",
            "l1_v", "l1_vals", "l1_qkv_ps", "l1_qkv", "l1_lgneg", "l1_lgsum", "l1_part", "l1_rest",
            "l1_split", "l1_T_ps", "l1_T", "l1_s_ps", "l1_max", "l1_nm", "l1_nmT_ps", "l1_nmT", "l1_p_ps", "l1_p",
            "l1_pv", "l1_oun", "l1_o_ps", "l1_o", "l1_oT_ps", "l1_oT", "l1_wo_ps", "l1_x2",
            "r_v", "x2_stored", "ticked", "zeroed", "r_rank_ps", "r_dest", "r_te", "scattered", "f_xT_ps", "f_w1", "f_xT", "f_h_ps",
            "f_h", "f_y_ps", "f_yt", "f_y")}
        s = type("Semaphores", (), S_)
        tile_loaded = [sem(f"tile_loaded{k}") for k in range(RING)]
        tile_stored = [sem(f"tile_stored{k}") for k in range(RING)]

        def since(e, which, i, per, n):
            if isinstance(i, int) and i * per + n - per <= 0:
                return
            e.wait_ge(which, i * per + (n - per))

        def apart(e):
            e.wait_ge(s.dve_setup, 1)

        def rounds(e, body):
            def at(i):
                body(*(b if 0 <= b < B else None for b in (i + 1, i, i - 1, i - 2)))

            for i in range(-1, 3):
                at(i)
            with e.Fori(3, B - 1) as i:
                body(i + 1, i, i - 1, i - 2)
            for i in range(B - 1, B + 2):
                at(i)

        N_L0V, N_NV, N_L1V, N_QV = 11, 14, 22, 1

        block = ctx.enter_context(nc.Block())

        @block.sync
        def _(sp):
            xv = x.rearrange("b (t p) d -> p (b t) d", p=P)
            xs_ = xall[:].rearrange("p (n d) -> p n d", d=D)
            sp.dma_start(xs_[:, 0:TB, :], xv[:, 0:TB, :]).then_inc(s.loaded_x0, 16)
            sp.dma_start(cst[:], consts[:, 0:C_STAY]).then_inc(s.loaded_consts, 16)
            sp.dma_start(sel_rows, consts[:, C_SEL:C_ALL]).then_inc(s.loaded_consts, 16)
            for k, (w, b) in enumerate(((Wq, bq), (Wk, bk), (Wv, bv))):
                sp.dma_start(wqkv0[:, k * D:(k + 1) * D], w).then_inc(s.loaded_qkv, 16)
                sp.dma_start(bqkv0[:, k * D:(k + 1) * D], b.rearrange("(o d) -> o d", o=1).broadcast_to([P, D])).then_inc(s.loaded_qkv, 16)
            for n in range(TB, NT, (NT - TB) // 3):
                rows = slice(n, n + (NT - TB) // 3)
                sp.dma_start(xs_[:, rows, :], xv[:, rows, :]).then_inc(s.loaded_x, 16)
            for k, w in enumerate((wq1, wk1, wv1)):
                sp.dma_start(wqkvg1[:, k * D:(k + 1) * D], w).then_inc(s.loaded_setup, 16)
            sp.dma_start(wqkvg1[:, 3 * D:], gate_w).then_inc(s.loaded_setup, 16)
            sp.dma_start(wo_sb[:], wo1).then_inc(s.loaded_setup, 16)
            def keep_rows(a):
                sp.wait_ge(s.l0_xn1, a + 1)
                sp.dma_start(xn1rows[bass.ds(a, 1)].rearrange("b t p d -> p (b t) d") if not isinstance(a, int) else
                             xn1rows[a:a + 1].rearrange("b t p d -> p (b t) d"), xn1[:]).then_inc(s.l0_kept, 16)

            def store_x2(q):
                sp.wait_ge(s.l1_x2, q + 2)
                sp.dma_start((out[q:q + 1] if isinstance(q, int) else out[bass.ds(q, 1)]).rearrange(
                    "b (t p) d -> p (b t) d", p=P), xs_[:, q * TB:(q + 1) * TB, :] if isinstance(q, int) else
                    xs_[:, bass.ds(q * TB, TB), :]).then_inc(s.x2_stored, 16)

            keep_rows(0)
            with sp.Fori(1, B - 1) as a:
                keep_rows(a)
                store_x2(a - 1)
            keep_rows(B - 1)
            sp.wait_ge(s.l0_kept, 16 * B)
            sp.wait_ge(s.l0_cT_ps, 5 * B)
            for rows, tiles in parts:
                sp.dma_start(rows[:, :, 0:D], xn1rows.rearrange("b t p d -> p (b t) d")[:, tiles, :]).then_inc(s.rows_back, 16)
            store_x2(B - 2)
            sp.wait_ge(s.scattered, 16 * NT)
            for k in range(RING):
                sp.dma_start(xs[:, k, :], xsorted[k * P:(k + 1) * P, :]).then_inc(tile_loaded[k], 16)
            store_x2(B - 1)
            with sp.Fori(1, ST // RING) as r:
                for k in range(RING):
                    since(sp, s.f_xT, r, RING, k + 1)
                    sp.dma_start(xs[:, k, :], xsorted[bass.ds(r * (RING * P) + k * P, P), :]).then_inc(tile_loaded[k], 16)

        @block.gpsimd
        def _(pool):
            pool.dma_start(up[:], e_up.rearrange("(c p) d -> p c d", p=P)).then_inc(s.loaded_up, 16)
            pool.wait_ge(s.dve_setup, 1)
            xz = xsorted.rearrange("(p r) d -> p r d", p=P)
            for n in range(0, ST, ZR):
                pool.dma_start(xz[:, n:min(n + ZR, ST), :], empty[:, 0:min(ZR, ST - n), :]).then_inc(s.zeroed, 16)
            pool.dma_start(w1_sb[:].rearrange("p (e f) -> p e f", e=NE), w1.rearrange("e d f -> d e f")).then_inc(s.loaded_w, 16)
            pool.dma_start(w2_sb[:].rearrange("p (e d) -> p e d", d=D), w2.rearrange("e (c p) d -> p (e c) d", p=P)).then_inc(s.loaded_w, 16)
            pool.dma_start(b2_sb[:], b2.rearrange("(o e) d -> o (e d)", o=1).broadcast_to([P, NE * D])).then_inc(s.loaded_w, 16)

            def masks(i):
                def sums(u):
                    tu, hu = u // PH, u % PH
                    sm = sims[:, tu].rearrange("p (h s) k -> p h s k", s=2)
                    if u == POOL_SUMS[0]:
                        pool.wait_ge(s.l0_simcopy, i + 1)
                    if u >= GRING:
                        pool.wait_ge(s.l0_mask, i * UNITS + (u - GRING + 1))
                    else:
                        since(pool, s.l0_mask, i, UNITS, UNITS - GRING + u + 1)
                    pool.tensor_tensor(g[:, u % GRING, :].rearrange("p (a b) -> p a b", a=NKEYS),
                                       bc(sm[:, hu, 0, :], 2, NKEYS), bc(sm[:, hu, 1, :], 1, NKEYS),
                                       ALU.add).then_inc(s.l0_sum, 1)

                for u in range(UNITS):
                    if u == 0:
                        for w in POOL_SUMS:
                            if w < GRING - 1:
                                sums(w)
                    if u + GRING - 1 in POOL_SUMS:
                        sums(u + GRING - 1)
                    t, h = u // PH, u % PH
                    if h == 0 or u == UNITS - 1:
                        continue
                    pool.wait_ge(s.l0_mask, i * UNITS + (u + 1))
                    k = t * (PH - 1) + h
                    if h > 1:
                        pool.wait_ge(s.l0_coef, i * N_ADDS + (k - 1))
                    pool.tensor_tensor(coef[:, t, :], coef[:, t, :], m[:, u % RING, :], ALU.add).then_inc(s.l0_coef, 1)

            masks(0)
            with pool.Fori(1, B) as i:
                masks(i)

            pool.wait_ge(s.zeroed, 16 * NZ)
            pool.wait_ge(s.r_dest, 1)
            pool.wait_ge(s.rows_back, 32)
            for n in range(NT):
                pool.indirect_dma_start(xsorted, bass.IndirectOffsetOnAxis(ap=dest_u[:, n:n + 1], axis=0),
                                        back[0][:, n, :] if n < BACK0 else back[1][:, n - BACK0, :],
                                        None).then_inc(s.scattered, 16)

            pool.wait_ge(s.x2_stored, 16 * B)
            rows = out.rearrange("b s d -> (b s) d")

            def add_results(r):
                for k in range(RING):
                    if not isinstance(r, int) or k:
                        pool.wait_ge(s.ticked, r * RING + k)
                    pool.wait_ge(s.f_y, r * RING + (k + 1))
                    pool.tensor_tensor(pool_tick[:], ones[:, 0:1], ones[:, 0:1], ALU.add).then_inc(s.ticked, 1)
                    pool.indirect_dma_start(rows, bass.IndirectOffsetOnAxis(ap=y_token[:, k:k + 1], axis=0),
                                            ys[:, k, :], None, bounds_check=NT * P - 1, oob_is_err=False,
                                            compute_op=ALU.add).then_inc(tile_stored[k], 16)

            add_results(0)
            with pool.Fori(1, ST // RING) as r:
                add_results(r)
            for k in range(RING):
                pool.wait_ge(tile_stored[k], 16 * (ST // RING))

        @block.tensor
        def _(pe):
            mm = pe.matmul

            pe.wait_ge(s.loaded_consts, 32)
            pe.wait_ge(s.loaded_keys, 16 * 5)
            for c in range(4):
                ins = pe.transpose(bank[0][:, c * P:(c + 1) * P], key_rows[:, c, :], ident)
            ins.then_inc(s.pe_setup, 1)
            for c in range(EC):
                ins = pe.transpose(bank[1 + c // 4][:, (c % 4) * P:(c % 4 + 1) * P], down_rows[:, c, :], ident)
            ins.then_inc(s.pe_setup, 1)
            pe.transpose(bank[3][:, 0:NE * FC], b1_rows[:], ident[0:NE * FC, 0:NE * FC]).then_inc(s.pe_setup, 1)
            pe.wait_ge(s.act_setup, 1)
            kT = keysT[:].rearrange("p (h k s) -> p h s k", h=PH, s=2)
            for c in range(2 * PH):
                ins = mm(bank[4][:, c * NKEYS:(c + 1) * NKEYS], wqp[:, c, :], kT[:, c // 2, c % 2, :],
                         start=True, stop=True)
            ins.then_inc(s.pe_setup, 1)
            pe.wait_ge(s.act_setup, 5)
            pe.wait_ge(s.dve_setup, 1)

            def l1_front(j, f, m_):
                if isinstance(j, int) and j == 0:
                    pe.wait_ge(s.loaded_setup, 16 * 5)
                """Projections and router logits, then the split q and k turned."""
                pe.wait_ge(s.l0_xn1T, j + 1)
                if f is not None:
                    pe.wait_ge(s.l0_z, f + 1)
                elif m_ is not None:
                    pe.wait_ge(s.l0_hid, m_ * 4 + 4)
                for t in range(TB):
                    mm(bank[1 + t][:, 0:3 * D + NE], xn1T[:, t * P:(t + 1) * P], wqkvg1[:], start=True,
                       stop=True).then_inc(s.l1_qkv_ps, 1)

            def l1_turn(j, f, q):
                pe.wait_ge(s.l1_split, j * 4 + 4)
                if q is not None:
                    pe.wait_ge(s.l1_p, q * NH + NH)
                if f is not None:
                    pe.wait_ge(s.l0_m, f + 1)
                for n in range(4):
                    ww, tt_ = n % 2, n // 2
                    b = bank[q_bank[n]][:].bitcast(BF16)
                    for c in range(NH // 2):
                        src = split[:, tt_, ww, 2 * c:2 * c + 2, :].rearrange("p h c -> p (h c)")
                        ins = pe.transpose(b[:, c * P:(c + 1) * P], src, ident_b[:])
                    ins.then_inc(s.l1_T_ps, 1)

            def head(ap, h):
                return ap[HB * (h % 2):HB * (h % 2) + SLOTS * HD, h // 2, :]

            def l1_score(j, h):
                if h == 0:
                    pe.wait_ge(s.l1_T, j * 4 + 4)
                if h >= RING:
                    pe.wait_ge(s.l1_max, j * NH + (h - RING + 1))
                b, q, k = bank[4 + h % RING], head(QT, h), head(KT, h)
                mm(b[:, 128:384], ident_b[:], mask_q[:], start=True, stop=False, skip_group_check=True)
                mm(b[:, 0:256], q[:, P:2 * P], k, start=False, stop=False, skip_group_check=True)
                mm(b[:, 256:384], q[:, 0:P], k[:, 0:P], start=False, stop=True,
                   skip_group_check=True).then_inc(s.l1_s_ps, 1)

            def l1_turn_max(j):
                pe.wait_ge(s.l1_nm, j + 1)
                b = bank[7][:].bitcast(BF16)
                for t in range(TB):
                    ins = pe.transpose(b[:, t * P:(t + 1) * P], nmp[:, t].rearrange("p c r -> p (c r)"), ident_b[:])
                ins.then_inc(s.l1_nmT_ps, 1)

            def l1_prob(j, h, a):
                if h == 0:
                    pe.wait_ge(s.l1_nmT, j + 1)
                    if a is not None:
                        pe.wait_ge(s.l0_hc, a * 4 + 4)
                if h >= RING:
                    pe.wait_ge(s.l1_p, j * NH + (h - RING + 1))
                b, q, k = bank[4 + h % RING], head(QT, h), head(KT, h)
                diag = b[:, 0:512].rearrange("p (a c) -> p a c", a=2)[:, :, 0:P]
                mm(diag, ident_b[:], mask_k[:], start=True, stop=False, skip_group_check=True)
                mm(b[:, 0:256], k[:, 0:P], q, start=False, stop=False, skip_group_check=True)
                mm(b[:, 256:384], k[:, P:2 * P], q[:, P:2 * P], start=False, stop=False, skip_group_check=True)
                half = slice(HB * (h % 2), HB * (h % 2) + 3 * NH)
                sel = sel_b[half, h * P:(h + 1) * P]
                mm(b[:, 0:256], sel, nmT[half, :], start=False, stop=False, skip_group_check=True)
                mm(b[:, 256:384], sel, nmT[half, P:2 * P], start=False, stop=True,
                   skip_group_check=True).then_inc(s.l1_p_ps, 1)

            def l1_values(j, h):
                if h == 0:
                    pe.wait_ge(s.l1_vals, j + 1)
                pe.wait_ge(s.l1_p, j * NH + (h + 1))
                half, g_ = h // 8, h // 2 % 4
                o = bank[7][32 * g_:32 * g_ + 32, half * 256:half * 256 + 256]
                p = pT[:, h % RING, :]
                mm(o, vaug[:, 0, h, :], p[:, 0:2 * P], start=(h % 2 == 0), stop=False, skip_group_check=True)
                mm(o[:, P:2 * P], vaug[:, 1, h, :], p[:, 2 * P:3 * P], start=False, stop=(h % 2 == 1),
                   skip_group_check=True).then_inc(s.l1_pv, 1)

            def l1_turn_values(j):
                pe.wait_ge(s.l1_oun, j + 1)
                for t in range(TB):
                    for half in range(2):
                        ins = pe.transpose(bank[7][:, (t * 2 + half) * P:(t * 2 + half + 1) * P],
                                           oun[:, (half * TB + t) * P:(half * TB + t + 1) * P], ident)
                ins.then_inc(s.l1_o_ps, 1)

            def l1_out(j, f):
                pe.wait_ge(s.l1_o, j + 1)
                if f is not None:
                    pe.wait_ge(s.l0_sims, f * TB + 2)
                for t in range(TB):
                    ins = pe.transpose(bank[0][:, t * P:(t + 1) * P], o_sb[:, t, :], ident)
                ins.then_inc(s.l1_oT_ps, 1)
                pe.wait_ge(s.l1_oT, j + 1)
                for t in range(TB):
                    ins = mm(bank[3][:, t * P:(t + 1) * P], oT[:, t * P:(t + 1) * P], wo_sb[:], start=True, stop=True)
                ins.then_inc(s.l1_wo_ps, 1)

            def l0_turn(f):
                pe.wait_ge(s.l0_norm, f + 1)
                for w in range(2):
                    for t in range(TB):
                        ins = pe.transpose(bank[0][:, (w * TB + t) * P:(w * TB + t + 1) * P], xr[:, w, t, :], ident)
                ins.then_inc(s.l0_xrT_ps, 1)

            def l0_project(f, m_):
                if isinstance(f, int) and f == 0:
                    pe.wait_ge(s.loaded_qkv, 16 * 6)
                pe.wait_ge(s.l0_xrT, f + 1)
                if m_ is not None:
                    pe.wait_ge(s.l0_hid, m_ * 4 + 4)
                for t in range(TB):
                    mm(bank[1 + t][:, 0:3 * D], xrT[:, t * P:(t + 1) * P], wqkv0[:], start=True,
                       stop=True).then_inc(s.l0_qkv_ps, 1)

            def l0_search(f, a):
                if a is not None:
                    pe.wait_ge(s.l0_xn1T, a + 1)
                for t in range(TB):
                    mm(bank[3 * t][:], xrT[:, (TB + t) * P:(TB + t + 1) * P], fold[:], start=True,
                       stop=True).then_inc(s.l0_sim_ps, 1)

            def l0_attention_1(f, a):
                pe.wait_ge(s.l0_kv, f + 1)
                if a is not None:
                    pe.wait_ge(s.l1_qkv, a * 2 + 2)
                for t in range(TB):
                    mm(bank[1][0:LAND, 0:D], pool_mat[:, t, :], kk_sb[:, t, :], start=(t == 0), stop=(t == 1))
                for t in range(TB):
                    mm(bank[1][:, D:2 * D], kk_sb[:, t, :], kv_sb[:, t, :], start=(t == 0), stop=(t == 1))
                for t in range(TB):
                    ins = pe.transpose(bank[2][:, t * P:(t + 1) * P], ez[:, t, 0, :], ident)
                ins.then_inc(s.l0_kl_ps, 1)

            def l0_attention_2(f):
                pe.wait_ge(s.l0_kl, f * 3 + 3)
                mm(bank[2][:, 0:D], klS[:], klS[:], start=True, stop=True).then_inc(s.l0_g_ps, 1)

            def l0_attention_3(f):
                pe.wait_ge(s.l0_g, f + 1)
                mm(bank[1][:, 0:D], gS[:], hS[:], start=True, stop=True).then_inc(s.l0_m_ps, 1)

            def l0_attention_4(f):
                pe.wait_ge(s.l0_m, f + 1)
                for t in range(TB):
                    ins = mm(bank[2][:, t * P:(t + 1) * P], eqT[:, t * P:(t + 1) * P], mS[:], start=True, stop=True)
                ins.then_inc(s.l0_att_ps, 1)

            def l0_down(i):
                pe.wait_ge(s.l0_m, i + 1)
                pe.wait_ge(s.l0_att, i + 1)
                for c in range(EC // 2):
                    if c >= 2:
                        pe.wait_ge(s.l0_hid, i * 4 + (c - 1))
                    for h in range(2):
                        e = 2 * c + h
                        ins = mm(bank[1 + c % 2][:, h * 256:(h + 1) * 256], downT[:, e * P:(e + 1) * P],
                                 xrT[:, 256:512], start=True, stop=True)
                    ins.then_inc(s.l0_down_ps, 1)

            def l0_turn_coef_0(m_, f, a, q):
                pe.wait_ge(s.l0_coef, m_ * N_ADDS + (PH - 1))
                if f is not None:
                    pe.wait_ge(s.l0_sims, f * TB + TB)
                if q is not None:
                    pe.wait_ge(s.l1_oT, q + 1)
                if a is not None:
                    pe.wait_ge(s.l1_max, a * NH + NH)
                for c in range(EC // 2):
                    for h in range(2):
                        e = 2 * c + h
                        ins = pe.transpose(bank[c_bank[c]][:, h * TB * P:(h * TB + 1) * P],
                                           coef[:, 0, e * P:(e + 1) * P], ident)
                ins.then_inc(s.l0_cT_ps, 1)

            def l0_turn_coef_1(a):
                pe.wait_ge(s.l0_coef, a * N_ADDS + N_ADDS)
                pe.wait_ge(s.l0_mask, a * UNITS + UNITS)
                for c in range(EC // 2):
                    for h in range(2):
                        e = 2 * c + h
                        o = bank[c_bank[c]][:, (h * TB + 1) * P:(h * TB + 2) * P]
                        mm(o, coef[:, 1, e * P:(e + 1) * P], ident, start=True, stop=False, skip_group_check=True)
                        ins = mm(o, m[:, (UNITS - 1) % RING, e * P:(e + 1) * P], ident, start=False, stop=True,
                                 skip_group_check=True)
                    ins.then_inc(s.l0_cT_ps, 1)

            def l0_up(a):
                if isinstance(a, int) and a == 0:
                    pe.wait_ge(s.loaded_up, 16)
                if not isinstance(a, int) or a:
                    pe.wait_ge(s.l1_x2, a)
                for c in range(EC // 2):
                    pe.wait_ge(s.l0_hc, a * 4 + (c + 1))
                    for h in range(2):
                        for t in range(TB):
                            e = 2 * c + h
                            ins = mm(bank[3][:, t * P:(t + 1) * P],
                                     hid[:, c, (h * TB + t) * P:(h * TB + t + 1) * P], up[:, e, :],
                                     start=(e == 0 and t == 0), stop=(e == EC - 1), skip_group_check=True)
                    ins.then_inc(s.l0_up_ps, 1)

            def l0_turn_x1(a):
                pe.wait_ge(s.l0_xn1, a + 1)
                for t in range(TB):
                    ins = pe.transpose(bank[3][:, t * P:(t + 1) * P], xn1[:, t, :], ident)
                ins.then_inc(s.l0_xn1T_ps, 1)

            def rank():
                pe.wait_ge(s.l1_rest, B)
                mm(bank[0][:, 0:NT * NE], cst[:, C_TRI:C_TRI + P], onehot[:], start=True, stop=True)
                mm(bank[0][:, NT * NE:2 * NT * NE], ones[:], onehot[:], start=True, stop=True,
                   skip_group_check=True).then_inc(s.r_rank_ps, 1)

            def l1_heads(q, a, first, last):
                if q is None:
                    return
                for h in range(first, last + 1):
                    l1_prob(q, h, a)
                    if h:
                        l1_values(q, h - 1)
                if last == NH - 1:
                    l1_values(q, NH - 1)

            def body(f, m_, a, q):
                if a is not None:
                    l0_turn_coef_1(a)
                    l0_up(a)
                if m_ is not None:
                    l0_down(m_)
                if f is not None:
                    l0_turn(f)
                if a is not None:
                    l0_turn_x1(a)
                l1_heads(q, a, 0, 0)
                if f is not None:
                    l0_project(f, m_)
                l1_heads(q, a, 1, 2)
                if a is not None:
                    l1_front(a, f, m_)
                l1_heads(q, a, 3, 3)
                if f is not None:
                    l0_search(f, a)
                l1_heads(q, a, 4, 8)
                if a is not None and isinstance(a, int) and a == B - 1:
                    rank()
                if f is not None:
                    l0_attention_1(f, a)
                l1_heads(q, a, 9, 9)
                if f is not None:
                    l0_attention_2(f)
                l1_heads(q, a, 10, 10)
                if f is not None:
                    l0_attention_3(f)
                l1_heads(q, a, 11, 12)
                if f is not None:
                    l0_attention_4(f)
                l1_heads(q, a, 13, 15)
                if a is not None:
                    l1_turn(a, f, q)
                if q is not None:
                    l1_turn_values(q)
                for h in range(NH):
                    if h == 6 and q is not None:
                        l1_out(q, f)
                    if a is not None:
                        l1_score(a, h)
                if m_ is not None:
                    l0_turn_coef_0(m_, f, a, q)
                if a is not None:
                    l1_turn_max(a)

            rounds(pe, body)

            pe.wait_ge(s.r_te, 1)
            pe.wait_ge(s.loaded_w, 16 * 3)

            def turn(r, k):
                n = r * RING + k
                pe.wait_ge(tile_loaded[k], r * 16 + 16)
                if not isinstance(n, int) or n:
                    pe.wait_ge(s.f_xT, n)
                pe.transpose(bank[2][:, 0:P], xs[:, k, 0:D], ident).then_inc(s.f_xT_ps, 1)

            def hidden(r, k):
                n = r * RING + k
                pe.wait_ge(s.f_xT, n + 1)
                pe.wait_ge(s.f_w1, n + 1)
                since(pe, s.f_h, r, RING * FC, (k + 1) * FC)
                for c in range(FC):
                    ins = mm(bank[3 + k][:, c * P:(c + 1) * P], w1e[:, k, c * P:(c + 1) * P],
                             xsT[:, k, :], start=True, stop=True)
                ins.then_inc(s.f_h_ps, 1)

            def result(r, k):
                n = r * RING + k
                e = pe.value_load(tile_ei[0:1, bass.ds(n, 1)], min_val=0, max_val=NE - 1)
                pe.wait_ge(s.f_h, n * FC + FC)
                since(pe, s.f_y, r, RING, k + 1)
                for c in range(FC):
                    ins = mm(bank[y_bank[k]][:, 0:D], hT[:, k, c, :], w2_sb[:, bass.ds(e * (FC * D) + c * D, D)],
                             start=(c == 0), stop=(c == FC - 1))
                ins.then_inc(s.f_y_ps, 1)

            def sorted_tiles(r, last=False):
                for k in range(RING):
                    if not (last and k + 2 >= RING):
                        turn(r + (k + 2) // RING, (k + 2) % RING)
                    if not (last and k + 1 >= RING):
                        hidden(r + (k + 1) // RING, (k + 1) % RING)
                    result(r, k)

            turn(0, 0)
            turn(0, 1)
            hidden(0, 0)
            sorted_tiles(0)
            with pe.Fori(1, ST // RING - 1) as r:
                sorted_tiles(r)
            sorted_tiles(ST // RING - 1, last=True)

        @block.scalar
        def _(act):
            def copy(o, i_):
                return act.activation(o, i_, ACT.Copy)

            act.dma_start(key_rows, keys.rearrange("h k s d -> (h k s) d").rearrange("(c p) d -> p c d", p=P)).then_inc(s.loaded_keys, 16)
            act.dma_start(wqp, w_q.rearrange("(c p) d -> p c d", p=P)).then_inc(s.loaded_keys, 16)
            act.dma_start(nw[:], norm_w.rearrange("(d o) -> d o", o=1)).then_inc(s.loaded_keys, 16)
            act.dma_start(b1_rows, b1.rearrange("e (c p) -> (e c) p", p=P)).then_inc(s.loaded_keys, 16)
            act.dma_start(down_rows, e_down.rearrange("(c p) d -> p c d", p=P)).then_inc(s.loaded_keys, 16)
            act.wait_ge(s.pe_setup, 1)
            copy(keysT[:], bank[0][:]).then_inc(s.act_setup, 1)
            act.wait_ge(s.pe_setup, 2)
            for c in range(2):
                act.activation(downT[:, c * 512:(c + 1) * 512], bank[1 + c][:], ACT.Copy, scale=nw[:, 0:1]).then_inc(s.act_setup, 1)
            act.wait_ge(s.pe_setup, 3)
            copy(b1_sb[:], bank[3][:, 0:NE * FC]).then_inc(s.act_setup, 1)
            act.wait_ge(s.pe_setup, 4)
            act.activation(fold[:], bank[4][:], ACT.Copy, scale=nw[:, 0:1]).then_inc(s.act_setup, 1)

            def l0_simcopy(i):
                since(act, s.l0_mask, i, UNITS, UNITS)
                copy(sims[:], sims_next[:]).then_inc(s.l0_simcopy, 1)

            def l0_turned(f):
                act.wait_ge(s.l0_xrT_ps, f + 1)
                copy(xrT[:], bank[0][:]).then_inc(s.l0_xrT, 1)

            def l0_sims(f):
                since(act, s.l0_tau, f, 1, 1)
                for t in range(TB):
                    act.wait_ge(s.l0_sim_ps, f * TB + (t + 1))
                    copy(sims_next[:, t].rearrange("p g k -> p (g k)"), bank[3 * t][:]).then_inc(s.l0_sims, 1)

            def l0_exp(i):
                act.wait_ge(s.l0_zmax, i + 1)
                for t in range(TB):
                    for w in range(2):
                        act.activation(ez[:, t, w, :], z[:, t, w, :], ACT.Exp, bias=zmax[:, t, w:w + 1],
                                       accum_out=zsum[:, t, w:w + 1]).then_inc(s.l0_exp, 1)

            def l0_attention_1(i):
                act.wait_ge(s.l0_kl_ps, i + 1)
                copy(klS[:], bank[1][0:LAND, 0:D]).then_inc(s.l0_kl, 1)
                copy(hS[:], bank[1][:, D:2 * D]).then_inc(s.l0_kl, 1)
                copy(eqT[:], bank[2][:, 0:TB * P]).then_inc(s.l0_kl, 1)

            def l0_attention_2(i):
                act.wait_ge(s.l0_g_ps, i + 1)
                copy(gS[:], bank[2][:, 0:D]).then_inc(s.l0_g, 1)

            def l0_attention_3(i):
                act.wait_ge(s.l0_m_ps, i + 1)
                copy(mS[:], bank[1][:, 0:D]).then_inc(s.l0_m, 1)

            def l0_down(i, a):
                if isinstance(i, int) and i == 0:
                    act.wait_ge(s.zeroed, 16 * NZ)
                for c in range(EC // 2):
                    if a is not None:
                        act.wait_ge(s.l0_up_ps, a * 4 + (c + 1))
                    act.wait_ge(s.l0_down_ps, i * 4 + (c + 1))
                    act.activation(hid[:, c, :], bank[1 + c % 2][:], ACT.Gelu).then_inc(s.l0_hid, 1)

            def l0_turned_x1(i):
                act.wait_ge(s.l0_xn1T_ps, i + 1)
                copy(xn1T[:], bank[3][:, 0:TB * P]).then_inc(s.l0_xn1T, 1)

            sp_all = split[:].rearrange("p t w h c -> p (t w h) c")
            r_all = rot[:].rearrange("p t w (h d) -> p (t w h) d", d=HD)

            def extra(src, w, part, ins=None):
                for t in range(TB):
                    v = src[:].rearrange("p (t w h) d -> p t w h d", t=TB, w=2)[:, t, w] if src is rest else \
                        src[:, t, w, :].rearrange("p (h d) -> p h d", d=HD)
                    for n, which in enumerate((QPART, KPART)[w]):
                        if which == part and n != part:
                            ins = copy(split[:, t, w, :, n * HD:(n + 1) * HD], v)
                return ins

            def l1_split_1(j):
                for t in range(TB):
                    act.wait_ge(s.l1_lgneg, j + 1)
                    act.activation(lge[:, t, :], lg[:, t, :], ACT.Exp, bias=lgneg[:, t:t + 1],
                                   accum_out=lgs[:, t:t + 1]).then_inc(s.l1_lgsum, 1)
                act.wait_ge(s.l1_qkv, j * 2 + 2)
                copy(sp_all[:, :, 0:HD], r_all).then_inc(s.l1_part, 1)

                extra(rot, 0, 0)
                extra(rot, 1, 0).then_inc(s.l1_split, 1)
            def l1_split_2(j):
                act.wait_ge(s.l1_rest, j + 1)
                copy(sp_all[:, :, HD:2 * HD], rest[:]).then_inc(s.l1_part, 1)
                extra(rest, 0, 1)
                extra(rest, 1, 1).then_inc(s.l1_split, 1)

            def l1_turn(j):
                for n, (t, w) in enumerate(((0, 0), (0, 1), (1, 0), (1, 1))):
                    act.wait_ge(s.l1_T_ps, j * 4 + (n + 1))
                    copy((QT, KT)[w][:, :, t * P:(t + 1) * P],
                         bank[q_bank[n]][:].bitcast(BF16).rearrange("p (c q) -> p c q", q=P)).then_inc(s.l1_T, 1)

            def l1_turn_max(j):
                act.wait_ge(s.l1_nmT_ps, j + 1)
                copy(nmT[:], bank[7][:].bitcast(BF16)[:, 0:TB * P]).then_inc(s.l1_nmT, 1)

            def l1_heads(q, first, last):
                if q is None:
                    return
                for h in range(first, last + 1):
                    act.wait_ge(s.l1_p_ps, q * NH + (h + 1))
                    if h >= RING:
                        act.wait_ge(s.l1_pv, q * NH + (h - RING + 1))
                    act.activation(pT[:, h % RING, :], bank[4 + h % RING][:, 0:384], ACT.Exp).then_inc(s.l1_p, 1)

            def l1_unturned(j):
                act.wait_ge(s.l1_pv, j * NH + NH)
                copy(oun, bank[7][:]).then_inc(s.l1_oun, 1)

            def l1_out(j):
                act.wait_ge(s.l1_oT_ps, j + 1)
                copy(oT[:], bank[0][:, 0:TB * P]).then_inc(s.l1_oT, 1)

            def body(f, m_, a, q):
                if m_ is not None:
                    l0_down(m_, a)
                if f is not None:
                    l0_turned(f)
                if a is not None:
                    l0_turned_x1(a)
                l1_heads(q, 0, 2)
                if f is not None:
                    l0_exp(f)
                l1_heads(q, 3, 3)
                if f is not None:
                    l0_sims(f)
                l1_heads(q, 4, 6)
                if a is not None:
                    l1_split_1(a)
                l1_heads(q, 7, 8)
                if a is not None:
                    l1_split_2(a)
                if f is not None:
                    l0_attention_1(f)
                l1_heads(q, 9, 9)
                if f is not None:
                    l0_attention_2(f)
                l1_heads(q, 10, 10)
                if f is not None:
                    l0_attention_3(f)
                l1_heads(q, 11, 15)
                if q is not None:
                    l1_unturned(q)
                if a is not None:
                    l1_turn(a)
                if q is not None:
                    l1_out(q)
                if f is not None:
                    l0_simcopy(f)
                if a is not None:
                    l1_turn_max(a)

            rounds(act, body)

            act.wait_ge(s.r_te, 1)

            def sorted_tiles(r):
                for k in range(RING):
                    n = r * RING + k
                    e = act.value_load(tile_ei[0:1, bass.ds(n, 1)], min_val=0, max_val=NE - 1)
                    act.wait_ge(s.f_h_ps, n + 1)
                    since(act, s.f_y_ps, r, RING, k + 1)
                    for c in range(FC):
                        act.activation(hT[:, k, c, :], bank[3 + k][:, c * P:(c + 1) * P], ACT.Gelu,
                                       bias=b1_sb[:, bass.ds(e * FC + c, 1)]).then_inc(s.f_h, 1)

            sorted_tiles(0)
            with act.Fori(1, ST // RING) as r:
                sorted_tiles(r)

        @block.vector
        def _(v):
            tt, ts, stt, cp = v.tensor_tensor, v.tensor_scalar, v.scalar_tensor_tensor, v.tensor_copy
            v.memset(ones[:], 1.0)
            v.memset(vaug[:], 0.0).then_inc(s.v_setup, 1)
            v.wait_ge(s.v_setup, 1)
            for e in range(2):
                v.memset(vcols[:, :, e, (HD + 1) * e + HD:(HD + 1) * e + HD + 1], 1.0)
            v.memset(split[:], 0.0)
            v.memset(nmp[:], 0.0).then_inc(s.l1_x2, 1)
            v.wait_ge(s.loaded_consts, 32)
            for a in range(2):
                cp(mask_q[:, a, :], cst[:, C_MASKQ:C_MASKQ + P])
                cp(mask_k[:, a, :], cst[:, C_MASKK:C_MASKK + P])
            cp(sel_b[:], sel_rows)
            cp(ident_b[:], ident)
            v.memset(empty[:, :, 0:D + 1], 0.0)
            v.memset(empty[:, :, D + 1:DX], float(NO_TOKEN)).then_inc(s.dve_setup, 1)
            v.wait_ge(s.dve_setup, 1)
            v.wait_ge(s.loaded_x0, 16)

            def carry_wait():
                v.memset(tick[:], 0.0)

            def norm_stats(c, f, a_):
                if isinstance(f, int) and f == 1:
                    v.wait_ge(s.loaded_x, 16 * 3)
                """Mean and variance of the rows of x of batches f and a_. sc: 1 and 2 are their factors
                1 / sqrt(variance + 1e-5); 0 is one of f's that also divides by the root of the normed
                row's mean square: rstd / sqrt(var rstd^2 + 1e-6) = 1 / sqrt(var (1 + 1e-6) + 1e-11)."""
                both = [n for n, b in enumerate((f, a_)) if b is not None]
                lo, hi = both[0], both[-1] + 1
                if a_ is not None:
                    apart(v)
                    v.wait_ge(s.l0_x1, a_ + 1)
                for n in both:
                    for t in range(TB):
                        ins = v.bn_stats(st[:, n, t, :], xall[:, bass.ds((f, a_)[n] * (TB * D) + t * D, D)])
                c.need(c.did(ins))
                carry_wait()
                for n in both:
                    for t in range(TB):
                        ins = v.bn_aggr(mv[:, n, t, :], st[:, n, t, :])
                c.need(c.did(ins))
                ins = ts(sv[:, 1 + lo:1 + hi, :], mv[:, lo:hi, :, 1], 1.0, 1e-5, ALU.mult, ALU.add)
                if f is not None:
                    ins = ts(sv[:, 0, :], mv[:, 0, :, 1], 1.0 + 1e-6, 1e-11, ALU.mult, ALU.add)
                c.need(c.did(ins))
                kinds = slice(2 * lo, 1 + hi)
                y, w = sc[:, kinds, :], sv[:, kinds, :]
                q = sq[:, kinds, :]
                c.need(c.did(v.tensor_single_scalar(y.bitcast(I32), w.bitcast(I32), 1, ALU.arith_shift_right)))
                c.need(c.did(ts(y.bitcast(I32), y.bitcast(I32), -1.0, float(0x5F3759DF), ALU.mult, ALU.add)))
                for _ in range(3):
                    c.need(c.did(tt(q, y, y, ALU.mult)))
                    c.need(c.did(stt(q, q, -0.5, w, ALU.mult, ALU.mult)))
                    c.need(c.did(stt(y, q, 1.5, y, ALU.add, ALU.mult)))

            def l0_front(i):
                for w in range(2):
                    for t in range(TB):
                        ins = ts(xr[:, w, t, :], xall[:, bass.ds(i * (TB * D) + t * D, D)], mv[:, 0, t, 0:1],
                                 sc[:, 1 - w, t:t + 1], ALU.subtract, ALU.mult)
                ins.then_inc(s.l0_norm, 1)

            def l0_softmax_1(i, c):
                if isinstance(i, int) and i == 0:
                    v.wait_ge(s.loaded_qkv, 16 * 6)
                for t in range(TB):
                    v.wait_ge(s.l0_qkv_ps, i * TB + (t + 1))
                    ins = tt(z[:, t].rearrange("p w d -> p (w d)"), bank[1 + t][:, 0:3 * D], bqkv0[:], ALU.add)
                ins.then_inc(s.l0_z, 1)
                v.wait_ge(s.l0_z, i + 1)
                for t in range(TB):
                    a = c.did(v.reduce_max(zmax[:, t, :], z[:, t, 0:2, :], axis=AX_X))
                c.need(a)
                ts(zmax[:], zmax[:], -1.0, None, ALU.mult).then_inc(s.l0_zmax, 1)

            def l0_softmax_2(i, c):
                v.wait_ge(s.l0_exp, i * 4 + 4)
                c.need(c.did(v.reciprocal(zrec[:], zsum[:])))
                for t in range(TB):
                    a = c.did(ts(kk_sb[:, t, :], ez[:, t, 1, :], zrec[:, t, 1:2], None, ALU.mult))
                c.need(a)
                tt(kv_sb[:], kk_sb[:], z[:, :, 2, :], ALU.mult).then_inc(s.l0_kv, 1)

            def l0_topk(i, c, t):
                apart(v)
                v.wait_ge(s.l0_sims, i * TB + (t + 1))
                for q in range(2 * PH):
                    ins = v.max(top[:, t, q, :], sims_next[:, t, q, :])
                c.need(c.did(ins))
                tp = top[:, t].rearrange("p (h s) k -> p h s k", s=2)
                c.need(c.did(tt(pair[:, t].rearrange("p h (a b) -> p h a b", a=TOPK), bc(tp[:, :, 0, :], 3, TOPK),
                                bc(tp[:, :, 1, :], 2, TOPK), ALU.add)))
                carry_wait()
                for h in range(PH):
                    ins = v.max(best[:, t, h, :], pair[:, t, h, :])
                c.did(ins)

            def l0_tau(i, c):
                since(v, s.l0_mask, i, UNITS, UNITS)
                c.need(c.n)
                ts(tau[:], best[:, :, :, TOPK - 1].rearrange("p t h -> p (t h)"), 0.0, None,
                   ALU.max).then_inc(s.l0_tau, 1)

            def l0_attention(i, c):
                v.wait_ge(s.l0_att_ps, i + 1)
                for t in range(TB):
                    xt = xall[:, bass.ds(i * (TB * D) + t * D, D)]
                    ins = stt(xt, bank[2][:, t * P:(t + 1) * P], zrec[:, t, 0:1], xt, ALU.mult, ALU.add)
                ins.then_inc(s.l0_att, 1)

            def l0_unit(i, u):
                t, h = u // PH, u % PH
                sm = sims[:, t].rearrange("p (h s) k -> p h s k", s=2)
                gu = g[:, u % GRING, :]
                if u in POOL_SUMS:
                    v.wait_ge(s.l0_sum, i * len(POOL_SUMS) + (POOL_SUMS.index(u) + 1))
                else:
                    if u == 0:
                        v.wait_ge(s.l0_simcopy, i + 1)
                        v.wait_ge(s.l0_tau, i + 1)
                    else:
                        v.wait_ge(s.l0_mask, i * UNITS + (u - GRING + 1))
                    tt(gu.rearrange("p (a b) -> p a b", a=NKEYS), bc(sm[:, h, 0, :], 2, NKEYS),
                       bc(sm[:, h, 1, :], 1, NKEYS), ALU.add).then_inc(s.l0_own, 1)
                    v.wait_ge(s.l0_own, i * len(OWN_SUMS) + (OWN_SUMS.index(u) + 1))
                if h == 0:
                    dst = coef[:, t, :]
                    since(v, s.l0_cT_ps, i, 5, 1 if t == 0 else 5)
                else:
                    dst = m[:, u % RING, :]
                    last = [w for w in range(u) if w % PH and w % RING == u % RING]
                    if last:
                        w = last[-1]
                        v.wait_ge(s.l0_coef, i * N_ADDS + ((w // PH) * (PH - 1) + w % PH))
                    elif u % RING == (UNITS - 1) % RING:
                        since(v, s.l0_cT_ps, i, 5, 5)
                    else:
                        since(v, s.l0_coef, i, N_ADDS, N_ADDS)
                stt(dst, gu, tau[:, u:u + 1], gu, ALU.is_ge, ALU.mult).then_inc(s.l0_mask, 1)

            def l0_weigh(i):
                for k in range(EC // 2):
                    v.wait_ge(s.l0_cT_ps, i * 5 + (k + 2))
                    tt(hid[:, k, :], bank[c_bank[k]][:], hid[:, k, :], ALU.mult).then_inc(s.l0_hc, 1)

            def l0_up_1(i):
                v.wait_ge(s.l0_up_ps, i * 4 + 4)
                xt = xall[:, bass.ds(i * (TB * D), TB * D)]
                tt(xt, xt, bank[3][:, 0:TB * P], ALU.add).then_inc(s.l0_x1, 1)

            def l0_up_2(i):
                since(v, s.l0_kept, i, 16, 16)
                for t in range(TB):
                    ins = ts(xn1[:, t, :], xall[:, bass.ds(i * (TB * D) + t * D, D)], mv[:, 1, t, 0:1],
                             sc[:, 2, t:t + 1], ALU.subtract, ALU.mult)
                ins.then_inc(s.l0_xn1, 1)

            def l1_front(j, c):
                cosv = cst[:, C_COS:C_COS + S].rearrange("p (t c) -> p t c", t=TB)
                sinv = cst[:, C_SIN:C_SIN + S].rearrange("p (t c) -> p t c", t=TB)
                for t in range(TB):
                    v.wait_ge(s.l1_qkv_ps, j * TB + (t + 1))
                    src = bank[1 + t][:, 0:256].rearrange("p (c e) -> p c e", e=2)
                    c.did(tt(ra[:].rearrange("p (c e) -> p c e", e=2), src, bc(cosv[:, t], 2, 2), ALU.mult))
                    a = c.did(tt(rb[:].rearrange("p (c e) -> p c e", e=2), src, bc(sinv[:, t], 2, 2), ALU.mult))
                    c.did(cp(vnext[:, t, :], bank[1 + t][:, 256:384]))
                    b_ = c.did(cp(lg[:, t, :], bank[1 + t][:, 384:384 + NE]))
                    c.need(b_)
                    r2 = rot[:, t].rearrange("p w (c e) -> p (w c) e", e=2)
                    ea, eb = (y[:].rearrange("p (c e) -> p c e", e=2) for y in (ra, rb))
                    c.did(tt(r2[:, :, 0], ea[:, :, 0], eb[:, :, 1], ALU.subtract))
                    ins = tt(r2[:, :, 1], ea[:, :, 1], eb[:, :, 0], ALU.add)
                    ins.then_inc(s.l1_qkv, 1)
                    apart(v)
                    v.wait_ge(s.l1_qkv, j * 2 + (t + 1))
                for t in range(TB):
                    a = c.did(v.max(lg8[:, t, :], lg[:, t, :]))
                c.need(a)
                carry_wait()
                for t in range(TB):
                    c.did(v.max_index(lgi[:, t, :], lg8[:, t, :], lg[:, t, :]))
                ts(lgneg[:], lg8[:, :, 0], -1.0, None, ALU.mult).then_inc(s.l1_lgneg, 1)
                v.wait_ge(s.l1_lgneg, j + 1)
                c.need(c.did(cp(lgf[:], lgi[:, :, 0])))
                for t in range(TB):
                    a = c.did(ts(onehot[:, bass.ds(j * (TB * NE) + t * NE, NE)], cst[:, C_IOTA8:C_IOTA8 + NE],
                             lgf[:, t:t + 1], None, ALU.is_equal))

            def l1_rest(j, c):
                v.wait_ge(s.l1_part, j * 2 + 1)
                sp_all = split[:].rearrange("p t w h c -> p (t w h) c")
                r_all = rot[:].rearrange("p t w (h d) -> p (t w h) d", d=HD)
                tt(rest[:], r_all, sp_all[:, :, 0:HD], ALU.subtract).then_inc(s.l1_rest, 1)
                v.wait_ge(s.l1_part, j * 2 + 2)
                rs = rest[:].rearrange("p (t w h) d -> p t w h d", t=TB, w=2)
                for w, n in ((0, 2), (1, 3)):
                    for t in range(TB):
                        ins = tt(split[:, t, w, :, n * HD:(n + 1) * HD], rs[:, t, w],
                                 split[:, t, w, :, HD:2 * HD], ALU.subtract)
                    ins.then_inc(s.l1_split, 1)
                v.wait_ge(s.l1_lgsum, j * 2 + 2)
                c.did(cp(esum[:, bass.ds(j * TB, TB)], lgs[:]))

            def l1_max(j, h):
                v.wait_ge(s.l1_s_ps, j * NH + (h + 1))
                b = bank[4 + h % RING]
                v.reduce_max(smax[:, 1, h:h + 1], b[:, 0:256], axis=AX_X)
                v.reduce_max(smax[:, 0, h:h + 1], b[:, 256:384], axis=AX_X).then_inc(s.l1_max, 1)

            def l1_nm(j, c):
                v.wait_ge(s.l1_max, j * NH + NH)
                c.need(c.did(ts(nm[:, :, :, 0], smax[:], -1.0, None, ALU.mult)))
                c.need(c.did(stt(srest[:], smax[:], -1.0, nm[:, :, :, 0], ALU.mult, ALU.subtract)))
                c.need(c.did(cp(nm[:, :, :, 1], srest[:])))
                c.need(c.did(tt(nm[:, :, :, 2], srest[:], nm[:, :, :, 1], ALU.subtract)))
                cp(nmp[:, :, 1, :], nmp[:, :, 0, :]).then_inc(s.l1_nm, 1)

            def l1_norm(j, c):
                v.wait_ge(s.l1_o_ps, j + 1)
                o = bank[7][:].rearrange("p (a m) -> p a m", m=32)[:, :, 0:2 * (HD + 1)].rearrange(
                    "p a (e d) -> p a e d", e=2)
                r = orec[:].rearrange("p t (c e) -> p (t c) e", e=2)
                c.need(c.did(v.reciprocal(r, o[:, :, :, HD])))
                tt(o_sb[:].rearrange("p t (c e d) -> p (t c) e d", e=2, d=HD), o[:, :, :, 0:HD],
                   bc(r, 3, HD), ALU.mult).then_inc(s.l1_o, 1)

            def l1_values(j):
                vn = vnext[:].rearrange("p t (c e d) -> p (t c) e d", e=2, d=HD)
                for e in range(2):
                    ins = cp(vcols[:, :, e, (HD + 1) * e:(HD + 1) * e + HD], vn[:, :, e, :])
                ins.then_inc(s.l1_vals, 1)

            def l1_out(j):
                v.wait_ge(s.l1_wo_ps, j + 1)
                xt = xall[:, bass.ds(j * (TB * D), TB * D)]
                tt(xt, xt, bank[3][:, 0:TB * P], ALU.add).then_inc(s.l1_x2, 1)

            def places():
                c = Marks(v, s.r_v, 0)
                c.did(v.reciprocal(esum[:], esum[:]))
                v.wait_ge(s.r_rank_ps, 1)
                cp(rank[:], bank[0][:, 0:NT * NE])
                c.need(c.did(cp(tot[:], bank[0][:, NT * NE:2 * NT * NE])))
                tv = tot[:].rearrange("p (n e) -> p e n", e=NE)
                for e in range(NE):
                    a = c.did(v.tensor_tensor_scan(incl[:, e, :], ones[:, 0:NT], tv[:, e, :], 0.0, ALU.mult, ALU.add))
                c.need(a)
                c.need(c.did(ts(ntile_i[:], incl[:, :, NT - 1], float(P - 1), None, ALU.add)))
                c.need(c.did(v.tensor_single_scalar(ntile_i[:], ntile_i[:], 7, ALU.arith_shift_right)))
                c.need(c.did(cp(ntile[:], ntile_i[:])))
                c.need(c.did(v.tensor_tensor_scan(nincl[:], ones[:, 0:NE], ntile[:], 0.0, ALU.mult, ALU.add)))
                a = c.did(tt(ntile[:], nincl[:], ntile[:], ALU.subtract))
                c.need(c.did(tt(tot[:], rank[:], tot[:], ALU.subtract)))
                rv = rank[:].rearrange("p (n e) -> p n e", e=NE)
                c.need(c.did(tt(tv, tv, incl[:], ALU.add)))
                c.need(c.did(stt(rv, bc(ntile[:], 1, NT), float(P), tot[:].rearrange("p (n e) -> p n e", e=NE),
                                 ALU.mult, ALU.add)))
                c.need(c.did(tt(rank[:], rank[:], onehot[:], ALU.mult)))
                c.need(c.did(v.reduce_sum(dest[:], rv, axis=AX_X)))
                v.wait_ge(s.l0_cT_ps, 5 * B)
                for rows, tiles in parts:
                    cp(rows[:, :, D:D + 1], esum[:, tiles].unsqueeze(2))
                    cp(rows[:, :, D + 1:DX], cst[:, C_TOKEN:C_TOKEN + NT][:, tiles].unsqueeze(2))
                cp(dest_u[:], dest[:]).then_inc(s.r_dest, 1)
                c.need(c.did(tt(tcmp[:], bc(cst[:, C_IOTAST:C_IOTAST + ST], 2, NE), bc(nincl[:], 1, ST), ALU.is_ge)))
                c.need(c.did(v.reduce_sum(tile_e[:], tcmp[:], axis=AX_X)))
                ts(tile_ei[:], tile_e[:], float(NE - 1), None, ALU.min).then_inc(s.r_te, 1)
                v.wait_ge(s.r_te, 1)

            def body(f, m_, a, q):
                r = f if f is not None else None if a is None else a + 2
                cf, cn, ca, cq = (None if b is None else Marks(v, x_, b * n) for b, x_, n in
                                  ((f, s.l0_v, N_L0V), (r, s.n_v, N_NV), (a, s.l1_v, N_L1V), (q, s.q_v, N_QV)))

                def units(first, last):
                    if m_ is not None:
                        for u in range(first, last + 1):
                            l0_unit(m_, u)

                units(0, 1)
                if a is not None:
                    l0_weigh(a)
                units(2, 3)
                if a is not None:
                    l0_up_1(a)
                if r is not None:
                    norm_stats(cn, f, a)
                if a is not None:
                    l0_up_2(a)
                if f is not None:
                    l0_front(f)
                units(4, 5)
                if f is not None:
                    l0_softmax_1(f, cf)
                units(6, 6)
                if a is not None:
                    l1_front(a, ca)
                if f is not None:
                    l0_softmax_2(f, cf)
                units(7, 7)
                if a is not None:
                    l1_rest(a, ca)
                if a is not None and isinstance(a, int) and a == B - 1:
                    ca.need(ca.n)
                    places()
                units(8, 8)
                if f is not None:
                    l0_topk(f, cf, 0)
                units(9, 9)
                if f is not None:
                    l0_topk(f, cf, 1)
                units(10, 11)
                if f is not None:
                    l0_attention(f, cf)
                units(12, 13)
                if q is not None:
                    l1_norm(q, cq)
                if a is not None:
                    l1_values(a)
                for h in range(NH):
                    if a is not None:
                        l1_max(a, h)
                    if h == 4:
                        units(14, 14)
                    if h == 7 and q is not None:
                        l1_out(q)
                    if h == 11:
                        units(15, 15)
                if a is not None:
                    l1_nm(a, ca)
                if f is not None:
                    l0_tau(f, cf)
                for c, n in ((cf, N_L0V), (cn, N_NV), (ca, N_L1V), (cq, N_QV)):
                    assert c is None or c.n == n, [x_ and x_.n for x_ in (cf, cn, ca, cq)]

            rounds(v, body)
            v.wait_ge(s.loaded_w, 16 * 3)

            def ready(r, k):
                n = r * RING + k
                e = v.value_load(tile_ei[0:1, bass.ds(n, 1)], min_val=0, max_val=NE - 1)
                since(v, s.f_h_ps, r, RING, k + 1)
                cp(w1e[:, k, :], w1_sb[:, bass.ds(e * FF, FF)]).then_inc(s.f_w1, 1)
                since(v, s.f_y, r, RING, k + 1)
                v.wait_ge(s.f_xT_ps, n + 1)
                cp(meta[:, k, :], xs[:, k, D:DX])
                cp(xsT[:, k, :], bank[2][:, 0:P]).then_inc(s.f_xT, 1)

            def result(r, k):
                n = r * RING + k
                e = v.value_load(tile_ei[0:1, bass.ds(n, 1)], min_val=0, max_val=NE - 1)
                since(v, s.f_y, r, RING, k + 1)
                v.wait_ge(s.f_y_ps, n + 1)
                since(v, tile_stored[k], r, 16, 16)
                tt(yt[:, k, :], bank[y_bank[k]][:, 0:D], b2_sb[:, bass.ds(e * D, D)], ALU.add).then_inc(s.f_yt, 1)
                cp(y_token[:, k:k + 1], meta[:, k, 1:2])
                v.wait_ge(s.f_yt, n + 1)
                ts(ys[:, k, :], yt[:, k, :], meta[:, k, 0:1], None, ALU.mult).then_inc(s.f_y, 1)

            def sorted_tiles(r, last=False):
                for k in range(RING):
                    if not (last and k + 2 >= RING):
                        ready(r + (k + 2) // RING, (k + 2) % RING)
                    result(r, k)

            ready(0, 0)
            ready(0, 1)
            sorted_tiles(0)
            with v.Fori(1, ST // RING - 1) as r:
                sorted_tiles(r)
            sorted_tiles(ST // RING - 1, last=True)


_INS = ["L0_attn_hidden_states", "L0_attn_Wq", "L0_attn_bq", "L0_attn_Wk", "L0_attn_bk", "L0_attn_Wv", "L0_attn_bv",
        "L0_ffn_w_q", "L0_ffn_keys", "L0_ffn_expert_down", "L0_ffn_expert_up", "L0_ffn_norm_w",
        "L1_attn_wq", "L1_attn_wk", "L1_attn_wv", "L1_attn_wo", "L1_ffn_gate_w", "L1_ffn_w1", "L1_ffn_b1",
        "L1_ffn_w2", "L1_ffn_b2"]


def kernel(**inputs):
    import numpy as np
    import concourse.bacc as bacc
    from concourse.bass_utils import run_bass_kernel_spmd

    nc = bacc.Bacc("TRN2", target_bir_lowering=False, num_devices=1)
    arrays = {f"in_{name}": np.ascontiguousarray(inputs[name]) for name in _INS}
    arrays["in_shape_constants"] = shape_constants(np)
    args = [nc.dram_tensor(n, a.shape, mybir.dt.from_np(a.dtype), kind="ExternalInput").ap() for n, a in arrays.items()]
    out = nc.dram_tensor("out_dram", (B, S, D), F32, kind="ExternalOutput").ap()
    build(nc, *args, out)
    r = run_bass_kernel_spmd(nc, [arrays], core_ids=[0])
    return r.results[0]["out_dram"]
```
